# Optimizing a Trainium2 kernel written in Bass

```python
import numpy as np
import jax
import jax.numpy as jnp

def _softmax(x, axis=-1):
    return jax.nn.softmax(x, axis=axis)

def _gelu(x):
    return jax.nn.gelu(x, approximate=True)

def _silu(x):
    return jax.nn.silu(x)

def _sigmoid(x):
    return jax.nn.sigmoid(x)

def _layernorm(x, axis=-1, eps=1e-05):
    m = jnp.mean(x, axis=axis, keepdims=True)
    v = jnp.var(x, axis=axis, keepdims=True)
    return (x - m) / jnp.sqrt(v + eps)

def _scatter_add(tgt, idx, src, axis=0):
    return tgt.at[idx].add(src)

def _segment_sum(src, seg, n):
    return jax.ops.segment_sum(src, seg, n)
kernel_name = 'mk_perceiver_d4_seqx_r4_752383'

def setup_inputs(seed: int=0):
    np.random.seed(seed)
    _w = jnp.asarray

    def _rec_inputs():
        import jax
        import jax.numpy as jnp
        _rk = jax.random.key(seed)
        x = -0.0003929 + 0.9999 * jax.random.normal(jax.random.fold_in(_rk, 1), (1, 128, 256), jnp.float32)
        _lenS = 128 - jax.random.randint(jax.random.fold_in(_rk, 7), (1,), 0, max(1, 128 // 4) + 1, jnp.int32)
        _lenS2 = 12544 - jax.random.randint(jax.random.fold_in(_rk, 8), (1,), 0, max(1, 12544 // 4) + 1, jnp.int32)
        _ctx_1024P = jax.random.normal(jax.random.fold_in(_rk, 11), (1, 16, 256), jnp.float32)
        _ctx_1024c = jax.random.dirichlet(jax.random.fold_in(_rk, 511), 0.3 * jnp.ones((16,), jnp.float32), (1, 12544))
        _ctx_1024t = jnp.einsum('bsk,bkd->bsd', _ctx_1024c, _ctx_1024P)
        _ctx_1024t = _ctx_1024t * jax.lax.rsqrt(jnp.mean(jnp.square(_ctx_1024t)) + 1e-12) * 0.953939
        ctx_1024 = 2.81802e-05 + 1.00001 * (_ctx_1024t + 0.3 * jax.random.normal(jax.random.fold_in(_rk, 611), (1, 12544, 256), jnp.float32))
        _validS = jnp.arange(128)[None, :] < _lenS[:, None]
        _validS2 = jnp.arange(12544)[None, :] < _lenS2[:, None]
        _causal = jnp.tril(jnp.ones((128, 128), dtype=bool))
        mask_SxS2_ik0 = jnp.where(jnp.broadcast_to(_validS2[0:1, :], (128, 12544)), 0, 1).astype(jnp.int32)
        mask_BxSxS2_ff0 = jnp.where(jnp.ones((1, 128, 12544), dtype=bool), 0.0, -1000000000.0).astype(jnp.float32)
        return (x, ctx_1024, mask_SxS2_ik0, mask_BxSxS2_ff0)
    x, ctx_1024, mask_SxS2_ik0, mask_BxSxS2_ff0 = _rec_inputs()

    def _L0_xattn_setup():
        import jax, jax.numpy as jnp
        import numpy as np
        D1, D2, D3 = (256, 256, 256)
        key = jax.random.key(seed)
        k1, k2, kw, kb = jax.random.split(key, 4)
        x1 = jax.random.normal(k1, (8, 512, D1), dtype=jnp.float32)
        x2 = jax.random.normal(k2, (8, 512, D2), dtype=jnp.float32)
        bound = 1.0 / np.sqrt(D1 + D2)
        W = jax.random.uniform(kw, (D3, D1 + D2), minval=-bound, maxval=bound, dtype=jnp.float32)
        b = jax.random.uniform(kb, (D3,), minval=-bound, maxval=bound, dtype=jnp.float32)
        return {'x1': x1, 'x2': x2, 'W': W, 'b': b}
    _L0_xattn_all = _L0_xattn_setup()
    _L0_xattn_in = {k: v for k, v in _L0_xattn_all.items() if k in ('W', 'b')}
    del _L0_xattn_all

    def _L0_attn_setup():
        import jax, jax.numpy as jnp
        import numpy as np
        D_MODEL = 256
        N_HEADS = 16
        D_HEAD = D_MODEL // N_HEADS
        EPS = 1e-05

        def _forward(x, ln_g, ln_b, W_qkv, b_qkv, W_gate, b_gate, W_proj, b_proj):
            B, T, D = x.shape
            H, d = (N_HEADS, D_HEAD)
            mu = jnp.mean(x, axis=-1, keepdims=True)
            var = jnp.mean((x - mu) ** 2, axis=-1, keepdims=True)
            x_norm = (x - mu) * jax.lax.rsqrt(var + EPS) * ln_g + ln_b
            qkv = x_norm @ W_qkv + b_qkv
            q, k, v = jnp.split(qkv, 3, axis=-1)
            gate = jax.nn.sigmoid(x @ W_gate + b_gate)
            gate = gate / (jnp.mean(gate, axis=-1, keepdims=True) + EPS)
            q = (q * gate).reshape(B, T, H, d)
            k = (k * gate).reshape(B, T, H, d)
            v = v.reshape(B, T, H, d)
            q = jax.nn.relu(q.astype(jnp.float32)) ** 2 + EPS
            k = jax.nn.relu(k.astype(jnp.float32)) ** 2 + EPS
            v = v.astype(jnp.float32)
            qT = jnp.transpose(q, (1, 0, 2, 3))
            kT = jnp.transpose(k, (1, 0, 2, 3))
            vT = jnp.transpose(v, (1, 0, 2, 3))

            def step(carry, inp):
                kv_s, k_s = carry
                q_t, k_t, v_t = inp
                kv_s = kv_s + k_t[..., :, None] * v_t[..., None, :]
                k_s = k_s + k_t
                num = jnp.einsum('bhd,bhdm->bhm', q_t, kv_s)
                den = jnp.einsum('bhd,bhd->bh', q_t, k_s)[..., None] + EPS
                return ((kv_s, k_s), num / den)
            init = (jnp.zeros((B, H, d, d), jnp.float32), jnp.zeros((B, H, d), jnp.float32))
            _, outT = jax.lax.scan(step, init, (qT, kT, vT))
            out = jnp.transpose(outT, (1, 0, 2, 3)).astype(x.dtype).reshape(B, T, D)
            return out @ W_proj + b_proj
        key = jax.random.key(seed)
        ks = jax.random.split(key, 7)
        B, T = (4, 512)
        s = 1.0 / np.sqrt(D_MODEL)
        return {'x': jax.random.normal(ks[0], (B, T, D_MODEL), dtype=jnp.float32), 'ln_g': jnp.ones((D_MODEL,), jnp.float32), 'ln_b': jnp.zeros((D_MODEL,), jnp.float32), 'W_qkv': jax.random.normal(ks[1], (D_MODEL, 3 * D_MODEL), jnp.float32) * s, 'b_qkv': jnp.zeros((3 * D_MODEL,), jnp.float32), 'W_gate': jax.random.normal(ks[2], (D_MODEL, D_MODEL), jnp.float32) * s, 'b_gate': jnp.zeros((D_MODEL,), jnp.float32), 'W_proj': jax.random.normal(ks[3], (D_MODEL, D_MODEL), jnp.float32) * s, 'b_proj': jnp.zeros((D_MODEL,), jnp.float32)}
    _L0_attn_all = _L0_attn_setup()
    _L0_attn_in = {k: v for k, v in _L0_attn_all.items() if k in ('ln_g', 'ln_b', 'W_qkv', 'b_qkv', 'W_gate', 'b_gate', 'W_proj', 'b_proj')}
    del _L0_attn_all

    def _L0_ffn_setup():
        import jax, jax.numpy as jnp
        import numpy as np
        TOP_K = 2
        key = jax.random.key(seed)
        ks = jax.random.split(key, 5)
        B, S, D, H, E = (2, 512, 256, 704, 8)
        x = jax.random.normal(ks[0], (B, S, D), dtype=jnp.float32)
        Wg = jax.random.normal(ks[1], (E, D), dtype=jnp.float32) * 0.02
        W1 = jax.random.normal(ks[2], (E, H, D), dtype=jnp.float32) * 0.02
        W2 = jax.random.normal(ks[3], (E, H, D), dtype=jnp.float32) * 0.02
        W3 = jax.random.normal(ks[4], (E, D, H), dtype=jnp.float32) * 0.02
        return {'x': x, 'Wg': Wg, 'W1': W1, 'W2': W2, 'W3': W3}
    _L0_ffn_all = _L0_ffn_setup()
    _L0_ffn_in = {k: v for k, v in _L0_ffn_all.items() if k in ('Wg', 'W1', 'W2', 'W3')}
    del _L0_ffn_all

    def _L1_xattn_setup():
        import jax, jax.numpy as jnp
        import numpy as np
        B, L_ENC, L_DEC, D = (16, 128, 128, 256)
        key = jax.random.key(seed)
        k1, k2, k3, k4, k5, k6 = jax.random.split(key, 6)
        encoder_hc = jax.random.normal(k1, (B, L_ENC, D), dtype=jnp.float32)
        decoder_hq = jax.random.normal(k2, (B, L_DEC, D), dtype=jnp.float32)
        w_sim = jax.random.normal(k3, (3 * D,), dtype=jnp.float32) * 0.02
        b_sim = jax.random.normal(k4, (1,), dtype=jnp.float32) * 0.02
        W_qv = jax.random.normal(k5, (4 * D, D), dtype=jnp.float32) * 0.02
        b_qv = jax.random.normal(k6, (D,), dtype=jnp.float32) * 0.02
        return {'encoder_hc': encoder_hc, 'decoder_hq': decoder_hq, 'w_sim': w_sim, 'b_sim': b_sim, 'W_qv': W_qv, 'b_qv': b_qv}
    _L1_xattn_all = _L1_xattn_setup()
    _L1_xattn_in = {k: v for k, v in _L1_xattn_all.items() if k in ('w_sim', 'b_sim', 'W_qv', 'b_qv')}
    del _L1_xattn_all

    def _L1_attn_setup():
        import jax, jax.numpy as jnp
        import numpy as np
        HEADS = 16
        LN_EPS = 1e-05

        def _ln(v, w, b):
            mu = jnp.mean(v, axis=-1, keepdims=True)
            var = jnp.mean(jnp.square(v - mu), axis=-1, keepdims=True)
            return (v - mu) * jax.lax.rsqrt(var + LN_EPS) * w + b
        key = jax.random.key(seed)
        ks = jax.random.split(key, 5)
        b, t, e = (2, 512, 256)
        x = jax.random.normal(ks[0], (b, t, e), dtype=jnp.float32)
        scale = 0.02
        Wk = jax.random.normal(ks[1], (e, e), dtype=jnp.float32) * scale
        Wq = jax.random.normal(ks[2], (e, e), dtype=jnp.float32) * scale
        Wv = jax.random.normal(ks[3], (e, e), dtype=jnp.float32) * scale
        Wu = jax.random.normal(ks[4], (e, e), dtype=jnp.float32) * scale
        s = e // HEADS
        return {'x': x, 'Wk': Wk, 'Wq': Wq, 'Wv': Wv, 'Wu': Wu, 'kln_w': jnp.ones((s,), jnp.float32), 'kln_b': jnp.zeros((s,), jnp.float32), 'qln_w': jnp.ones((s,), jnp.float32), 'qln_b': jnp.zeros((s,), jnp.float32)}
    _L1_attn_all = _L1_attn_setup()
    _L1_attn_in = {k: v for k, v in _L1_attn_all.items() if k in ('Wk', 'Wq', 'Wv', 'Wu', 'kln_w', 'kln_b', 'qln_w', 'qln_b')}
    del _L1_attn_all

    def _L1_ffn_setup():
        import jax, jax.numpy as jnp
        import numpy as np
        B, S, H, F, G = (8, 512, 256, 1024, 128)
        EPS = 1e-05

        def _dequant(q, scales, g):
            K, N = q.shape
            w = (q.astype(jnp.float32) - 128.0).reshape(K // g, g, N) * scales[:, None, :]
            return w.reshape(K, N)
        key = jax.random.key(seed)
        ks = jax.random.split(key, 8)
        x = jax.random.normal(ks[0], (B, S, H), dtype=jnp.float32)
        ln_gamma = jnp.ones((H,), jnp.float32)
        ln_beta = jnp.zeros((H,), jnp.float32)
        fc1_q = jax.random.randint(ks[1], (H, F), 0, 64, dtype=jnp.int32)
        fc2_q = jax.random.randint(ks[2], (F, H), 0, 64, dtype=jnp.int32)
        fc1_scales = jax.random.uniform(ks[3], (H // G, F), jnp.float32) * 0.02 + 0.001
        fc2_scales = jax.random.uniform(ks[4], (F // G, H), jnp.float32) * 0.02 + 0.001
        fc1_bias = jax.random.normal(ks[5], (F,), jnp.float32) * 0.02
        fc2_bias = jax.random.normal(ks[6], (H,), jnp.float32) * 0.02
        return {'x': x, 'ln_gamma': ln_gamma, 'ln_beta': ln_beta, 'fc1_q': fc1_q, 'fc1_scales': fc1_scales, 'fc1_bias': fc1_bias, 'fc2_q': fc2_q, 'fc2_scales': fc2_scales, 'fc2_bias': fc2_bias}
    _L1_ffn_all = _L1_ffn_setup()
    _L1_ffn_in = {k: v for k, v in _L1_ffn_all.items() if k in ('ln_gamma', 'ln_beta', 'fc1_q', 'fc1_scales', 'fc1_bias', 'fc2_q', 'fc2_scales', 'fc2_bias')}
    del _L1_ffn_all

    def _L2_xattn_setup():
        import jax, jax.numpy as jnp
        import numpy as np
        D_MODEL = 256
        NUM_HEADS = 16
        D_K = D_MODEL // NUM_HEADS
        BATCH = 4
        SEQ = 512

        def _split_heads(x):
            b, s, _ = x.shape
            return x.reshape(b, s, NUM_HEADS, D_K).transpose(0, 2, 1, 3)
        key = jax.random.key(seed)
        ks = jax.random.split(key, 12)
        s = 0.02
        inp = {'Q': jax.random.normal(ks[0], (BATCH, SEQ, D_MODEL), jnp.float32), 'K': jax.random.normal(ks[1], (BATCH, SEQ, D_MODEL), jnp.float32), 'V': jax.random.normal(ks[2], (BATCH, SEQ, D_MODEL), jnp.float32), 'mask': jnp.tril(jnp.ones((SEQ, SEQ), jnp.int32)), 'Wq': jax.random.normal(ks[3], (D_MODEL, D_MODEL), jnp.float32) * s, 'bq': jax.random.normal(ks[4], (D_MODEL,), jnp.float32) * s, 'Wk': jax.random.normal(ks[5], (D_MODEL, D_MODEL), jnp.float32) * s, 'bk': jax.random.normal(ks[6], (D_MODEL,), jnp.float32) * s, 'Wv': jax.random.normal(ks[7], (D_MODEL, D_MODEL), jnp.float32) * s, 'bv': jax.random.normal(ks[8], (D_MODEL,), jnp.float32) * s, 'Wo': jax.random.normal(ks[9], (D_MODEL, D_MODEL), jnp.float32) * s, 'bo': jax.random.normal(ks[10], (D_MODEL,), jnp.float32) * s}
        return inp
    _L2_xattn_all = _L2_xattn_setup()
    _L2_xattn_in = {k: v for k, v in _L2_xattn_all.items() if k in ('Wq', 'bq', 'Wk', 'bk', 'Wv', 'bv', 'Wo', 'bo')}
    del _L2_xattn_all

    def _L2_attn_setup():
        import jax, jax.numpy as jnp
        import numpy as np
        NUM_HEADS = 16
        HIDDEN = 256
        HEAD_DIM = HIDDEN // NUM_HEADS
        B, L = (1, 512)
        key = jax.random.key(seed)
        ks = jax.random.split(key, 5)
        scale = 1.0 / np.sqrt(HIDDEN)
        x = jax.random.normal(ks[0], (B, L, HIDDEN), dtype=jnp.float32)
        Wq = jax.random.normal(ks[1], (HIDDEN, HIDDEN), dtype=jnp.float32) * scale
        Wk = jax.random.normal(ks[2], (HIDDEN, HIDDEN), dtype=jnp.float32) * scale
        Wv = jax.random.normal(ks[3], (HIDDEN, HIDDEN), dtype=jnp.float32) * scale
        Wo = jax.random.normal(ks[4], (HIDDEN, HIDDEN), dtype=jnp.float32) * scale
        return {'x': x, 'Wq': Wq, 'Wk': Wk, 'Wv': Wv, 'Wo': Wo}
    _L2_attn_all = _L2_attn_setup()
    _L2_attn_in = {k: v for k, v in _L2_attn_all.items() if k in ('Wq', 'Wk', 'Wv', 'Wo')}
    del _L2_attn_all

    def _L2_ffn_setup():
        import jax, jax.numpy as jnp
        import numpy as np
        B, S, H, E, K, I = (4, 512, 256, 8, 2, 1024)
        GATE_EPS = 1e-06
        LN_EPS = 1e-05
        key = jax.random.key(seed)
        k0, k1, k2, k3 = jax.random.split(key, 4)
        x = jax.random.normal(k0, (B, S, H), jnp.float32)
        gate_w = jax.random.normal(k1, (E, H), jnp.float32) * np.float32(np.sqrt(2.0 / (H + E)))
        expert_bias = jnp.zeros((E,), jnp.float32)
        w_up = jax.random.normal(k2, (E, I, H), jnp.float32) * np.float32(np.sqrt(2.0 / (H + I)))
        w_down = jax.random.normal(k3, (E, H, I), jnp.float32) * np.float32(np.sqrt(2.0 / (H + I)))
        return {'x': x, 'gate_w': gate_w, 'expert_bias': expert_bias, 'w_up': w_up, 'w_down': w_down}
    _L2_ffn_all = _L2_ffn_setup()
    _L2_ffn_in = {k: v for k, v in _L2_ffn_all.items() if k in ('gate_w', 'expert_bias', 'w_up', 'w_down')}
    del _L2_ffn_all

    def _L3_xattn_setup():
        import jax, jax.numpy as jnp
        import numpy as np
        _NEG_INF_FP32 = -1000000000.0
        B, L, D, H = (2, 512, 256, 16)

        def _split_heads(t, heads):
            b, l, d = t.shape
            return t.reshape(b, l, heads, d // heads).transpose(0, 2, 1, 3)
        key = jax.random.key(seed)
        ks = jax.random.split(key, 6)
        s = 0.02
        return {'x': jax.random.normal(ks[0], (B, L, D), jnp.float32), 'y': jax.random.normal(ks[1], (B, L, D), jnp.float32), 'bias': jnp.zeros((B, L, L), jnp.float32), 'Wq': jax.random.normal(ks[2], (D, D), jnp.float32) * s, 'Wk': jax.random.normal(ks[3], (D, D), jnp.float32) * s, 'Wv': jax.random.normal(ks[4], (D, D), jnp.float32) * s, 'Wo': jax.random.normal(ks[5], (D, D), jnp.float32) * s}
    _L3_xattn_all = _L3_xattn_setup()
    _L3_xattn_in = {k: v for k, v in _L3_xattn_all.items() if k in ('Wq', 'Wk', 'Wv', 'Wo')}
    del _L3_xattn_all

    def _L3_attn_setup():
        import jax, jax.numpy as jnp
        import numpy as np
        H = 16
        EPS = 1e-06
        key = jax.random.key(seed)
        ks = jax.random.split(key, 5)
        B, N, D = (4, 1024, 256)
        x = jax.random.normal(ks[0], (B, N, D), dtype=jnp.float32)
        q = jax.random.normal(ks[1], (D,), dtype=jnp.float32)
        k = jax.random.normal(ks[2], (D,), dtype=jnp.float32)
        log_decay = jax.random.normal(ks[3], (H,), dtype=jnp.float32)
        norm_weight = jnp.ones((D,), dtype=jnp.float32)
        o_w = jax.random.normal(ks[4], (D, D), dtype=jnp.float32) * 0.02
        return {'x': x, 'q': q, 'k': k, 'log_decay': log_decay, 'norm_weight': norm_weight, 'o_w': o_w}
    _L3_attn_all = _L3_attn_setup()
    _L3_attn_in = {k: v for k, v in _L3_attn_all.items() if k in ('q', 'k', 'log_decay', 'norm_weight', 'o_w')}
    del _L3_attn_all

    def _L3_ffn_setup():
        import jax, jax.numpy as jnp
        import numpy as np
        TOP_K = 2
        CAPACITY_FACTOR = 1.25

        def _moe_forward(x, gate_w, wi_gate, wi_up, wo):
            B, S, D = x.shape
            E = wi_gate.shape[0]
            N = B * S
            capacity = max(int(N / E * CAPACITY_FACTOR), 1)
            x_flat = x.reshape(N, D)
            router_logits = x_flat @ gate_w.T
            router_probs = jax.nn.softmax(router_logits, axis=-1)
            top_k_probs, top_k_idx = jax.lax.top_k(router_probs, TOP_K)
            top_k_probs = top_k_probs / jnp.sum(top_k_probs, axis=-1, keepdims=True)
            out = jnp.zeros_like(x_flat)
            experts = jnp.arange(E, dtype=jnp.int32)
            for k in range(TOP_K):
                eid = top_k_idx[:, k]
                ew = top_k_probs[:, k]
                onehot = (eid[:, None] == experts[None, :]).astype(jnp.int32)
                pos_all = jnp.cumsum(onehot, axis=0) - 1
                pos = jnp.take_along_axis(pos_all, eid[:, None].astype(jnp.int32), axis=1)[:, 0]
                valid = pos < capacity
                pos_c = jnp.where(valid, pos, 0)
                disp = jnp.zeros((E, capacity, D), x_flat.dtype).at[eid, pos_c].add(jnp.where(valid[:, None], x_flat, 0.0))
                gate = jax.nn.silu(jnp.einsum('ecd,efd->ecf', disp, wi_gate))
                up = jnp.einsum('ecd,efd->ecf', disp, wi_up)
                expert_out = jnp.einsum('ecf,edf->ecd', gate * up, wo)
                tok_out = expert_out[eid, pos_c]
                out = out + jnp.where(valid[:, None], ew[:, None] * tok_out, 0.0)
            return out.reshape(B, S, D)
        key = jax.random.key(seed)
        k1, k2, k3, k4, k5 = jax.random.split(key, 5)
        B, S, D, F, E = (4, 512, 256, 1024, 8)
        return {'x': jax.random.normal(k1, (B, S, D), dtype=jnp.float32), 'gate_w': jax.random.normal(k2, (E, D), dtype=jnp.float32) * 0.02, 'wi_gate': jax.random.normal(k3, (E, F, D), dtype=jnp.float32) * 0.02, 'wi_up': jax.random.normal(k4, (E, F, D), dtype=jnp.float32) * 0.02, 'wo': jax.random.normal(k5, (E, D, F), dtype=jnp.float32) * 0.02}
    _L3_ffn_all = _L3_ffn_setup()
    _L3_ffn_in = {k: v for k, v in _L3_ffn_all.items() if k in ('gate_w', 'wi_gate', 'wi_up', 'wo')}
    del _L3_ffn_all
    return {'x': x, 'ctx_1024': ctx_1024, 'mask_SxS2_ik0': mask_SxS2_ik0, 'mask_BxSxS2_ff0': mask_BxSxS2_ff0, 'L0_xattn_W': _L0_xattn_in['W'], 'L0_xattn_b': _L0_xattn_in['b'], 'L0_attn_ln_g': _L0_attn_in['ln_g'], 'L0_attn_ln_b': _L0_attn_in['ln_b'], 'L0_attn_W_qkv': _L0_attn_in['W_qkv'], 'L0_attn_b_qkv': _L0_attn_in['b_qkv'], 'L0_attn_W_gate': _L0_attn_in['W_gate'], 'L0_attn_b_gate': _L0_attn_in['b_gate'], 'L0_attn_W_proj': _L0_attn_in['W_proj'], 'L0_attn_b_proj': _L0_attn_in['b_proj'], 'L0_ffn_Wg': _L0_ffn_in['Wg'], 'L0_ffn_W1': _L0_ffn_in['W1'], 'L0_ffn_W2': _L0_ffn_in['W2'], 'L0_ffn_W3': _L0_ffn_in['W3'], 'L1_xattn_w_sim': _L1_xattn_in['w_sim'], 'L1_xattn_b_sim': _L1_xattn_in['b_sim'], 'L1_xattn_W_qv': _L1_xattn_in['W_qv'], 'L1_xattn_b_qv': _L1_xattn_in['b_qv'], 'L1_attn_Wk': _L1_attn_in['Wk'], 'L1_attn_Wq': _L1_attn_in['Wq'], 'L1_attn_Wv': _L1_attn_in['Wv'], 'L1_attn_Wu': _L1_attn_in['Wu'], 'L1_attn_kln_w': _L1_attn_in['kln_w'], 'L1_attn_kln_b': _L1_attn_in['kln_b'], 'L1_attn_qln_w': _L1_attn_in['qln_w'], 'L1_attn_qln_b': _L1_attn_in['qln_b'], 'L1_ffn_ln_gamma': _L1_ffn_in['ln_gamma'], 'L1_ffn_ln_beta': _L1_ffn_in['ln_beta'], 'L1_ffn_fc1_q': _L1_ffn_in['fc1_q'], 'L1_ffn_fc1_scales': _L1_ffn_in['fc1_scales'], 'L1_ffn_fc1_bias': _L1_ffn_in['fc1_bias'], 'L1_ffn_fc2_q': _L1_ffn_in['fc2_q'], 'L1_ffn_fc2_scales': _L1_ffn_in['fc2_scales'], 'L1_ffn_fc2_bias': _L1_ffn_in['fc2_bias'], 'L2_xattn_Wq': _L2_xattn_in['Wq'], 'L2_xattn_bq': _L2_xattn_in['bq'], 'L2_xattn_Wk': _L2_xattn_in['Wk'], 'L2_xattn_bk': _L2_xattn_in['bk'], 'L2_xattn_Wv': _L2_xattn_in['Wv'], 'L2_xattn_bv': _L2_xattn_in['bv'], 'L2_xattn_Wo': _L2_xattn_in['Wo'], 'L2_xattn_bo': _L2_xattn_in['bo'], 'L2_attn_Wq': _L2_attn_in['Wq'], 'L2_attn_Wk': _L2_attn_in['Wk'], 'L2_attn_Wv': _L2_attn_in['Wv'], 'L2_attn_Wo': _L2_attn_in['Wo'], 'L2_ffn_gate_w': _L2_ffn_in['gate_w'], 'L2_ffn_expert_bias': _L2_ffn_in['expert_bias'], 'L2_ffn_w_up': _L2_ffn_in['w_up'], 'L2_ffn_w_down': _L2_ffn_in['w_down'], 'L3_xattn_Wq': _L3_xattn_in['Wq'], 'L3_xattn_Wk': _L3_xattn_in['Wk'], 'L3_xattn_Wv': _L3_xattn_in['Wv'], 'L3_xattn_Wo': _L3_xattn_in['Wo'], 'L3_attn_q': _L3_attn_in['q'], 'L3_attn_k': _L3_attn_in['k'], 'L3_attn_log_decay': _L3_attn_in['log_decay'], 'L3_attn_norm_weight': _L3_attn_in['norm_weight'], 'L3_attn_o_w': _L3_attn_in['o_w'], 'L3_ffn_gate_w': _L3_ffn_in['gate_w'], 'L3_ffn_wi_gate': _L3_ffn_in['wi_gate'], 'L3_ffn_wi_up': _L3_ffn_in['wi_up'], 'L3_ffn_wo': _L3_ffn_in['wo']}

def reference(x, ctx_1024, mask_SxS2_ik0, mask_BxSxS2_ff0, L0_xattn_W, L0_xattn_b, L0_attn_ln_g, L0_attn_ln_b, L0_attn_W_qkv, L0_attn_b_qkv, L0_attn_W_gate, L0_attn_b_gate, L0_attn_W_proj, L0_attn_b_proj, L0_ffn_Wg, L0_ffn_W1, L0_ffn_W2, L0_ffn_W3, L1_xattn_w_sim, L1_xattn_b_sim, L1_xattn_W_qv, L1_xattn_b_qv, L1_attn_Wk, L1_attn_Wq, L1_attn_Wv, L1_attn_Wu, L1_attn_kln_w, L1_attn_kln_b, L1_attn_qln_w, L1_attn_qln_b, L1_ffn_ln_gamma, L1_ffn_ln_beta, L1_ffn_fc1_q, L1_ffn_fc1_scales, L1_ffn_fc1_bias, L1_ffn_fc2_q, L1_ffn_fc2_scales, L1_ffn_fc2_bias, L2_xattn_Wq, L2_xattn_bq, L2_xattn_Wk, L2_xattn_bk, L2_xattn_Wv, L2_xattn_bv, L2_xattn_Wo, L2_xattn_bo, L2_attn_Wq, L2_attn_Wk, L2_attn_Wv, L2_attn_Wo, L2_ffn_gate_w, L2_ffn_expert_bias, L2_ffn_w_up, L2_ffn_w_down, L3_xattn_Wq, L3_xattn_Wk, L3_xattn_Wv, L3_xattn_Wo, L3_attn_q, L3_attn_k, L3_attn_log_decay, L3_attn_norm_weight, L3_attn_o_w, L3_ffn_gate_w, L3_ffn_wi_gate, L3_ffn_wi_up, L3_ffn_wo):
    import jax
    import jax.numpy as jnp

    def _L0_xattn_ref(x1, x2, W, b):
        import jax, jax.numpy as jnp
        import numpy as np
        D1, D2, D3 = (256, 256, 256)
        d1 = x1.shape[-1]
        W1 = W[:, :d1]
        W2 = W[:, d1:]
        part1 = jnp.einsum('bld,ed->ble', x1, W1)
        part2 = jnp.einsum('bld,ed->be', x2, W2) / x2.shape[1]
        return part1 + part2[:, None, :] + b

    def _L0_attn_ref(x, ln_g, ln_b, W_qkv, b_qkv, W_gate, b_gate, W_proj, b_proj):
        import jax, jax.numpy as jnp
        import numpy as np
        D_MODEL = 256
        N_HEADS = 16
        D_HEAD = D_MODEL // N_HEADS
        EPS = 1e-05

        def _forward(x, ln_g, ln_b, W_qkv, b_qkv, W_gate, b_gate, W_proj, b_proj):
            B, T, D = x.shape
            H, d = (N_HEADS, D_HEAD)
            mu = jnp.mean(x, axis=-1, keepdims=True)
            var = jnp.mean((x - mu) ** 2, axis=-1, keepdims=True)
            x_norm = (x - mu) * jax.lax.rsqrt(var + EPS) * ln_g + ln_b
            qkv = x_norm @ W_qkv + b_qkv
            q, k, v = jnp.split(qkv, 3, axis=-1)
            gate = jax.nn.sigmoid(x @ W_gate + b_gate)
            gate = gate / (jnp.mean(gate, axis=-1, keepdims=True) + EPS)
            q = (q * gate).reshape(B, T, H, d)
            k = (k * gate).reshape(B, T, H, d)
            v = v.reshape(B, T, H, d)
            q = jax.nn.relu(q.astype(jnp.float32)) ** 2 + EPS
            k = jax.nn.relu(k.astype(jnp.float32)) ** 2 + EPS
            v = v.astype(jnp.float32)
            qT = jnp.transpose(q, (1, 0, 2, 3))
            kT = jnp.transpose(k, (1, 0, 2, 3))
            vT = jnp.transpose(v, (1, 0, 2, 3))

            def step(carry, inp):
                kv_s, k_s = carry
                q_t, k_t, v_t = inp
                kv_s = kv_s + k_t[..., :, None] * v_t[..., None, :]
                k_s = k_s + k_t
                num = jnp.einsum('bhd,bhdm->bhm', q_t, kv_s)
                den = jnp.einsum('bhd,bhd->bh', q_t, k_s)[..., None] + EPS
                return ((kv_s, k_s), num / den)
            init = (jnp.zeros((B, H, d, d), jnp.float32), jnp.zeros((B, H, d), jnp.float32))
            _, outT = jax.lax.scan(step, init, (qT, kT, vT))
            out = jnp.transpose(outT, (1, 0, 2, 3)).astype(x.dtype).reshape(B, T, D)
            return out @ W_proj + b_proj
        return _forward(x, ln_g, ln_b, W_qkv, b_qkv, W_gate, b_gate, W_proj, b_proj)

    def _L0_ffn_ref(x, Wg, W1, W2, W3):
        import jax, jax.numpy as jnp
        import numpy as np
        TOP_K = 2
        B, S, D = x.shape
        E = Wg.shape[0]
        xt = x.reshape(B * S, D)
        scores = xt @ Wg.T
        topk_scores, topk_idx = jax.lax.top_k(scores, TOP_K)
        gate = jax.nn.silu(jnp.einsum('td,ehd->teh', xt, W1))
        up = jnp.einsum('td,ehd->teh', xt, W2)
        y = jnp.einsum('teh,edh->ted', gate * up, W3)
        onehot = jax.nn.one_hot(topk_idx, E, dtype=x.dtype)
        w = jnp.einsum('tke,tk->te', onehot, topk_scores)
        out = jnp.einsum('te,ted->td', w, y)
        return out.reshape(B, S, D)

    def _L1_xattn_ref(encoder_hc, decoder_hq, w_sim, b_sim, W_qv, b_qv):
        import jax, jax.numpy as jnp
        import numpy as np
        B, L_ENC, L_DEC, D = (16, 128, 128, 256)
        d = encoder_hc.shape[-1]
        w1, w2, w3 = (w_sim[:d], w_sim[d:2 * d], w_sim[2 * d:])
        Sim = (encoder_hc @ w1)[:, :, None] + (decoder_hq @ w2)[:, None, :] + jnp.einsum('bid,bjd->bij', encoder_hc * w3, decoder_hq) + b_sim[0]
        A = jax.nn.softmax(Sim, axis=2)
        hq_hat = jnp.einsum('bij,bjd->bid', A, decoder_hq)
        Batt = jax.nn.softmax(jnp.max(Sim, axis=2), axis=1)
        hc_bar = jnp.einsum('bi,bid->bd', Batt, encoder_hc)[:, None, :]
        hc_hat = jnp.broadcast_to(hc_bar, encoder_hc.shape)
        feats = jnp.concatenate([encoder_hc, hq_hat, encoder_hc * hq_hat, encoder_hc * hc_hat], axis=-1)
        hcq = feats @ W_qv + b_qv
        return hcq

    def _L1_attn_ref(x, Wk, Wq, Wv, Wu, kln_w, kln_b, qln_w, qln_b):
        import jax, jax.numpy as jnp
        import numpy as np
        HEADS = 16
        LN_EPS = 1e-05

        def _ln(v, w, b):
            mu = jnp.mean(v, axis=-1, keepdims=True)
            var = jnp.mean(jnp.square(v - mu), axis=-1, keepdims=True)
            return (v - mu) * jax.lax.rsqrt(var + LN_EPS) * w + b
        b, t, e = x.shape
        h = HEADS
        s = e // h
        k = (x @ Wk.T).reshape(b, t, h, s)
        q = (x @ Wq.T).reshape(b, t, h, s)
        v = (x @ Wv.T).reshape(b, t, h, s)
        k = _ln(k, kln_w, kln_b)
        q = _ln(q, qln_w, qln_b)
        scalefactor = 1.0 / np.sqrt(s).astype(np.float32)
        dot = jnp.einsum('bqhs,bkhs->bhqk', q, k) * scalefactor
        causal = jnp.triu(jnp.ones((t, t), dtype=bool), k=1)
        dot = jnp.where(causal, -jnp.inf, dot)
        attn = jax.nn.softmax(dot, axis=-1)
        out = jnp.einsum('bhqk,bkhs->bqhs', attn, v).reshape(b, t, e)
        return out @ Wu.T

    def _L1_ffn_ref(x, ln_gamma, ln_beta, fc1_q, fc1_scales, fc1_bias, fc2_q, fc2_scales, fc2_bias):
        import jax, jax.numpy as jnp
        import numpy as np
        B, S, H, F, G = (8, 512, 256, 1024, 128)
        EPS = 1e-05

        def _dequant(q, scales, g):
            K, N = q.shape
            w = (q.astype(jnp.float32) - 128.0).reshape(K // g, g, N) * scales[:, None, :]
            return w.reshape(K, N)
        residual = x
        mu = jnp.mean(x, axis=-1, keepdims=True)
        var = jnp.mean(jnp.square(x - mu), axis=-1, keepdims=True)
        h = (x - mu) * jax.lax.rsqrt(var + EPS) * ln_gamma + ln_beta
        hf = h.reshape(-1, H)
        w1 = _dequant(fc1_q, fc1_scales, G)
        y = hf @ w1 + fc1_bias
        y = jax.nn.silu(y)
        w2 = _dequant(fc2_q, fc2_scales, G)
        z = y @ w2 + fc2_bias
        return residual + 0.5 * z.reshape(residual.shape)

    def _L2_xattn_ref(Q, K, V, mask, Wq, bq, Wk, bk, Wv, bv, Wo, bo):
        import jax, jax.numpy as jnp
        import numpy as np
        D_MODEL = 256
        NUM_HEADS = 16
        D_K = D_MODEL // NUM_HEADS
        BATCH = 4
        SEQ = 512

        def _split_heads(x):
            b, s, _ = x.shape
            return x.reshape(b, s, NUM_HEADS, D_K).transpose(0, 2, 1, 3)
        q = _split_heads(Q @ Wq.T + bq)
        k = _split_heads(K @ Wk.T + bk)
        v = _split_heads(V @ Wv.T + bv)
        scale = 1.0 / jnp.sqrt(jnp.asarray(D_K, q.dtype))
        scores = jnp.einsum('bhqd,bhkd->bhqk', q, k) * scale
        scores = jnp.where(mask == 0, jnp.asarray(-jnp.inf, scores.dtype), scores)
        attn = jax.nn.softmax(scores, axis=-1)
        out = jnp.einsum('bhqk,bhkd->bhqd', attn, v)
        b, h, s, dk = out.shape
        out = out.transpose(0, 2, 1, 3).reshape(b, s, h * dk)
        return out @ Wo.T + bo

    def _L2_attn_ref(x, Wq, Wk, Wv, Wo):
        import jax, jax.numpy as jnp
        import numpy as np
        NUM_HEADS = 16
        HIDDEN = 256
        HEAD_DIM = HIDDEN // NUM_HEADS
        B, L = (1, 512)
        Bx, Lx, _ = x.shape
        q = (x @ Wq.T).reshape(Bx, Lx, NUM_HEADS, HEAD_DIM)
        k = (x @ Wk.T).reshape(Bx, Lx, NUM_HEADS, HEAD_DIM)
        v = (x @ Wv.T).reshape(Bx, Lx, NUM_HEADS, HEAD_DIM)
        q = jax.nn.elu(q) + 1.0
        k = jax.nn.elu(k) + 1.0
        kv = jnp.einsum('blhd,blhe->blhde', k, v)
        kv_cumsum = jnp.cumsum(kv, axis=1)
        k_cumsum = jnp.cumsum(k, axis=1)
        out = jnp.einsum('blhd,blhde->blhe', q, kv_cumsum)
        denom = jnp.clip(jnp.einsum('blhd,blhd->blh', q, k_cumsum), 1e-06, None)
        out = out / denom[..., None]
        return out.reshape(Bx, Lx, HIDDEN) @ Wo.T

    def _L2_ffn_ref(x, gate_w, expert_bias, w_up, w_down):
        import jax, jax.numpy as jnp
        import numpy as np
        B, S, H, E, K, I = (4, 512, 256, 8, 2, 1024)
        GATE_EPS = 1e-06
        LN_EPS = 1e-05
        logits = jnp.einsum('bsh,eh->bse', x, gate_w) + expert_bias
        weights = jax.nn.softmax(logits, axis=-1)
        top_w, top_i = jax.lax.top_k(weights, K)
        top_w = top_w / (jnp.sum(top_w, axis=-1, keepdims=True) + GATE_EPS)
        sparse_w = jnp.sum(jax.nn.one_hot(top_i, E, dtype=weights.dtype) * top_w[..., None], axis=-2)
        out = jnp.zeros_like(x)
        for e in range(E):
            h = jax.nn.gelu(jnp.einsum('bsh,ih->bsi', x, w_up[e]), approximate=False)
            y = jnp.einsum('bsi,hi->bsh', h, w_down[e])
            out = out + sparse_w[..., e:e + 1] * y
        mu = jnp.mean(out, axis=-1, keepdims=True)
        var = jnp.mean(jnp.square(out - mu), axis=-1, keepdims=True)
        out = (out - mu) * jax.lax.rsqrt(var + LN_EPS)
        return out + x

    def _L3_xattn_ref(x, y, bias, Wq, Wk, Wv, Wo):
        import jax, jax.numpy as jnp
        import numpy as np
        _NEG_INF_FP32 = -1000000000.0
        B, L, D, H = (2, 512, 256, 16)

        def _split_heads(t, heads):
            b, l, d = t.shape
            return t.reshape(b, l, heads, d // heads).transpose(0, 2, 1, 3)
        q = _split_heads(x @ Wq, H)
        k = _split_heads(y @ Wk, H)
        v = _split_heads(y @ Wv, H)
        depth = k.shape[-1]
        scale = jnp.asarray(depth, q.dtype) ** (-0.5)
        logits = jnp.einsum('bhqd,bhkd->bhqk', q, k) * scale
        logits = logits + bias[:, None, :, :] * _NEG_INF_FP32
        weights = jax.nn.softmax(logits, axis=-1)
        out = jnp.einsum('bhqk,bhkd->bhqd', weights, v)
        out = out.transpose(0, 2, 1, 3).reshape(x.shape[0], x.shape[1], D)
        return out @ Wo

    def _L3_attn_ref(x, q, k, log_decay, norm_weight, o_w):
        import jax, jax.numpy as jnp
        import numpy as np
        H = 16
        EPS = 1e-06
        b, n, dm = x.shape
        dh = dm // H
        qh = q.reshape(H, dh)
        kh = k.reshape(H, dh)
        v = x.reshape(b, n, H, dh)
        lam = jax.nn.sigmoid(log_decay)

        def step(S, v_t):
            S = lam[None, :, None, None] * S + kh[None, :, :, None] * v_t[:, :, None, :]
            o_t = jnp.einsum('hd,bhdv->bhv', qh, S)
            return (S, o_t)
        S0 = jnp.zeros((b, H, dh, dh), dtype=x.dtype)
        _, o = jax.lax.scan(step, S0, jnp.moveaxis(v, 1, 0))
        o = jnp.moveaxis(o, 0, 1).reshape(b, n, dm)
        o = o * jax.lax.rsqrt(jnp.mean(o * o, axis=-1, keepdims=True) + EPS) * norm_weight
        return o @ o_w.T

    def _L3_ffn_ref(x, gate_w, wi_gate, wi_up, wo):
        import jax, jax.numpy as jnp
        import numpy as np
        TOP_K = 2
        CAPACITY_FACTOR = 1.25

        def _moe_forward(x, gate_w, wi_gate, wi_up, wo):
            B, S, D = x.shape
            E = wi_gate.shape[0]
            N = B * S
            capacity = max(int(N / E * CAPACITY_FACTOR), 1)
            x_flat = x.reshape(N, D)
            router_logits = x_flat @ gate_w.T
            router_probs = jax.nn.softmax(router_logits, axis=-1)
            top_k_probs, top_k_idx = jax.lax.top_k(router_probs, TOP_K)
            top_k_probs = top_k_probs / jnp.sum(top_k_probs, axis=-1, keepdims=True)
            out = jnp.zeros_like(x_flat)
            experts = jnp.arange(E, dtype=jnp.int32)
            for k in range(TOP_K):
                eid = top_k_idx[:, k]
                ew = top_k_probs[:, k]
                onehot = (eid[:, None] == experts[None, :]).astype(jnp.int32)
                pos_all = jnp.cumsum(onehot, axis=0) - 1
                pos = jnp.take_along_axis(pos_all, eid[:, None].astype(jnp.int32), axis=1)[:, 0]
                valid = pos < capacity
                pos_c = jnp.where(valid, pos, 0)
                disp = jnp.zeros((E, capacity, D), x_flat.dtype).at[eid, pos_c].add(jnp.where(valid[:, None], x_flat, 0.0))
                gate = jax.nn.silu(jnp.einsum('ecd,efd->ecf', disp, wi_gate))
                up = jnp.einsum('ecd,efd->ecf', disp, wi_up)
                expert_out = jnp.einsum('ecf,edf->ecd', gate * up, wo)
                tok_out = expert_out[eid, pos_c]
                out = out + jnp.where(valid[:, None], ew[:, None] * tok_out, 0.0)
            return out.reshape(B, S, D)
        return _moe_forward(x, gate_w, wi_gate, wi_up, wo)
    x = x + _L0_xattn_ref(_layernorm(x, axis=-1), ctx_1024, L0_xattn_W, L0_xattn_b)
    x = x + _L0_attn_ref(_layernorm(x, axis=-1), L0_attn_ln_g, L0_attn_ln_b, L0_attn_W_qkv, L0_attn_b_qkv, L0_attn_W_gate, L0_attn_b_gate, L0_attn_W_proj, L0_attn_b_proj)
    x = x + _L0_ffn_ref(_layernorm(x, axis=-1), L0_ffn_Wg, L0_ffn_W1, L0_ffn_W2, L0_ffn_W3)
    x = x + _L1_xattn_ref(_layernorm(x, axis=-1), ctx_1024, L1_xattn_w_sim, L1_xattn_b_sim, L1_xattn_W_qv, L1_xattn_b_qv)
    x = x + _L1_attn_ref(_layernorm(x, axis=-1), L1_attn_Wk, L1_attn_Wq, L1_attn_Wv, L1_attn_Wu, L1_attn_kln_w, L1_attn_kln_b, L1_attn_qln_w, L1_attn_qln_b)
    x = x + _L1_ffn_ref(_layernorm(x, axis=-1), L1_ffn_ln_gamma, L1_ffn_ln_beta, L1_ffn_fc1_q, L1_ffn_fc1_scales, L1_ffn_fc1_bias, L1_ffn_fc2_q, L1_ffn_fc2_scales, L1_ffn_fc2_bias)
    x = x + _L2_xattn_ref(_layernorm(x, axis=-1), ctx_1024, ctx_1024, mask_SxS2_ik0, L2_xattn_Wq, L2_xattn_bq, L2_xattn_Wk, L2_xattn_bk, L2_xattn_Wv, L2_xattn_bv, L2_xattn_Wo, L2_xattn_bo)
    x = x + _L2_attn_ref(_layernorm(x, axis=-1), L2_attn_Wq, L2_attn_Wk, L2_attn_Wv, L2_attn_Wo)
    x = x + _L2_ffn_ref(_layernorm(x, axis=-1), L2_ffn_gate_w, L2_ffn_expert_bias, L2_ffn_w_up, L2_ffn_w_down)
    x = x + _L3_xattn_ref(_layernorm(x, axis=-1), ctx_1024, mask_BxSxS2_ff0, L3_xattn_Wq, L3_xattn_Wk, L3_xattn_Wv, L3_xattn_Wo)
    x = x + _L3_attn_ref(_layernorm(x, axis=-1), L3_attn_q, L3_attn_k, L3_attn_log_decay, L3_attn_norm_weight, L3_attn_o_w)
    x = x + _L3_ffn_ref(_layernorm(x, axis=-1), L3_ffn_gate_w, L3_ffn_wi_gate, L3_ffn_wi_up, L3_ffn_wo)
    return x

_drawn_inputs = setup_inputs


def setup_inputs(seed=0):
    import zlib

    import numpy as np

    out = dict(_drawn_inputs(seed))
    spreads = {'L0_attn_ln_g': (1.0, 0.2),
     'L0_attn_ln_b': (0.0, 0.1),
     'L0_attn_b_qkv': (0.0, 0.1),
     'L0_attn_b_gate': (0.0, 0.8),
     'L0_attn_b_proj': (0.0, 0.1),
     'L1_attn_kln_w': (1.0, 0.6),
     'L1_attn_kln_b': (0.0, 2.0),
     'L1_attn_qln_w': (1.0, 0.6),
     'L1_attn_qln_b': (0.0, 2.0),
     'L1_ffn_ln_gamma': (1.0, 0.2),
     'L1_ffn_ln_beta': (0.0, 0.1),
     'L2_ffn_expert_bias': (0.0, 2.0),
     'L3_attn_norm_weight': (1.0, 0.6)}
    factors = {'L0_ffn_Wg': 6.656,
     'L0_ffn_W1': 4.563,
     'L0_ffn_W2': 4.263,
     'L0_ffn_W3': 5.373,
     'L1_xattn_w_sim': 11.982,
     'L1_xattn_b_qv': 40.957,
     'L1_attn_Wk': 59.264,
     'L1_attn_Wq': 61.904,
     'L1_attn_Wu': 25.776,
     'L1_ffn_fc1_bias': 64.0,
     'L1_ffn_fc2_bias': 64.0,
     'L2_xattn_Wq': 64.0,
     'L2_xattn_bq': 64.0,
     'L2_xattn_Wk': 64.0,
     'L2_xattn_Wv': 64.0,
     'L2_xattn_bv': 64.0,
     'L2_xattn_Wo': 64.0,
     'L2_xattn_bo': 200.0,
     'L2_attn_Wq': 64.0,
     'L2_attn_Wk': 64.0,
     'L2_attn_Wv': 8.0,
     'L2_attn_Wo': 8.0,
     'L2_ffn_gate_w': 200.0,
     'L2_ffn_w_up': 200.0,
     'L2_ffn_w_down': 200.0,
     'L3_xattn_Wq': 64.0,
     'L3_xattn_Wk': 64.0,
     'L3_xattn_Wv': 64.0,
     'L3_xattn_Wo': 64.0,
     'L3_attn_q': 64.0,
     'L3_attn_k': 64.0,
     'L3_attn_log_decay': 64.0,
     'L3_attn_o_w': 64.0,
     'L3_ffn_gate_w': 64.0,
     'L3_ffn_wi_gate': 64.0,
     'L3_ffn_wi_up': 64.0,
     'L3_ffn_wo': 64.0,
     'L1_attn_Wv': 8.0,
     'L2_xattn_bk': 64.0}
    for name, (base, spread) in spreads.items():
        noise = np.random.default_rng([zlib.crc32(name.encode()), seed]).standard_normal(out[name].shape)
        drawn = base * np.exp(spread * noise) if base else spread * noise
        out[name] = jnp.asarray(drawn.astype(out[name].dtype))
    for name, factor in factors.items():
        out[name] = (out[name] * factor).astype(out[name].dtype)
    return out
```

```python
from contextlib import ExitStack

import numpy as np

import concourse.bass as bass
import concourse.mybir as mybir

F32 = mybir.dt.float32
I32 = mybir.dt.int32
ALU = mybir.AluOpType
ACT = mybir.ActivationFunctionType
X = mybir.AxisListType.X

P = 128
D = 256
KD = D // P
H = 16
DH = D // H
HH = H // KD
NK = 12544
TK = 112
HC = 896
CH = 2 * HC
NC = NK // CH
TC = CH // TK
TH = HC // TK
BANK = 512
E = 8
BIG = 3.0e38
MASKED = 1.0e30
CAPACITY = int(P / E * 1.25)

LAYERS = ["L0x", "L0a", "L0f", "L1x", "L1a", "L1f", "L2x", "L2a", "L2f", "L3x", "L3a", "L3f"]
FF = {"L0f": 704, "L2f": 1024, "L3f": 1024}
GATED = ("L0f", "L3f")

PACKS = {
    "L0x": dict(w1=512, w2=512, b=256),
    "L0a": dict(qkv=1536, gate=512, proj=512, ln_g=256, ln_b=256, b_qkv=768, b_gate=256, b_out=256),
    "L0f": dict(gate=16),
    "L1x": dict(w_qv=2048, w_sim=768, b_sim=1, b_out=256),
    "L1a": dict(qkv=1536, proj=512, ln_w=512, ln_b=512),
    "L1f": dict(ln_g=256, ln_b=256, b1=1024, b2=256),
    "L2x": dict(wq=512, wk=512, wv=512, proj=512, bq=256, bk=2, bv=256, b_out=256),
    "L2a": dict(qkv=1536, proj=512),
    "L2f": dict(gate=16, bias=8),
    "L3x": dict(wq=512, wk=512, wv=512, proj=512),
    "L3a": dict(proj=512, q=256, k=256, log_decay=16, norm=256),
    "L3f": dict(gate=16),
}
CONSTS = dict(ident=128, causal=128, causal_bias=128, steps=128, head=8, before=64)

NORM = {"dve": ["var", "xn", "xT"], "pool": ["rstd"], "pe": ["xnT"], "act": []}
NORM2 = {"dve": ["var2", "x2", "x2T"], "pool": ["rstd2"], "pe": ["x2T_ps"], "act": []}
TAIL = {"dve": ["o", "oT"], "pool": [], "pe": ["oT_ps", "out"], "act": []}


def stage_lists(layers):
    lists = {e: [] for e in ("pe", "dve", "act", "pool")}

    def add(layer, **stages):
        for e, names in stages.items():
            lists[e] += [f"{layer}.{n}" for n in names]

    for layer in layers:
        add(layer, **NORM)
        if layer == "L0x":
            add(layer, dve=["mean"], pe=["out"])
        elif layer == "L0a":
            add(layer, **NORM2)
            add(layer, pe=["gate_ps", "qkv_ps", "qkT_ps", "A_ps", "num_ps"],
                dve=["g", "qk", "qblk", "AT"], act=["sig"])
            add(layer, **TAIL)
        elif layer == "L2a":
            add(layer, pe=["qkv_ps", "qkT_ps", "A_ps", "num_ps"], dve=["neg", "qk", "qblk", "AT"], act=["elu"])
            add(layer, **TAIL)
        elif layer == "L1a":
            add(layer, pe=["qkv_ps", "qkT_ps", "S_ps", "pT_ps", "num_ps"],
                dve=["var2", "qk", "kblk", "sm", "pT"], act=["p"], pool=["rstd2"])
            add(layer, **TAIL)
        elif layer == "L3a":
            add(layer, pe=["num_ps"], dve=["abs", "onep", "ln", "V", "var2"], act=["e", "ln1p", "decay"],
                pool=["rstd2"])
            add(layer, **TAIL)
        elif layer == "L1x":
            add(layer, dve=["A", "AT", "max", "bat", "f", "fT"], pe=["AT_ps", "hc_ps", "fT_ps", "out"],
                pool=["gmax"], act=["bat"])
        elif layer == "L1f":
            add(layer, **NORM2)
            add(layer, pe=["z_ps", "yT_ps", "out"], dve=["w", "z", "yT"], act=["y"])
        elif layer in ("L2x", "L3x"):
            add(layer, pe=["q_ps", "qT_ps"], dve=["q", "qblk"])
            add(layer, **TAIL)
        elif layer == "L0f":
            add(layer, pe=["logit"], dve=["weights"])
        elif layer == "L2f":
            add(layer, pe=["logit"], dve=["logit", "weights", "var3"], act=["prob"], pool=["rstd3"])
        elif layer == "L3f":
            add(layer, pe=["logit", "pos"], dve=["logit", "onehot", "weights"], act=["prob"])
        add(layer, dve=["end"])
    return lists


def unit_groups():
    seq = []
    for h in range(H):
        if h % 4 == 1 and h > 1:
            seq.append(("O", (h - 5) // 4, 0, "dve"))
        seq += [("T", h, g, "act" if g % 2 == 0 else "dve") for g in range(4)]
    seq.append(("O", 3, 0, "dve"))
    return seq


GROUPS = unit_groups()
GROUP_AT = {g[:3]: n for n, g in enumerate(GROUPS)}
TAKEN = {e: [sum(g[3] == e for g in GROUPS[:n + 1]) for n in range(len(GROUPS))] for e in ("act", "dve")}
NG = len(GROUPS)


def build(nc, a, layers=LAYERS):
    ctx = ExitStack()
    with ctx:
        def sb(name, shape, dt=F32):
            return ctx.enter_context(nc.sbuf_tensor(name, shape, dt))

        def sem(name):
            return ctx.enter_context(nc.semaphore(name))

        S4 = ctx.enter_context(nc.psum_tensor("S4", [P, 4, BANK], F32))
        T2 = ctx.enter_context(nc.psum_tensor("T2", [P, 2, BANK], F32))
        O2 = ctx.enter_context(nc.psum_tensor("O2", [P, 2, BANK], F32))
        S4f = S4[:, :, :].rearrange("p b n -> p (b n)")

        x = sb("x", [P, D])
        xn = sb("xn", [P, D])
        x2 = sb("x2", [P, D])
        xT = sb("xT", [P, KD, P])
        x2T = sb("x2T", [P, KD, P])
        consts = sb("consts", [P, sum(CONSTS.values())])
        packs = sb("packs", [P, 2, max(sum(p.values()) for p in PACKS.values())])
        arena = sb("arena", [P, NK])
        ctx_in = sb("ctx_in", [P, 2, KD, HC])
        sc = sb("sc", [P, 2, CH])
        pT = sb("pT", [P, 4, BANK])
        o_sb = sb("o_sb", [P, 2, BANK])
        mask_bias = sb("mask_bias", [P, CH])
        fb = sb("fb", [P, 2, 3 * KD * 1024])
        work = sb("work", [P, 1536])
        small = sb("small", [P, 512])

        kT = arena[:, 0:KD * CH].rearrange("p (k n) -> p k n", k=KD)
        vv = arena[0:TK, KD * CH:KD * CH + TC * D].rearrange("p (t d) -> p t d", t=TC)
        at = KD * CH + TC * D
        blk = arena[:, at:at + H * P].rearrange("p (h n) -> p h n", h=H)
        mask_in = arena[:, at + H * P:at + H * P + CH]
        mats = sc[:, :, :].rearrange("p a n -> p (a n)")[:, 0:H * P]
        mats3 = mats.rearrange("p (h n) -> p h n", h=H)
        matsT = arena[:, 0:H * P]
        matsT3 = matsT.rearrange("p (h n) -> p h n", h=H)
        oT = arena[:, 2048:2048 + D].rearrange("p (k n) -> p k n", k=KD)
        halfT = arena[:, 2304:2304 + D].rearrange("p (k n) -> p k n", k=KD)
        vaug = arena[:, 2560:2560 + H * (DH + 1)].rearrange("p (h n) -> p h n", h=H)
        num = arena[:, 2832:2832 + H * (DH + 1)].rearrange("p (h n) -> p h n", h=H)
        hid = arena[:, 0:1024]
        hidT = arena[:, 1024:2048].rearrange("p (t n) -> p t n", t=E)
        gated = arena[:, 3200:4224]
        yacc = arena[:, 4224:4480]

        at = 0
        C = {}
        for name, w in CONSTS.items():
            C[name] = consts[:, at:at + w]
            at += w
        ident = C["ident"]

        def pk(layer, name, k=None):
            at = 0
            for n, w in PACKS[layer].items():
                if n == name:
                    break
                at += w
            piece = packs[:, layers.index(layer) % 2, at:at + w]
            return piece.rearrange("p (k n) -> p k n", k=k) if k else piece

        cols = [0]

        def take(w):
            cols[0] += w
            assert cols[0] <= 512
            return small[:, cols[0] - w:cols[0]]

        stats, mv, rstd, half = take(6), take(2), take(1), take(64)
        vsum, head_a, head_b, lam = take(32), take(32), take(32), take(16)
        n_old, n_half, n_new, l_new = take(16), take(16), take(16), take(16)
        alpha, l_sum, wts, wcur = take(16), take(16), take(8), take(2)
        maxes, sums, row, row_max = take(14), take(14), take(1), take(1)
        gmax, bat, rec, prob = take(1), take(1), take(1), take(8)
        rank, one0, one1 = take(8), take(8), take(8)
        eye_a, mean, tick = take(64), take(2), take(1)
        parts4 = sb("parts", [P, NC, 2, KD])
        oc = work[:, 0:256]
        acc = work[:, 256:512]

        minus_half = sb("minus_half", [P, 2 * H])
        filled = sem("minus_half_filled")

        STAGES = stage_lists(layers)
        stages = {e: sem(f"{e}_stages") for e in STAGES}
        counted = {e: 0 for e in STAGES}

        def done(e, ins, name):
            assert STAGES[e][counted[e]] == name, (e, name, STAGES[e][counted[e]])
            counted[e] += 1
            ins.then_inc(stages[e], 1)

        def need(eng, e, name):
            eng.wait_ge(stages[e], STAGES[e].index(name) + 1)

        consts_in = sem("consts_in")
        x_in = sem("x_in")
        pack_in = [sem(f"pack{n}_in") for n in range(2)]
        stored = sem("stored")
        own = {e: sem(f"{e}_own") for e in ("dve", "act")}
        owned = {"dve": 0, "act": 0}

        def packed(eng, layer):
            n = layers.index(layer)
            eng.wait_ge(pack_in[n % 2], 16 * (n // 2 + 1))

        L = {}

        def sems(layer, *names):
            L[layer] = {n: sem(f"{layer}_{n}") for n in names}

        for layer in layers:
            if layer == "L0x":
                sems(layer, "ctx_in0", "ctx_in1", "ctx_in2", "summed")
            elif layer == "L1x":
                sems(layer, "ctx_in0", "ctx_in1", "s_ready", "s_taken", "p_ready", "nat_in0", "nat_in1", "t_ready", "t_dve", "t_act",
                     "pv_ready", "pv_taken")
            elif layer in ("L2x", "L3x"):
                sems(layer, "ctx_in0", "ctx_in1", "mask_in", "mask_taken", "kp_ready", "kp_taken", "vp_ready", "vp_taken",
                     "s_ready", "s_taken", "p_ready", "t_ready", "t_dve", "t_act", "pv_done", "o_taken",
                     "delta", "alpha", "finished")
            elif layer == "L1f":
                sems(layer, "q_in")
            elif layer in FF:
                sems(layer, "w_in0", "w_in1", "g_ready", "act_done", "h_ready", "t_ready", "t_dve", "t_act", "y_ready",
                     "y_taken")

        block = ctx.enter_context(nc.Block())

        @block.sync
        def _(sp):
            def load_pack(layer):
                n = layers.index(layer)
                if n >= 2:
                    need(sp, "dve", f"{layers[n - 2]}.end")
                w = sum(PACKS[layer].values())
                sp.dma_start(packs[:, n % 2, 0:w], a[f"pack_{layer}"]).then_inc(pack_in[n % 2], 16)

            sp.dma_start(x[:, :], a["x"]).then_inc(x_in, 16)
            sp.dma_start(consts[:, :], a["consts"]).then_inc(consts_in, 16)
            for layer in layers[:2]:
                load_pack(layer)

            def load_ctx(s, n, half):
                sp.dma_start(ctx_in[:, half], a["ctx_cols"][bass.ds(n, 1)].rearrange(
                    "a p k n -> p (a k) n")).then_inc(s, 16)

            def load_expert(layer, e, b):
                F = FF[layer]
                m = KD * (2 if layer in GATED else 1) * F
                s = L[layer][f"w_in{b}"]
                sp.dma_start(fb[:, b, 0:m], a[f"up_{layer}"][bass.ds(e, 1)].rearrange(
                    "a p n -> p (a n)")).then_inc(s, 16)
                sp.dma_start(fb[0:F // E, b, m:m + E * D], a[f"down_{layer}"][bass.ds(e, 1)].rearrange(
                    "a p n -> p (a n)")).then_inc(s, 16)

            for i, layer in enumerate(layers):
                prev = layers[i - 1] if i else None
                if layer == "L0x":
                    s = L[layer]
                    bufs = [ctx_in[:, :, :, :].rearrange("p h k n -> p (h k n)"),
                            sc[:, :, :].rearrange("p a n -> p (a n)"), arena[:, 0:KD * CH]]
                    for c in range(NC):
                        if c >= 3:
                            sp.wait_ge(s["summed"], c - 2)
                        for half in range(2):
                            dst = bufs[c % 3].rearrange("p (h n) -> p h n", h=2)[:, half]
                            sp.dma_start(dst, a["ctx_cols"][2 * c + half].rearrange("p k n -> p (k n)")) \
                                .then_inc(s[f"ctx_in{c % 3}"], 16)
                    if "L0f" in layers:
                        for e in range(2):
                            load_expert("L0f", e, e)
                elif layer == "L1x":
                    s = L[layer]
                    if prev:
                        need(sp, "dve", f"{prev}.end")
                    for half in range(2):
                        load_ctx(s[f"ctx_in{half}"], half, half)
                    with sp.Fori(1, NC) as c:
                        for half in range(2):
                            sp.wait_ge(s["s_ready"], 2 * c - 1 + half)
                            load_ctx(s[f"ctx_in{half}"], 2 * c + half, half)
                    def load_nat(n, half):
                        sp.dma_start(fb[0:TK, half, 0:TH * D], a["ctx_rows"][bass.ds(n, 1)].rearrange(
                            "a p n -> p (a n)")).then_inc(s[f"nat_in{half}"], 16)
                    for half in range(2):
                        load_nat(half, half)
                    with sp.Fori(1, NC) as c:
                        for half in range(2):
                            sp.wait_ge(s["pv_ready"], 2 * c - 1 + half)
                            load_nat(2 * c + half, half)
                elif layer in ("L2x", "L3x"):
                    s = L[layer]
                    if prev:
                        need(sp, "dve", f"{prev}.end")

                    def load_mask(c):
                        dst = mask_in.bitcast(I32) if layer == "L2x" else mask_in
                        sp.dma_start(dst, a[f"mask_{layer}"][bass.ds(c, 1)].rearrange("a p n -> p (a n)")) \
                            .then_inc(s["mask_in"], 16)

                    for half in range(2):
                        load_ctx(s[f"ctx_in{half}"], half, half)
                    load_mask(0)
                    if i + 1 < len(layers):
                        load_pack(layers[i + 1])
                    if i + 2 < len(layers):
                        for e in range(2):
                            load_expert(layers[i + 2], e, e)
                    with sp.Fori(1, NC) as c:
                        sp.wait_ge(s["mask_taken"], c)
                        load_mask(c)
                        sp.wait_ge(s["vp_ready"], 8 * c)
                        for half in range(2):
                            load_ctx(s[f"ctx_in{half}"], 2 * c + half, half)
                elif layer == "L1f":
                    s = L[layer]
                    if prev:
                        need(sp, "dve", f"{prev}.end")
                    for b in range(2):
                        sp.dma_start(fb[:, b, 0:2048].bitcast(I32), a[f"fc{b + 1}_q"]).then_inc(s["q_in"], 16)
                        sp.dma_start(fb[:, b, 2048:4096], a[f"fc{b + 1}_scales"]).then_inc(s["q_in"], 16)
                elif layer in FF:
                    s = L[layer]
                    if i < 2:
                        for e in range(2):
                            load_expert(layer, e, e)
                    with sp.Fori(1, E // 2) as n:
                        for b in range(2):
                            sp.wait_ge(s["y_ready"], 2 * n + (b - 1))
                            load_expert(layer, 2 * n + b, b)
                if i + 2 < len(layers) and layers[i + 1] not in ("L2x", "L3x"):
                    load_pack(layers[i + 2])

            need(sp, "dve", f"{layers[-1]}.end")
            sp.dma_start(a["out"], x[:, :]).then_inc(stored, 16)
            sp.wait_ge(stored, 16)

        @block.gpsimd
        def _(pool):
            def power(layer, stage, of, t, out):
                need(pool, "dve", f"{layer}.{of}")
                done("pool", nc.gpsimd.tensor_tensor(out, t, minus_half[:, 0:t.shape[1]], ALU.pow), f"{layer}.{stage}")

            nc.gpsimd.memset(minus_half[:, :], -0.5).then_inc(filled, 1)
            pool.wait_ge(filled, 1)
            for layer in layers:
                power(layer, "rstd", "var", mv[:, 1:2], rstd)
                if layer in ("L0a", "L1f"):
                    power(layer, "rstd2", "var2", mv[:, 1:2], rstd)
                elif layer == "L1a":
                    power(layer, "rstd2", "var2", head_a, head_b)
                elif layer == "L3a":
                    power(layer, "rstd2", "var2", mv[:, 1:2], rstd)
                elif layer == "L2f":
                    power(layer, "rstd3", "var3", mv[:, 1:2], rstd)
                elif layer == "L1x":
                    need(pool, "dve", f"{layer}.max")
                    done("pool", nc.gpsimd.partition_all_reduce(gmax, row_max, P, bass.bass_isa.ReduceOp.max),
                         f"{layer}.gmax")

        @block.tensor
        def _(pe):
            mm = nc.tensor.matmul

            def transposes(out, src, n, w=P):
                for t in range(n):
                    last = nc.tensor.transpose(out[0:w, t * P:(t + 1) * P], src[:, t * w:(t + 1) * w], ident)
                return last

            def product(out, lhsT, rhs, n=KD):
                for k in range(n):
                    last = mm(out, lhsT[:, k, :], rhs[:, k, :], start=(k == 0), stop=(k == n - 1))
                return last

            def norm(layer):
                need(pe, "dve", f"{layer}.xn")
                done("pe", transposes(T2[:, 0], xn, KD), f"{layer}.xnT")

            def norm2(layer):
                need(pe, "dve", f"{layer}.x2")
                done("pe", transposes(T2[:, 1], x2, KD), f"{layer}.x2T_ps")

            def tail(layer):
                need(pe, "dve", f"{layer}.o")
                done("pe", transposes(T2[:, 1], x2, KD), f"{layer}.oT_ps")
                need(pe, "dve", f"{layer}.oT")
                done("pe", product(O2[:, 0, 0:D], oT, pk(layer, "proj", KD)), f"{layer}.out")

            def qkv(layer, src):
                w = pk(layer, "qkv", KD)
                product(S4[:, 0], src, w[:, :, 0:2 * D])
                done("pe", product(S4[:, 1, 0:D], src, w[:, :, 2 * D:3 * D]), f"{layer}.qkv_ps")
                need(pe, "dve", f"{layer}.qk")
                done("pe", transposes(T2[:, 0], work, 2 * KD), f"{layer}.qkT_ps")

            def heads_products(stat, rhs):
                for b in range(4):
                    last = mm(S4[:, b], stat[:, b // 2, :], rhs[:, 4 * b:4 * b + 4, :], start=True, stop=True)
                return last

            def cross(layer):
                s = L[layer]
                wq, wk, wv = (pk(layer, n, KD) for n in ("wq", "wk", "wv"))
                need(pe, "dve", f"{layer}.xT")
                done("pe", product(O2[:, 0, 0:D], xT, wq), f"{layer}.q_ps")
                need(pe, "dve", f"{layer}.q")
                done("pe", transposes(T2[:, 1], x2, KD), f"{layer}.qT_ps")

                def key_block(n):
                    hf, nb = divmod(n, 4)
                    for k in range(KD):
                        last = mm(S4[:, n % 4, 0:HC // 2], wk[:, k, hf * P:(hf + 1) * P],
                                  ctx_in[:, nb // 2, k, (nb % 2) * (HC // 2):(nb % 2 + 1) * (HC // 2)],
                                  start=(k == 0), stop=(k == KD - 1))
                    last.then_inc(s["kp_ready"], 1)

                def scores(h):
                    for half in range(2):
                        for n0, n1 in ((0, BANK), (BANK, HC)):
                            last = mm(S4f[:, half * 2 * BANK + n0:half * 2 * BANK + n1], blk[:, h, :],
                                      kT[:, h // HH, half * HC + n0:half * HC + n1], start=True, stop=True)
                        last.then_inc(s["s_ready"], 1)

                for half in range(2):
                    pe.wait_ge(s[f"ctx_in{half}"], 16)
                for n in range(8):
                    if n >= 4:
                        pe.wait_ge(s["kp_taken"], n - 3)
                    key_block(n)
                need(pe, "dve", f"{layer}.qblk")

                def chunk(c, last_chunk):
                    pe.wait_ge(s["kp_taken"], 8 * c + 8)
                    for b in range(8):
                        if b >= 4:
                            pe.wait_ge(s["vp_taken"], 8 * c + (b - 3))
                        for t in (2 * b, 2 * b + 1):
                            for k in range(KD):
                                last = mm(S4[0:TK, b % 4, (t % 2) * D:(t % 2 + 1) * D],
                                          ctx_in[:, t // TH, k, (t % TH) * TK:(t % TH + 1) * TK], wv[:, k, :],
                                          start=(k == 0), stop=(k == KD - 1))
                        last.then_inc(s["vp_ready"], 1)
                    pe.wait_ge(s["vp_taken"], 8 * c + 8)
                    scores(0)

                    def values(h, g):
                        e = GROUPS[GROUP_AT["T", h, g]][3]
                        pe.wait_ge(s[f"t_{e}"], TAKEN[e][-1] * c + TAKEN[e][GROUP_AT["T", h, g]])
                        quad = h // 4
                        if h % 4 == 0 and g == 0 and quad >= 2:
                            pe.wait_ge(s["o_taken"], 4 * c + (quad - 1))
                        for i in range(4):
                            last = mm(O2[32 * i:32 * i + 32, quad % 2, (h % 4) * P:(h % 4 + 1) * P],
                                      vv[:, 4 * g + i, (h // 2) * 32:(h // 2 + 1) * 32],
                                      pT[0:TK, g, i * P:(i + 1) * P], start=(g == 0), stop=(g == 3))
                        last.then_inc(s["pv_done"], 1)

                    waiting = None
                    for n, (kind, h, g, _) in enumerate(GROUPS):
                        if kind == "T" and g == 0:
                            if h < H - 1:
                                for half in range(2):
                                    pe.wait_ge(s["s_taken"], 32 * c + (2 * h + 1 + half))
                                    for n0, n1 in ((0, BANK), (BANK, HC)):
                                        last = mm(S4f[:, half * 2 * BANK + n0:half * 2 * BANK + n1],
                                                  blk[:, h + 1, :],
                                                  kT[:, (h + 1) // HH, half * HC + n0:half * HC + n1],
                                                  start=True, stop=True)
                                    last.then_inc(s["s_ready"], 1)
                            elif not last_chunk:
                                for half in range(2):
                                    pe.wait_ge(s[f"ctx_in{half}"], 16 * c + 32)
                                pe.wait_ge(s["s_taken"], 32 * c + 32)
                                for m in range(4):
                                    key_block(m)
                            pe.wait_ge(s["p_ready"], 16 * c + (h + 1))
                        if kind == "O":
                            if n == NG - 1:
                                values(*waiting)
                                waiting = None
                            pe.wait_ge(s["o_taken"], 4 * c + (h + 1))
                        if n >= 2:
                            e = GROUPS[n - 2][3]
                            pe.wait_ge(s[f"t_{e}"], TAKEN[e][-1] * c + TAKEN[e][n - 2])
                        if kind == "T":
                            last = transposes(T2[:, n % 2], sc[:, h % 2, 4 * g * TK:(4 * g + 4) * TK], 4, TK)
                        else:
                            last = transposes(T2[:, n % 2], o_sb[:, h % 2], 4)
                        last.then_inc(s["t_ready"], 1)
                        if waiting:
                            values(*waiting)
                            waiting = None
                        if kind == "T":
                            waiting = (h, g)
                    if not last_chunk:
                        for m in range(4, 8):
                            pe.wait_ge(s["kp_taken"], 8 * c + (8 + m - 3))
                            key_block(m)
                    for e in ("act", "dve"):
                        pe.wait_ge(s[f"t_{e}"], TAKEN[e][-1] * c + TAKEN[e][-1])

                with pe.Fori(0, NC - 1) as c:
                    chunk(c, False)
                chunk(NC - 1, True)
                tail(layer)

            def experts(layer):
                s = L[layer]
                F = FF[layer]
                m = KD * F
                need(pe, "dve", f"{layer}.weights")

                def expert(e, b, n):
                    pe.wait_ge(s[f"w_in{b}"], 32 * n + 32)
                    for j in range(2 if layer in GATED else 1):
                        w = fb[:, b, j * m:(j + 1) * m].rearrange("p (k n) -> p k n", k=KD)
                        for i in range(2):
                            last = product(S4[:, 2 * j + i, 0:F // 2], xT, w[:, :, i * F // 2:(i + 1) * F // 2])
                        last.then_inc(s["g_ready"], 1)
                    w = fb[0:F // E, b, (m * (2 if layer in GATED else 1)):][:, 0:E * D] \
                        .rearrange("p (t n) -> p t n", t=E)
                    pe.wait_ge(s["h_ready"], e + 1)
                    for j in range(2):
                        last = transposes(T2[:, j], hid[:, j * F // 2:(j + 1) * F // 2], 4, F // E)
                        last.then_inc(s["t_ready"], 1)
                    pe.wait_ge(s["t_dve"], e + 1)
                    pe.wait_ge(s["t_act"], e + 1)
                    for t in range(E):
                        last = mm(O2[:, b, 0:D], hidT[0:F // E, t, :], w[:, t, :], start=(t == 0), stop=(t == E - 1))
                    last.then_inc(s["y_ready"], 1)

                with pe.Fori(0, E // 2) as n:
                    for b in range(2):
                        expert(2 * n + b, b, n)

            pe.wait_ge(consts_in, 16)
            for layer in layers:
                norm(layer)
                packed(pe, layer)
                if layer == "L0x":
                    need(pe, "dve", f"{layer}.xT")
                    for k in range(KD):
                        mm(O2[:, 0, 0:D], xT[:, k, :], pk(layer, "w1", KD)[:, k, :], start=(k == 0), stop=False)
                    need(pe, "dve", f"{layer}.mean")
                    for k in range(KD):
                        last = mm(O2[:, 0, 0:D], x2T[:, k, :], pk(layer, "w2", KD)[:, k, :], start=False,
                                  stop=(k == KD - 1))
                    done("pe", last, f"{layer}.out")
                elif layer == "L0a":
                    norm2(layer)
                    need(pe, "dve", f"{layer}.xT")
                    done("pe", product(O2[:, 0, 0:D], xT, pk(layer, "gate", KD)), f"{layer}.gate_ps")
                    need(pe, "dve", f"{layer}.x2T")
                    qkv(layer, x2T)
                elif layer in ("L1a", "L2a"):
                    need(pe, "dve", f"{layer}.xT")
                    qkv(layer, xT)
                if layer in ("L0a", "L2a"):
                    need(pe, "dve", f"{layer}.qblk")
                    done("pe", heads_products(halfT, blk), f"{layer}.A_ps")
                    need(pe, "dve", f"{layer}.AT")
                    for h in range(H):
                        last = mm(O2[:, 1, h * (DH + 1):(h + 1) * (DH + 1)], mats3[:, h, :], vaug[:, h, :],
                                  start=True, stop=True)
                    done("pe", last, f"{layer}.num_ps")
                    tail(layer)
                elif layer == "L1a":
                    need(pe, "dve", f"{layer}.kblk")
                    done("pe", heads_products(halfT, blk), f"{layer}.S_ps")
                    need(pe, "act", f"{layer}.p")
                    for b in range(4):
                        last = transposes(S4[:, b], mats[:, b * BANK:(b + 1) * BANK], 4)
                    done("pe", last, f"{layer}.pT_ps")
                    need(pe, "dve", f"{layer}.pT")
                    for h in range(H):
                        last = mm(O2[:, 1, h * DH:(h + 1) * DH], matsT3[:, h, :], vaug[:, h, 0:DH],
                                  start=True, stop=True)
                    done("pe", last, f"{layer}.num_ps")
                    tail(layer)
                elif layer == "L3a":
                    need(pe, "dve", f"{layer}.V")
                    for h in range(H):
                        last = mm(O2[:, 1, h * DH:(h + 1) * DH], mats3[:, h, :], vaug[:, h, 0:DH],
                                  start=True, stop=True)
                    done("pe", last, f"{layer}.num_ps")
                    tail(layer)
                elif layer == "L1f":
                    norm2(layer)
                    need(pe, "dve", f"{layer}.x2T")
                    need(pe, "dve", f"{layer}.w")
                    w1 = fb[:, 0, 0:2048].rearrange("p (k n) -> p k n", k=KD)
                    w2 = fb[:, 1, 0:2048].rearrange("p (t n) -> p t n", t=8)
                    for i in range(2):
                        last = product(S4[:, i], x2T, w1[:, :, i * BANK:(i + 1) * BANK])
                    done("pe", last, f"{layer}.z_ps")
                    need(pe, "act", f"{layer}.y")
                    for i in range(2):
                        last = transposes(S4[:, 2 + i], hid[:, i * BANK:(i + 1) * BANK], 4)
                    done("pe", last, f"{layer}.yT_ps")
                    need(pe, "dve", f"{layer}.yT")
                    done("pe", product(O2[:, 0, 0:D], hidT, w2, 8), f"{layer}.out")
                elif layer in ("L2x", "L3x"):
                    cross(layer)
                elif layer in FF:
                    need(pe, "dve", f"{layer}.xT")
                    done("pe", product(O2[:, 0, 0:E], xT, pk(layer, "gate", KD)), f"{layer}.logit")
                    if layer == "L3f":
                        need(pe, "dve", f"{layer}.onehot")
                        mm(O2[:, 1, 0:E], C["causal"], one0, start=True, stop=True)
                        done("pe", mm(O2[:, 1, E:2 * E], C["causal"], one1, start=True, stop=True), f"{layer}.pos")
                    experts(layer)
                elif layer == "L1x":
                    s = L[layer]
                    need(pe, "dve", f"{layer}.A")
                    done("pe", transposes(T2[:, 1], x2, KD), f"{layer}.AT_ps")
                    need(pe, "dve", f"{layer}.AT")

                    def sim(c, first):
                        for half in range(2):
                            pe.wait_ge(s[f"ctx_in{half}"], 16 * c + 16)
                            if not first:
                                pe.wait_ge(s["s_taken"], 2 * c - 1 + half)
                            for n0, n1 in ((0, BANK), (BANK, HC)):
                                for k in range(KD):
                                    last = mm(S4f[:, half * 2 * BANK + n0:half * 2 * BANK + n1], x2T[:, k, :],
                                              ctx_in[:, half, k, n0:n1], start=(k == 0), stop=(k == KD - 1))
                            last.then_inc(s["s_ready"], 1)

                    sim(0, True)
                    with pe.Fori(1, NC) as c:
                        sim(c, False)

                    def attend(c, first):
                        for half in range(2):
                            pe.wait_ge(s["p_ready"], 2 * c + half + 1)
                            if half or not first:
                                pe.wait_ge(s["t_dve"], 2 * c + half)
                                pe.wait_ge(s["t_act"], 2 * c + half)
                            for g in range(2):
                                last = transposes(T2[:, g], sc[:, half, 4 * g * TK:(4 * g + 4) * TK], 4, TK)
                                last.then_inc(s["t_ready"], 1)
                            pe.wait_ge(s[f"nat_in{half}"], 16 * c + 16)
                            if not first:
                                pe.wait_ge(s["pv_taken"], 2 * c - 1 + half)
                            for g in range(2):
                                pe.wait_ge(s["t_act" if g else "t_dve"], 2 * c + half + 1)
                                for i in range(4):
                                    t = 4 * g + i
                                    last = mm(O2[:, half, 0:D], pT[0:TK, 2 * half + g, i * P:(i + 1) * P],
                                              fb[0:TK, half, t * D:(t + 1) * D], start=(t == 0), stop=(t == TH - 1))
                            last.then_inc(s["pv_ready"], 1)

                    attend(0, True)
                    with pe.Fori(1, NC) as c:
                        attend(c, False)
                    need(pe, "dve", f"{layer}.bat")
                    done("pe", mm(O2[:, 0, 0:D + 1], mats3[:, 0, :], work[:, 512:512 + D + 1], start=True, stop=True),
                         f"{layer}.hc_ps")
                    need(pe, "dve", f"{layer}.f")
                    transposes(S4[:, 0], arena[:, 0:512], 4)
                    done("pe", transposes(S4[:, 1], arena[:, 512:768], 2), f"{layer}.fT_ps")
                    need(pe, "dve", f"{layer}.fT")
                    w = pk(layer, "w_qv", 8)
                    fT = arena[:, 1024:1024 + 768].rearrange("p (k n) -> p k n", k=6)
                    for k in range(8):
                        last = mm(O2[:, 1, 0:D], xT[:, k, :] if k < 2 else fT[:, k - 2, :], w[:, k, :],
                                  start=(k == 0), stop=(k == 7))
                    done("pe", last, f"{layer}.out")

        @block.scalar
        def _(act):
            def cross(layer):
                s = L[layer]
                bias = pk(layer, "bk") if layer == "L2x" else None

                def keys(n, count):
                    act.wait_ge(s["kp_ready"], count)
                    hf, nb = divmod(n, 4)
                    dst = kT[:, hf, nb * (HC // 2):(nb + 1) * (HC // 2)]
                    if bias is None:
                        ins = nc.scalar.activation(dst, S4[:, n % 4, 0:HC // 2], ACT.Copy)
                    else:
                        ins = nc.scalar.activation(dst, S4[:, n % 4, 0:HC // 2], ACT.Identity, bias=bias[:, hf:hf + 1])
                    ins.then_inc(s["kp_taken"], 1)

                def take_group(c, n):
                    kind, h, g, _ = GROUPS[n]
                    act.wait_ge(s["t_ready"], NG * c + (n + 1))
                    if h >= 1:
                        act.wait_ge(s["pv_done"], 64 * c + (4 * (h - 1) + g + 1))
                    nc.scalar.activation(pT[0:TK, g, :], T2[0:TK, n % 2, :], ACT.Copy).then_inc(s["t_act"], 1)

                def take_quad(c, quad):
                    act.wait_ge(s["pv_done"], 64 * c + 16 * (quad + 1))
                    if quad >= 2:
                        act.wait_ge(s["t_ready"], NG * c + (GROUP_AT["O", quad - 2, 0] + 1))
                    nc.scalar.activation(o_sb[:, quad % 2, :], O2[:, quad % 2, :], ACT.Copy).then_inc(s["o_taken"], 1)

                if bias is not None:
                    packed(act, layer)
                for n in range(8):
                    keys(n, n + 1)

                def chunk(c, last_chunk):
                    for h in range(H):
                        for g in (0, 2) if h else ():
                            take_group(c, GROUP_AT["T", h - 1, g])
                        act.wait_ge(s["s_taken"], 32 * c + (2 * h + 2))
                        nc.scalar.activation(sc[:, h % 2, :], sc[:, h % 2, :], ACT.Exp, bias=n_new[:, h:h + 1],
                                             scale=-1.0, accum_out=l_new[:, h:h + 1]).then_inc(s["p_ready"], 1)
                        if h % 4 == 0 and h:
                            take_quad(c, h // 4 - 1)
                    act.wait_ge(s["delta"], c + 1)
                    nc.scalar.activation(alpha, alpha, ACT.Exp).then_inc(s["alpha"], 1)
                    if not last_chunk:
                        for n in range(4):
                            keys(n, 8 * c + (8 + n + 1))
                    for g in (0, 2):
                        take_group(c, GROUP_AT["T", H - 1, g])
                    take_quad(c, 3)
                    if not last_chunk:
                        for n in range(4, 8):
                            keys(n, 8 * c + (8 + n + 1))

                with act.Fori(0, NC - 1) as c:
                    chunk(c, False)
                chunk(NC - 1, True)

            def experts(layer):
                s = L[layer]
                F = FF[layer]
                per = 2 if layer in GATED else 1
                fn = ACT.Silu if layer in GATED else ACT.Gelu

                def expert(e):
                    act.wait_ge(s["g_ready"], per * e + 1)
                    nc.scalar.activation(gated[:, 0:F].rearrange("p (i n) -> p i n", i=2), S4[:, 0:2, 0:F // 2], fn) \
                        .then_inc(s["act_done"], 1)
                    act.wait_ge(s["t_ready"], 2 * e + 2)
                    nc.scalar.activation(hidT[0:F // E, 4:8, :].rearrange("p t n -> p (t n)"), T2[0:F // E, 1, :],
                                         ACT.Copy).then_inc(s["t_act"], 1)

                with act.Fori(0, E // 2) as n:
                    for b in range(2):
                        expert(2 * n + b)

            for layer in layers:
                if layer == "L0a":
                    need(act, "dve", f"{layer}.g")
                    done("act", nc.scalar.activation(x2[:, :], x2[:, :], ACT.Sigmoid, accum_out=row), f"{layer}.sig")
                elif layer == "L2a":
                    need(act, "dve", f"{layer}.neg")
                    done("act", nc.scalar.activation(work[:, 512:1024], work[:, 512:1024], ACT.Exp), f"{layer}.elu")
                elif layer == "L1a":
                    need(act, "dve", f"{layer}.sm")
                    done("act", nc.scalar.activation(mats, mats, ACT.Exp), f"{layer}.p")
                elif layer == "L3a":
                    need(act, "dve", f"{layer}.abs")
                    done("act", nc.scalar.activation(head_a[:, 0:H], head_b[:, 0:H], ACT.Exp, scale=-1.0),
                         f"{layer}.e")
                    need(act, "dve", f"{layer}.onep")
                    done("act", nc.scalar.activation(head_b[:, 0:H], head_a[:, 0:H], ACT.Ln), f"{layer}.ln1p")
                    need(act, "dve", f"{layer}.ln")
                    for h in range(H):
                        last = nc.scalar.activation(mats3[:, h, :], C["steps"], ACT.Exp, scale=lam[:, h:h + 1])
                    done("act", last, f"{layer}.decay")
                elif layer == "L1f":
                    need(act, "dve", f"{layer}.z")
                    done("act", nc.scalar.activation(hid, hid, ACT.Silu), f"{layer}.y")
                elif layer in ("L2x", "L3x"):
                    cross(layer)
                elif layer in FF:
                    if layer != "L0f":
                        need(act, "dve", f"{layer}.logit")
                        done("act", nc.scalar.activation(prob, prob, ACT.Exp, accum_out=row), f"{layer}.prob")
                    experts(layer)
                elif layer == "L1x":
                    s = L[layer]
                    need(act, "pool", f"{layer}.gmax")
                    need(act, "dve", f"{layer}.max")

                    def soften(c, first):
                        for half in range(2):
                            if not first:
                                act.wait_ge(s["t_ready"], 4 * c + (2 * half - 2))
                            nc.scalar.activation(sc[:, half, 0:HC], arena[:, bass.ds(c * CH + half * HC, HC)], ACT.Exp,
                                                 bias=rec, accum_out=sums[:, bass.ds(2 * c + half, 1)]) \
                                .then_inc(s["p_ready"], 1)
                            act.wait_ge(s["t_ready"], 4 * c + (2 * half + 2))
                            if not first:
                                act.wait_ge(s["pv_ready"], 2 * c + half - 1)
                            nc.scalar.activation(pT[0:TK, 2 * half + 1, :], T2[0:TK, 1, :], ACT.Copy) \
                                .then_inc(s["t_act"], 1)

                    soften(0, True)
                    with act.Fori(1, NC) as c:
                        soften(c, False)
                    done("act", nc.scalar.activation(bat, row_max, ACT.Exp, bias=gmax, scale=1.0), f"{layer}.bat")

        @block.vector
        def _(dve):
            V = nc.vector

            def link(ins):
                owned["dve"] += 1
                ins.then_inc(own["dve"], 1)
                dve.wait_ge(own["dve"], owned["dve"])

            def bcast(ap, n, inner=True):
                m = ap.shape[1]
                if inner:
                    return ap.unsqueeze(2).to_broadcast([P, m, n])
                return ap.unsqueeze(1).to_broadcast([P, n, m])

            def variance(src, layer, stage):
                link(V.bn_stats(stats, src))
                link(V.bn_aggr(mv, stats))
                done("dve", V.tensor_scalar(mv[:, 1:2], mv[:, 1:2], 1e-5, None, ALU.add), f"{layer}.{stage}")

            def scaled(out, src):
                return V.tensor_scalar(out, src, mv[:, 0:1], rstd, ALU.subtract, ALU.mult)

            def norm(layer):
                variance(x[:, :], layer, "var")
                need(dve, "pool", f"{layer}.rstd")
                done("dve", scaled(xn[:, :], x[:, :]), f"{layer}.xn")
                need(dve, "pe", f"{layer}.xnT")
                done("dve", V.tensor_copy(xT[:, :, :].rearrange("p k n -> p (k n)"), T2[:, 0, 0:D]), f"{layer}.xT")

            def norm2(layer):
                packed(dve, layer)
                variance(xn[:, :], layer, "var2")
                need(dve, "pool", f"{layer}.rstd2")
                link(scaled(x2[:, :], xn[:, :]))
                link(V.tensor_tensor(x2[:, :], x2[:, :], pk(layer, "ln_g"), ALU.mult))
                done("dve", V.tensor_tensor(x2[:, :], x2[:, :], pk(layer, "ln_b"), ALU.add), f"{layer}.x2")
                need(dve, "pe", f"{layer}.x2T_ps")
                done("dve", V.tensor_copy(x2T[:, :, :].rearrange("p k n -> p (k n)"), T2[:, 1, 0:D]), f"{layer}.x2T")

            def tail(layer):
                need(dve, "pe", f"{layer}.oT_ps")
                done("dve", V.tensor_copy(oT.rearrange("p k n -> p (k n)"), T2[:, 1, 0:D]), f"{layer}.oT")
                need(dve, "pe", f"{layer}.out")
                residual(layer, O2[:, 0, 0:D])

            def residual(layer, out):
                if "b_out" in PACKS[layer] or "b" in PACKS[layer]:
                    link(V.tensor_tensor(x[:, :], x[:, :], pk(layer, "b_out" if "b_out" in PACKS[layer] else "b"),
                                         ALU.add))
                done("dve", V.tensor_tensor(x[:, :], out, x[:, :], ALU.add), f"{layer}.end")
                need(dve, "dve", f"{layer}.end")

            def spread(psum, stage):
                for k in range(KD):
                    last = V.tensor_tensor(blk[:, k * HH:(k + 1) * HH, :], bcast(psum[:, k * P:(k + 1) * P], HH, False),
                                           bcast(C["head"], P), ALU.mult)
                done("dve", last, stage)

            def ranks(src):
                a3 = half.rearrange("p (e j) -> p e j", e=E)
                b3 = eye_a.rearrange("p (e j) -> p e j", e=E)
                link(V.tensor_tensor(b3, bcast(src, E, False), bcast(src, E), ALU.is_equal))
                link(V.tensor_tensor(eye_a, eye_a, C["before"], ALU.mult))
                link(V.tensor_tensor(a3, bcast(src, E, False), bcast(src, E), ALU.is_gt))
                link(V.tensor_tensor(half, half, eye_a, ALU.add))
                link(V.tensor_reduce(rank, a3, X, ALU.add))

            def softmax_gate(layer, bias):
                need(dve, "pe", f"{layer}.logit")
                if bias is None:
                    link(V.tensor_copy(prob, O2[:, 0, 0:E]))
                else:
                    link(V.tensor_tensor(prob, O2[:, 0, 0:E], bias, ALU.add))
                link(V.tensor_reduce(rec, prob, X, ALU.max))
                done("dve", V.tensor_scalar(prob, prob, rec, None, ALU.subtract), f"{layer}.logit")
                need(dve, "act", f"{layer}.prob")
                link(V.reciprocal(rec, row))
                link(V.tensor_scalar(prob, prob, rec, None, ALU.mult))

            def experts(layer):
                s = L[layer]
                F = FF[layer]
                per = 2 if layer in GATED else 1

                def expert(e, b):
                    V.tensor_copy(wcur[:, b:b + 1], wts[:, bass.ds(e, 1)]).then_inc(s["y_taken"], 1)
                    dve.wait_ge(s["y_taken"], 3 * e + 1)
                    dve.wait_ge(s["act_done"], e + 1)
                    if layer in GATED:
                        dve.wait_ge(s["g_ready"], per * e + per)
                        V.scalar_tensor_tensor(
                            hid[:, 0:F].rearrange("p (i n) -> p i n", i=2), S4[:, 2:4, 0:F // 2], wcur[:, b:b + 1],
                            gated[:, 0:F].rearrange("p (i n) -> p i n", i=2), ALU.mult, ALU.mult) \
                            .then_inc(s["h_ready"], 1)
                    else:
                        V.tensor_scalar(hid[:, 0:F], gated[:, 0:F], wcur[:, b:b + 1], None, ALU.mult) \
                            .then_inc(s["h_ready"], 1)
                    dve.wait_ge(s["t_ready"], 2 * e + 1)
                    V.tensor_copy(hidT[0:F // E, 0:4, :].rearrange("p t n -> p (t n)"), T2[0:F // E, 0, :]) \
                        .then_inc(s["t_dve"], 1)
                    dve.wait_ge(s["y_ready"], e + 1)
                    V.tensor_tensor(yacc, O2[:, b, 0:D], yacc, ALU.add).then_inc(s["y_taken"], 2)
                    dve.wait_ge(s["y_taken"], 3 * e + 3)

                with dve.Fori(0, E // 2) as n:
                    for b in range(2):
                        expert(2 * n + b, b)

            def cross(layer):
                s = L[layer]
                packed(dve, layer)
                need(dve, "pe", f"{layer}.q_ps")
                if layer == "L2x":
                    link(V.tensor_tensor(x2[:, :], O2[:, 0, 0:D], pk(layer, "bq"), ALU.add))
                    done("dve", V.tensor_scalar(x2[:, :], x2[:, :], -DH ** -0.5, None, ALU.mult), f"{layer}.q")
                else:
                    done("dve", V.tensor_scalar(x2[:, :], O2[:, 0, 0:D], -DH ** -0.5, None, ALU.mult), f"{layer}.q")
                V.memset(n_old, BIG)
                V.memset(acc, 0.0)
                link(V.memset(l_sum, 0.0))
                need(dve, "pe", f"{layer}.qT_ps")
                spread(T2[:, 1], f"{layer}.qblk")

                def take_group(c, n):
                    kind, h, g, _ = GROUPS[n]
                    dve.wait_ge(s["t_ready"], NG * c + (n + 1))
                    if kind == "T":
                        if h >= 1:
                            dve.wait_ge(s["pv_done"], 64 * c + (4 * (h - 1) + g + 1))
                        V.tensor_copy(pT[0:TK, g, :], T2[0:TK, n % 2, :]).then_inc(s["t_dve"], 1)
                        return
                    src = T2[:, n % 2, :].rearrange("p (a b g m d) -> p a b m d g", a=2, b=2, g=4, m=2)
                    dst = oc[:, h * 4 * DH:(h + 1) * 4 * DH].rearrange("p (a b d) -> p a b d", a=2, b=2)
                    for b in range(2):
                        last = V.tensor_reduce(dst[:, :, b], src[:, :, b, b], X, ALU.add)
                    last.then_inc(s["t_dve"], 1)

                mine = [n for n, g in enumerate(GROUPS) if g[3] == "dve"]

                def chunk(c):
                    dve.wait_ge(s["mask_in"], 16 * c + 16)
                    if layer == "L2x":
                        ins = V.tensor_scalar(mask_bias[:, :], mask_in.bitcast(I32), 0.0, MASKED, ALU.is_equal, ALU.mult)
                    else:
                        ins = V.tensor_scalar(mask_bias[:, :], mask_in, 1.0e9, None, ALU.mult)
                    ins.then_inc(s["mask_taken"], 1)
                    for b in range(8):
                        dve.wait_ge(s["vp_ready"], 8 * c + (b + 1))
                        V.tensor_copy(vv[:, 2 * b:2 * b + 2, :].rearrange("p t n -> p (t n)"), S4[0:TK, b % 4, :]) \
                            .then_inc(s["vp_taken"], 1)
                    dve.wait_ge(s["mask_taken"], c + 1)
                    todo = list(mine)
                    for h in range(H):
                        for i in range(2):
                            dve.wait_ge(s["s_ready"], 32 * c + (2 * h + i + 1))
                            if h >= 2 and i == 0:
                                dve.wait_ge(s["t_ready"], NG * c + (GROUP_AT["T", h - 2, 3] + 1))
                            V.memset(tick, 0.0)
                            V.tensor_tensor_reduce(
                                sc[:, h % 2, i * HC:(i + 1) * HC], S4f[:, i * 2 * BANK:i * 2 * BANK + HC],
                                mask_bias[:, i * HC:(i + 1) * HC], 1.0, (n_half if i else n_old)[:, h:h + 1],
                                ALU.add, ALU.min, (n_new if i else n_half)[:, h:h + 1]).then_inc(s["s_taken"], 1)
                            dve.wait_ge(s["s_taken"], 32 * c + (2 * h + i + 1))
                        if h == H - 1:
                            V.tensor_tensor(alpha, n_new, n_old, ALU.subtract).then_inc(s["delta"], 1)
                            dve.wait_ge(s["delta"], c + 1)
                            V.tensor_copy(n_old, n_new).then_inc(s["finished"], 1)
                        while h and todo and todo[0] <= GROUP_AT["T", h - 1, 3]:
                            take_group(c, todo.pop(0))
                    for n in todo:
                        take_group(c, n)
                    dve.wait_ge(s["alpha"], c + 1)
                    V.tensor_tensor(acc.rearrange("p (h d) -> p h d", h=H), acc.rearrange("p (h d) -> p h d", h=H),
                                    bcast(alpha, DH), ALU.mult)
                    V.tensor_tensor(l_sum, l_sum, alpha, ALU.mult).then_inc(s["finished"], 1)
                    dve.wait_ge(s["finished"], 3 * c + 2)
                    dve.wait_ge(s["t_dve"], TAKEN["dve"][-1] * c + TAKEN["dve"][-1])
                    V.tensor_tensor(acc, acc, oc, ALU.add)
                    V.tensor_tensor(l_sum, l_sum, l_new, ALU.add).then_inc(s["finished"], 1)
                    dve.wait_ge(s["finished"], 3 * c + 3)

                with dve.Fori(0, NC - 1) as c:
                    chunk(c)
                chunk(NC - 1)
                link(V.reciprocal(l_sum, l_sum))
                ins = V.tensor_tensor(x2[:, :].rearrange("p (h d) -> p h d", h=H),
                                      acc.rearrange("p (h d) -> p h d", h=H), bcast(l_sum, DH), ALU.mult)
                if layer == "L2x":
                    link(ins)
                    ins = V.tensor_tensor(x2[:, :], x2[:, :], pk(layer, "bv"), ALU.add)
                done("dve", ins, f"{layer}.o")
                tail(layer)

            dve.wait_ge(x_in, 16)
            dve.wait_ge(consts_in, 16)
            for layer in layers:
                norm(layer)
                packed(dve, layer)
                x2h = x2[:, :].rearrange("p (h d) -> p h d", h=H)
                if layer == "L0x":
                    s = L[layer]
                    bufs = [ctx_in[:, :, :, :].rearrange("p h k n -> p (h k n)"),
                            sc[:, :, :].rearrange("p a n -> p (a n)"), arena[:, 0:KD * CH]]
                    for c in range(NC):
                        dve.wait_ge(s[f"ctx_in{c % 3}"], 32 * (c // 3 + 1))
                        V.tensor_reduce(parts4[:, c], bufs[c % 3].rearrange("p (h k n) -> p h k n", h=2, k=KD),
                                        X, ALU.add).then_inc(s["summed"], 1)
                    dve.wait_ge(s["summed"], NC)
                    link(V.tensor_reduce(mean, parts4.rearrange("p c h k -> p k (c h)"), X, ALU.add))
                    link(V.tensor_scalar(mean, mean, 1.0 / NK, None, ALU.mult))
                    done("dve", V.tensor_copy(x2T[:, :, :], bcast(mean, P)), f"{layer}.mean")
                    need(dve, "pe", f"{layer}.out")
                    residual(layer, O2[:, 0, 0:D])
                elif layer == "L0a":
                    norm2(layer)
                    need(dve, "pe", f"{layer}.gate_ps")
                    done("dve", V.tensor_tensor(x2[:, :], O2[:, 0, 0:D], pk(layer, "b_gate"), ALU.add), f"{layer}.g")
                    need(dve, "pe", f"{layer}.qkv_ps")
                    qk = work[:, 0:2 * D]
                    link(V.tensor_tensor(qk, S4[:, 0], pk(layer, "b_qkv")[:, 0:2 * D], ALU.add))
                    link(V.memset(vaug, 1.0))
                    V.tensor_tensor(vaug[:, :, 0:DH], S4[:, 1, 0:D].rearrange("p (h d) -> p h d", h=H),
                                    pk(layer, "b_qkv")[:, 2 * D:3 * D].rearrange("p (h d) -> p h d", h=H), ALU.add)
                    need(dve, "act", f"{layer}.sig")
                    link(V.tensor_scalar(rec, row, 1.0 / D, 1e-5, ALU.mult, ALU.add))
                    link(V.reciprocal(rec, rec))
                    link(V.tensor_scalar(x2[:, :], x2[:, :], rec, None, ALU.mult))
                    q3 = qk.rearrange("p (a n) -> p a n", a=2)
                    link(V.tensor_tensor(q3, q3, bcast(x2[:, :], 2, False), ALU.mult))
                    link(V.tensor_scalar(qk, qk, 0.0, None, ALU.max))
                    link(V.tensor_tensor(qk, qk, qk, ALU.mult))
                    done("dve", V.tensor_scalar(qk, qk, 1e-5, None, ALU.add), f"{layer}.qk")
                elif layer == "L2a":
                    need(dve, "pe", f"{layer}.qkv_ps")
                    qk = work[:, 0:2 * D]
                    done("dve", V.tensor_scalar(work[:, 512:1024], S4[:, 0], 0.0, None, ALU.min), f"{layer}.neg")
                    link(V.memset(vaug, 1.0))
                    V.tensor_copy(vaug[:, :, 0:DH], S4[:, 1, 0:D].rearrange("p (h d) -> p h d", h=H))
                    link(V.tensor_scalar(qk, S4[:, 0], 0.0, None, ALU.max))
                    need(dve, "act", f"{layer}.elu")
                    done("dve", V.tensor_tensor(qk, qk, work[:, 512:1024], ALU.add), f"{layer}.qk")
                if layer in ("L0a", "L2a"):
                    need(dve, "pe", f"{layer}.qkT_ps")
                    V.tensor_copy(halfT.rearrange("p k n -> p (k n)"), T2[:, 0, D:2 * D])
                    spread(T2[:, 0], f"{layer}.qblk")
                    need(dve, "pe", f"{layer}.A_ps")
                    done("dve", V.tensor_tensor(mats3, S4f.rearrange("p (h n) -> p h n", h=H),
                                                bcast(C["causal"], H, False), ALU.mult), f"{layer}.AT")
                    need(dve, "pe", f"{layer}.num_ps")
                    link(V.tensor_copy(num, O2[:, 1, 0:H * (DH + 1)].rearrange("p (h n) -> p h n", h=H)))
                    den = head_a[:, 0:H]
                    if layer == "L0a":
                        link(V.tensor_scalar(den, num[:, :, DH], 1e-5, None, ALU.add))
                    else:
                        link(V.tensor_scalar(den, num[:, :, DH], 1e-6, None, ALU.max))
                    link(V.reciprocal(den, den))
                    done("dve", V.tensor_tensor(x2h, num[:, :, 0:DH], bcast(den, DH), ALU.mult), f"{layer}.o")
                    tail(layer)
                elif layer == "L1a":
                    need(dve, "pe", f"{layer}.qkv_ps")
                    qk, q3 = work[:, 0:2 * D], work[:, 0:2 * D].rearrange("p (h d) -> p h d", d=DH)
                    sq, s3 = work[:, 512:1024], work[:, 512:1024].rearrange("p (h d) -> p h d", d=DH)
                    V.tensor_copy(vaug[:, :, 0:DH], S4[:, 1, 0:D].rearrange("p (h d) -> p h d", h=H))
                    link(V.tensor_copy(qk, S4[:, 0]))
                    link(V.tensor_reduce(vsum, q3, X, ALU.add))
                    link(V.tensor_scalar(vsum, vsum, 1.0 / DH, None, ALU.mult))
                    link(V.tensor_tensor(q3, q3, bcast(vsum, DH), ALU.subtract))
                    link(V.tensor_tensor(sq, qk, qk, ALU.mult))
                    link(V.tensor_reduce(vsum, s3, X, ALU.add))
                    done("dve", V.tensor_scalar(head_a, vsum, 1.0 / DH, 1e-5, ALU.mult, ALU.add), f"{layer}.var2")
                    need(dve, "pool", f"{layer}.rstd2")
                    link(V.tensor_tensor(q3, q3, bcast(head_b, DH), ALU.mult))
                    link(V.tensor_tensor(qk, qk, pk(layer, "ln_w"), ALU.mult))
                    link(V.tensor_tensor(qk, qk, pk(layer, "ln_b"), ALU.add))
                    done("dve", V.tensor_scalar(qk[:, 0:D], qk[:, 0:D], DH ** -0.5, None, ALU.mult), f"{layer}.qk")
                    need(dve, "pe", f"{layer}.qkT_ps")
                    V.tensor_copy(halfT.rearrange("p k n -> p (k n)"), T2[:, 0, 0:D])
                    spread(T2[:, 0, D:2 * D], f"{layer}.kblk")
                    need(dve, "pe", f"{layer}.S_ps")
                    link(V.tensor_tensor(mats3, S4f.rearrange("p (h n) -> p h n", h=H),
                                         bcast(C["causal_bias"], H, False), ALU.add))
                    link(V.tensor_reduce(head_a[:, 0:H], mats3, X, ALU.max))
                    done("dve", V.tensor_tensor(mats3, mats3, bcast(head_a[:, 0:H], P), ALU.subtract), f"{layer}.sm")
                    need(dve, "act", f"{layer}.p")
                    link(V.tensor_reduce(head_a[:, 0:H], mats3, X, ALU.add))
                    link(V.reciprocal(head_a[:, 0:H], head_a[:, 0:H]))
                    need(dve, "pe", f"{layer}.pT_ps")
                    done("dve", V.tensor_copy(matsT, S4f), f"{layer}.pT")
                    need(dve, "pe", f"{layer}.num_ps")
                    done("dve", V.tensor_tensor(x2h, O2[:, 1, 0:D].rearrange("p (h d) -> p h d", h=H),
                                                bcast(head_a[:, 0:H], DH), ALU.mult), f"{layer}.o")
                    tail(layer)
                elif layer == "L3a":
                    ld = pk(layer, "log_decay")
                    link(V.tensor_scalar(head_a[:, 0:H], ld, -1.0, None, ALU.mult))
                    done("dve", V.tensor_tensor(head_b[:, 0:H], head_a[:, 0:H], ld, ALU.max), f"{layer}.abs")
                    link(V.tensor_scalar(lam, ld, 0.0, None, ALU.min))
                    need(dve, "act", f"{layer}.e")
                    done("dve", V.tensor_scalar(head_a[:, 0:H], head_a[:, 0:H], 1.0, None, ALU.add), f"{layer}.onep")
                    need(dve, "act", f"{layer}.ln1p")
                    done("dve", V.tensor_tensor(lam, lam, head_b[:, 0:H], ALU.subtract), f"{layer}.ln")
                    link(V.tensor_tensor(work[:, 0:D], pk(layer, "q"), pk(layer, "k"), ALU.mult))
                    link(V.tensor_reduce(vsum[:, 0:H], work[:, 0:D].rearrange("p (h d) -> p h d", h=H), X, ALU.add))
                    V.tensor_tensor(vaug[:, :, 0:DH], xn[:, :].rearrange("p (h d) -> p h d", h=H),
                                    bcast(vsum[:, 0:H], DH), ALU.mult)
                    need(dve, "act", f"{layer}.decay")
                    done("dve", V.tensor_tensor(mats3, mats3, bcast(C["causal"], H, False), ALU.mult), f"{layer}.V")
                    need(dve, "pe", f"{layer}.num_ps")
                    link(V.tensor_copy(x2[:, :], O2[:, 1, 0:D]))
                    link(V.tensor_tensor(work[:, 0:D], x2[:, :], x2[:, :], ALU.mult))
                    link(V.tensor_reduce(rec, work[:, 0:D], X, ALU.add))
                    done("dve", V.tensor_scalar(mv[:, 1:2], rec, 1.0 / D, 1e-6, ALU.mult, ALU.add), f"{layer}.var2")
                    need(dve, "pool", f"{layer}.rstd2")
                    link(V.tensor_scalar(x2[:, :], x2[:, :], rstd, None, ALU.mult))
                    done("dve", V.tensor_tensor(x2[:, :], x2[:, :], pk(layer, "norm"), ALU.mult), f"{layer}.o")
                    tail(layer)
                elif layer == "L1f":
                    norm2(layer)
                    dve.wait_ge(L[layer]["q_in"], 64)
                    for b in range(2):
                        link(V.tensor_scalar(fb[:, b, 0:2048], fb[:, b, 0:2048].bitcast(I32), 128.0, None, ALU.subtract))
                    link(V.tensor_tensor(fb[:, 0, 0:2048], fb[:, 0, 0:2048], fb[:, 0, 2048:4096], ALU.mult))
                    done("dve", V.tensor_tensor(fb[:, 1, 0:2048], fb[:, 1, 0:2048], fb[:, 1, 2048:4096], ALU.mult),
                         f"{layer}.w")
                    need(dve, "pe", f"{layer}.z_ps")
                    done("dve", V.tensor_tensor(hid, S4f[:, 0:1024], pk(layer, "b1"), ALU.add), f"{layer}.z")
                    need(dve, "pe", f"{layer}.yT_ps")
                    done("dve", V.tensor_copy(hidT.rearrange("p t n -> p (t n)"), S4f[:, 1024:2048]), f"{layer}.yT")
                    link(V.tensor_tensor(x[:, :], x[:, :], xn[:, :], ALU.add))
                    need(dve, "pe", f"{layer}.out")
                    link(V.tensor_tensor(x2[:, :], O2[:, 0, 0:D], pk(layer, "b2"), ALU.add))
                    done("dve", V.scalar_tensor_tensor(x[:, :], x2[:, :], 0.5, x[:, :], ALU.mult, ALU.add),
                         f"{layer}.end")
                    need(dve, "dve", f"{layer}.end")
                elif layer in ("L2x", "L3x"):
                    cross(layer)
                elif layer in FF:
                    V.memset(yacc, 0.0)
                    if layer == "L0f":
                        need(dve, "pe", f"{layer}.logit")
                        link(V.tensor_copy(prob, O2[:, 0, 0:E]))
                        ranks(prob)
                        link(V.tensor_scalar(rank, rank, 2.0, None, ALU.is_lt))
                        done("dve", V.tensor_tensor(wts, rank, prob, ALU.mult), f"{layer}.weights")
                    elif layer == "L2f":
                        softmax_gate(layer, pk(layer, "bias"))
                        ranks(prob)
                        link(V.tensor_scalar(rank, rank, 2.0, None, ALU.is_lt))
                        link(V.tensor_tensor(wts, rank, prob, ALU.mult))
                        link(V.tensor_reduce(row, wts, X, ALU.add))
                        link(V.tensor_scalar(row, row, 1e-6, None, ALU.add))
                        link(V.reciprocal(row, row))
                        done("dve", V.tensor_scalar(wts, wts, row, None, ALU.mult), f"{layer}.weights")
                    else:
                        softmax_gate(layer, None)
                        ranks(prob)
                        link(V.tensor_scalar(one0, rank, 0.0, None, ALU.is_equal))
                        link(V.tensor_scalar(one1, rank, 1.0, None, ALU.is_equal))
                        done("dve", V.tensor_tensor(wts, one0, one1, ALU.add), f"{layer}.onehot")
                        need(dve, "dve", f"{layer}.onehot")
                        link(V.tensor_tensor(wts, wts, prob, ALU.mult))
                        link(V.tensor_reduce(row, wts, X, ALU.add))
                        link(V.reciprocal(row, row))
                        link(V.tensor_scalar(prob, prob, row, None, ALU.mult))
                        need(dve, "pe", f"{layer}.pos")
                        link(V.tensor_scalar(half[:, 0:2 * E], O2[:, 1, 0:2 * E], float(CAPACITY), None, ALU.is_le))
                        link(V.tensor_tensor(one0, one0, half[:, 0:E], ALU.mult))
                        link(V.tensor_tensor(one1, one1, half[:, E:2 * E], ALU.mult))
                        link(V.tensor_tensor(wts, one0, one1, ALU.add))
                        done("dve", V.tensor_tensor(wts, wts, prob, ALU.mult), f"{layer}.weights")
                    need(dve, "dve", f"{layer}.weights")
                    experts(layer)
                    if layer == "L2f":
                        variance(yacc, layer, "var3")
                        link(V.tensor_tensor(x[:, :], x[:, :], xn[:, :], ALU.add))
                        need(dve, "pool", f"{layer}.rstd3")
                        link(scaled(yacc, yacc))
                    residual(layer, yacc)
                elif layer == "L1x":
                    s = L[layer]
                    w = pk(layer, "w_sim")
                    link(V.tensor_tensor(x2[:, :], xn[:, :], w[:, 0:D], ALU.mult))
                    link(V.tensor_reduce(row, x2[:, :], X, ALU.add))
                    link(V.tensor_tensor(row, row, pk(layer, "b_sim"), ALU.add))
                    link(V.tensor_tensor(x2[:, :], xn[:, :], w[:, 2 * D:3 * D], ALU.mult))
                    done("dve", V.tensor_tensor(x2[:, :], x2[:, :], w[:, D:2 * D], ALU.add), f"{layer}.A")
                    need(dve, "pe", f"{layer}.AT_ps")
                    done("dve", V.tensor_copy(x2T[:, :, :].rearrange("p k n -> p (k n)"), T2[:, 1, 0:D]), f"{layer}.AT")
                    with dve.Fori(0, NC) as c:
                        for i in range(2):
                            dve.wait_ge(s["s_ready"], 2 * c + (i + 1))
                            V.tensor_scalar(arena[:, bass.ds(c * CH + i * HC, HC)],
                                            S4f[:, i * 2 * BANK:i * 2 * BANK + HC], row, None, ALU.add, ALU.max,
                                            accum_out=maxes[:, bass.ds(2 * c + i, 1)]).then_inc(s["s_taken"], 1)
                    dve.wait_ge(s["s_taken"], 2 * NC)
                    link(V.memset(acc, 0.0))
                    link(V.tensor_reduce(row_max, maxes, X, ALU.max))
                    done("dve", V.tensor_scalar(rec, row_max, -1.0, None, ALU.mult), f"{layer}.max")
                    need(dve, "pool", f"{layer}.gmax")
                    link(V.tensor_scalar(gmax, gmax, -1.0, None, ALU.mult))

                    def attend(c, first):
                        for i in range(2):
                            dve.wait_ge(s["t_ready"], 4 * c + (2 * i + 1))
                            if not first:
                                dve.wait_ge(s["pv_ready"], 2 * c + i - 1)
                            V.tensor_copy(pT[0:TK, 2 * i, :], T2[0:TK, 0, :]).then_inc(s["t_dve"], 1)
                            dve.wait_ge(s["pv_ready"], 2 * c + i + 1)
                            V.tensor_tensor(acc, O2[:, i, 0:D], acc, ALU.add).then_inc(s["pv_taken"], 1)
                            dve.wait_ge(s["pv_taken"], 2 * c + i + 1)

                    attend(0, True)
                    with dve.Fori(1, NC) as c:
                        attend(c, False)
                    dve.wait_ge(s["p_ready"], 2 * NC)
                    need(dve, "act", f"{layer}.bat")
                    V.tensor_copy(work[:, 512:512 + D], xn[:, :])
                    V.memset(work[:, 512 + D:512 + D + 1], 1.0)
                    done("dve", V.tensor_copy(mats3[:, 0, :], bat.to_broadcast([P, P])), f"{layer}.bat")
                    f = [arena[:, k * D:(k + 1) * D] for k in range(3)]
                    link(V.tensor_reduce(rec, sums, X, ALU.add))
                    link(V.reciprocal(rec, rec))
                    link(V.tensor_scalar(f[0], acc, rec, None, ALU.mult))
                    link(V.tensor_tensor(f[1], xn[:, :], f[0], ALU.mult))
                    need(dve, "pe", f"{layer}.hc_ps")
                    link(V.reciprocal(rec, O2[:, 0, D:D + 1]))
                    link(V.tensor_scalar(f[2], O2[:, 0, 0:D], rec, None, ALU.mult))
                    done("dve", V.tensor_tensor(f[2], f[2], xn[:, :], ALU.mult), f"{layer}.f")
                    need(dve, "pe", f"{layer}.fT_ps")
                    done("dve", V.tensor_copy(arena[:, 1024:1024 + 768], S4f[:, 0:768]), f"{layer}.fT")
                    need(dve, "pe", f"{layer}.out")
                    residual(layer, O2[:, 1, 0:D])


def blocks(w):
    k = w.shape[0] // P
    return w.reshape(k, P, w.shape[1]).transpose(1, 0, 2).reshape(P, k * w.shape[1])


def rows(*vs):
    return [np.broadcast_to(np.reshape(v, (1, -1)), (P, np.size(v))) for v in vs]


def pack(*parts):
    return np.ascontiguousarray(np.concatenate(parts, axis=1))


def constants():
    i = np.arange(P)
    e = np.arange(E)
    parts = [np.eye(P), i[:, None] <= i[None, :], np.where(i[None, :] <= i[:, None], 0.0, -MASKED),
             np.maximum(i[None, :] - i[:, None], 0), (i[:, None] // DH) == np.arange(HH)[None, :],
             np.broadcast_to((e[None, :] < e[:, None]).reshape(1, -1), (P, E * E))]
    return np.ascontiguousarray(np.concatenate([np.asarray(p, np.float32) for p in parts], axis=1))


def layout(i):
    c = i["ctx_1024"][0]
    L0W = i["L0_xattn_W"]
    out = {
        "x": i["x"][0],
        "consts": constants(),
        "ctx_cols": c.reshape(2 * NC, HC, KD, P).transpose(0, 3, 2, 1),
        "ctx_rows": c.reshape(2 * NC, TH, TK, D).transpose(0, 2, 1, 3).reshape(2 * NC, TK, TH * D),
        "mask_L2x": i["mask_SxS2_ik0"].reshape(P, NC, CH).transpose(1, 0, 2),
        "mask_L3x": i["mask_BxSxS2_ff0"][0].reshape(P, NC, CH).transpose(1, 0, 2),
        "fc1_q": blocks(i["L1_ffn_fc1_q"]),
        "fc2_q": blocks(i["L1_ffn_fc2_q"]),
        "fc1_scales": pack(*rows(i["L1_ffn_fc1_scales"])),
        "fc2_scales": pack(*rows(i["L1_ffn_fc2_scales"])),
        "pack_L0x": pack(blocks(L0W[:, :D].T), blocks(L0W[:, D:].T), *rows(i["L0_xattn_b"])),
        "pack_L0a": pack(blocks(i["L0_attn_W_qkv"]), blocks(i["L0_attn_W_gate"]), blocks(i["L0_attn_W_proj"]),
                         *rows(i["L0_attn_ln_g"], i["L0_attn_ln_b"], i["L0_attn_b_qkv"], i["L0_attn_b_gate"],
                               i["L0_attn_b_proj"])),
        "pack_L0f": pack(blocks(i["L0_ffn_Wg"].T)),
        "pack_L1x": pack(blocks(i["L1_xattn_W_qv"]),
                         *rows(i["L1_xattn_w_sim"], i["L1_xattn_b_sim"], i["L1_xattn_b_qv"])),
        "pack_L1a": pack(blocks(np.concatenate([i["L1_attn_Wq"].T, i["L1_attn_Wk"].T, i["L1_attn_Wv"].T], axis=1)),
                         blocks(i["L1_attn_Wu"].T),
                         *rows(np.tile(i["L1_attn_qln_w"], H), np.tile(i["L1_attn_kln_w"], H),
                               np.tile(i["L1_attn_qln_b"], H), np.tile(i["L1_attn_kln_b"], H))),
        "pack_L1f": pack(*rows(i["L1_ffn_ln_gamma"], i["L1_ffn_ln_beta"], i["L1_ffn_fc1_bias"], i["L1_ffn_fc2_bias"])),
        "pack_L2x": pack(*[blocks(i[f"L2_xattn_W{n}"].T) for n in "qkvo"], *rows(i["L2_xattn_bq"]),
                         i["L2_xattn_bk"].reshape(KD, P).T, *rows(i["L2_xattn_bv"], i["L2_xattn_bo"])),
        "pack_L2a": pack(blocks(np.concatenate([i[f"L2_attn_W{n}"].T for n in "qkv"], axis=1)),
                         blocks(i["L2_attn_Wo"].T)),
        "pack_L2f": pack(blocks(i["L2_ffn_gate_w"].T), *rows(i["L2_ffn_expert_bias"])),
        "pack_L3x": pack(*[blocks(i[f"L3_xattn_W{n}"]) for n in "qkvo"]),
        "pack_L3a": pack(blocks(i["L3_attn_o_w"].T), *rows(i["L3_attn_q"], i["L3_attn_k"], i["L3_attn_log_decay"],
                                                          i["L3_attn_norm_weight"])),
        "pack_L3f": pack(blocks(i["L3_ffn_gate_w"].T)),
    }
    ups = {"L0f": ["L0_ffn_W1", "L0_ffn_W2"], "L2f": ["L2_ffn_w_up"], "L3f": ["L3_ffn_wi_gate", "L3_ffn_wi_up"]}
    downs = {"L0f": "L0_ffn_W3", "L2f": "L2_ffn_w_down", "L3f": "L3_ffn_wo"}
    for layer, names in ups.items():
        F = FF[layer]
        out[f"up_{layer}"] = np.concatenate(
            [i[n].reshape(E, F, KD, P).transpose(0, 3, 2, 1).reshape(E, P, KD * F) for n in names], axis=2)
        out[f"down_{layer}"] = i[downs[layer]].reshape(E, D, E, F // E).transpose(0, 3, 2, 1).reshape(E, F // E, E * D)
    return {k: np.ascontiguousarray(v) for k, v in out.items()}


def kernel(**inputs):
    import concourse.bacc as bacc
    from concourse.bass_utils import run_bass_kernel_spmd

    arrays = layout({k: np.asarray(v) for k, v in inputs.items()})
    nc = bacc.Bacc("TRN2", target_bir_lowering=False, num_devices=1)
    args = {k: nc.dram_tensor(f"in_{k}", v.shape, mybir.dt.from_np(v.dtype), kind="ExternalInput").ap()
            for k, v in arrays.items()}
    args["out"] = nc.dram_tensor("out_x", (P, D), F32, kind="ExternalOutput").ap()
    build(nc, args)
    r = run_bass_kernel_spmd(nc, [{f"in_{k}": v for k, v in arrays.items()}], core_ids=[0])
    return r.results[0]["out_x"].reshape(1, P, D)
```

```python
from contextlib import ExitStack

import numpy as np

import concourse.bass as bass
import concourse.mybir as mybir

F32 = mybir.dt.float32
F32R = mybir.dt.float32r
I32 = mybir.dt.int32
ALU = mybir.AluOpType
ACT = mybir.ActivationFunctionType
X = mybir.AxisListType.X

P = 128
D = 256
KD = D // P
H = 16
DH = D // H
HH = H // KD
QR = 32
NP = H // 2
NK = 12544
TK = 112
HC = 896
CH = 2 * HC
NC = NK // CH
TC = CH // TK
TH = HC // TK
BANK = 512
E = 8
BIG = 3.0e38
MASKED = 1.0e30
CAPACITY = int(P / E * 1.25)

LAYERS = ["L0x", "L0a", "L0f", "L1x", "L1a", "L1f", "L2x", "L2a", "L2f", "L3x", "L3a", "L3f"]
FF = {"L0f": 704, "L2f": 1024, "L3f": 1024}
GATED = ("L0f", "L3f")

PACKS = {
    "L0x": dict(w1=512, w2=512, b=256),
    "L0a": dict(qkv=1536, gate=512, proj=512, ln_g=256, ln_b=256, b_qkv=768, b_gate=256, b_out=256),
    "L0f": dict(gate=16),
    "L1x": dict(w_qv=2048, w_sim=768, b_sim=1, b_out=256),
    "L1a": dict(qkv=1536, proj=512, ln_w=512, ln_b=512),
    "L1f": dict(ln_g=256, ln_b=256, b1=1024, b2=256),
    "L2x": dict(wq=512, wk=512, wv=512, proj=512, bq=256, bk=2, bv=256, b_out=256),
    "L2a": dict(qkv=1536, proj=512),
    "L2f": dict(gate=16, bias=8),
    "L3x": dict(wq=512, wk=512, wv=512, proj=512),
    "L3a": dict(proj=512, q=256, k=256, log_decay=16, norm=256),
    "L3f": dict(gate=16),
}
CONSTS = dict(ident=128, causal=128, causal_bias=128, steps=128, head=8, pair=2, before=64)

NORM = {"dve": ["var", "xn", "xT"], "pool": ["rstd"], "pe": ["xnT"], "act": []}
NORM2 = {"dve": ["var2", "x2", "x2T"], "pool": ["rstd2"], "pe": ["x2T_ps"], "act": []}
TAIL = {"dve": ["o", "oT"], "pool": [], "pe": ["oT_ps", "out"], "act": []}


def stage_lists(layers):
    lists = {e: [] for e in ("pe", "dve", "act", "pool")}

    def add(layer, **stages):
        for e, names in stages.items():
            lists[e] += [f"{layer}.{n}" for n in names]

    for layer in layers:
        add(layer, **NORM)
        if layer == "L0x":
            add(layer, dve=["mean"], pe=["out"])
        elif layer == "L0a":
            add(layer, **NORM2)
            add(layer, pe=["gate_ps", "qkv_ps", "qkT_ps", "A_ps", "num_ps"],
                dve=["g", "qk", "qblk", "AT"], act=["sig"])
            add(layer, **TAIL)
        elif layer == "L2a":
            add(layer, pe=["qkv_ps", "qkT_ps", "A_ps", "num_ps"], dve=["neg", "qk", "qblk", "AT"], act=["elu"])
            add(layer, **TAIL)
        elif layer == "L1a":
            add(layer, pe=["qkv_ps", "qkT_ps", "S_ps", "pT_ps", "num_ps"],
                dve=["var2", "qk", "kblk", "sm", "pT"], act=["p"], pool=["rstd2"])
            add(layer, **TAIL)
        elif layer == "L3a":
            add(layer, pe=["num_ps"], dve=["abs", "onep", "ln", "V", "var2"], act=["e", "ln1p", "decay"],
                pool=["rstd2"])
            add(layer, **TAIL)
        elif layer == "L1x":
            add(layer, dve=["A", "AT", "max", "bat", "f", "fT"], pe=["AT_ps", "hc_ps", "fT_ps", "out"],
                pool=["gmax"], act=["bat"])
        elif layer == "L1f":
            add(layer, **NORM2)
            add(layer, pe=["z_ps", "yT_ps", "out"], dve=["w", "z", "yT"], act=["y"])
        elif layer in ("L2x", "L3x"):
            add(layer, pe=["q_ps", "qT_ps"], dve=["q", "q4"])
            add(layer, **TAIL)
        elif layer == "L0f":
            add(layer, pe=["logit"], dve=["weights"])
        elif layer == "L2f":
            add(layer, pe=["logit"], dve=["logit", "weights", "var3"], act=["prob"], pool=["rstd3"])
        elif layer == "L3f":
            add(layer, pe=["logit", "pos"], dve=["logit", "onehot", "weights"], act=["prob"])
        add(layer, dve=["end"])
    return lists


def unit_groups():
    seq = []
    for h in range(H):
        if h % 4 == 1 and h > 1:
            seq.append(("O", (h - 5) // 4, 0, "dve"))
        seq += [("T", h, g, "act" if g % 2 == 0 else "dve") for g in range(4)]
    seq.append(("O", 3, 0, "dve"))
    return seq


GROUPS = unit_groups()
GROUP_AT = {g[:3]: n for n, g in enumerate(GROUPS)}
TAKEN = {e: [sum(g[3] == e for g in GROUPS[:n + 1]) for n in range(len(GROUPS))] for e in ("act", "dve")}
NG = len(GROUPS)
KEYS_AT = (3, 9)
LATE = (0,) + KEYS_AT


def build(nc, a, layers=LAYERS):
    ctx = ExitStack()
    with ctx:
        def sb(name, shape, dt=F32):
            return ctx.enter_context(nc.sbuf_tensor(name, shape, dt))

        def sem(name):
            return ctx.enter_context(nc.semaphore(name))

        S4 = ctx.enter_context(nc.psum_tensor("S4", [P, 4, BANK], F32))
        T2 = ctx.enter_context(nc.psum_tensor("T2", [P, 2, BANK], F32))
        O2 = ctx.enter_context(nc.psum_tensor("O2", [P, 2, BANK], F32))
        S4f = S4[:, :, :].rearrange("p b n -> p (b n)")

        x = sb("x", [P, D])
        xn = sb("xn", [P, D])
        x2 = sb("x2", [P, D])
        xT = sb("xT", [P, KD, P])
        x2T = sb("x2T", [P, KD, P])
        consts = sb("consts", [P, sum(CONSTS.values())])
        slots = [max(sum(PACKS[n].values()) for n in LAYERS[i::2]) for i in range(2)]
        packs = [sb(f"packs{i}", [P, slots[i]]) for i in range(2)]
        arena_at = nc.sbuf_base
        arena = sb("arena", [P, NK])
        ctx_in = sb("ctx_in", [P, 2, KD, HC])
        sc = sb("sc", [P, 3, CH])
        pT = sb("pT", [P, 4, BANK])
        o_sb = sb("o_sb", [P, 2, BANK])
        mask_bias = sb("mask_bias", [P, CH])
        wide_at = nc.sbuf_base
        wide = sb("wide", [P, NP * CH])
        fb = wide[:, 0:2 * 3 * KD * 1024].rearrange("p (b n) -> p b n", b=2)
        work = sb("work", [P, 1536])
        small = sb("small", [P, 512])

        vv = arena[0:TK, KD * CH:KD * CH + TC * D].rearrange("p (t d) -> p t d", t=TC)
        at = KD * CH + TC * D
        blk = arena[:, at:at + H * P].rearrange("p (h n) -> p h n", h=H)
        mask_in = arena[:, at + H * P:at + H * P + CH]
        keys_hl = nc.alloc_sbuf_tensor_at("keys_hl", [P, 2, CH], F32R, offset=arena_at)
        keys4 = nc.alloc_sbuf_tensor_at("keys4", [P, NP, CH], F32R, offset=wide_at)
        q4 = nc.alloc_sbuf_tensor_at("q4", [P, H, P], F32R, offset=arena_at + 4 * at)
        q_up = nc.alloc_sbuf_tensor_at("q_up", [P, NP * P], F32R, offset=arena_at + 4 * (at + H * P + CH))
        q_low = arena[:, at + H * P + CH:at + H * P + CH + NP * P]
        assert at + H * P + CH + NP * P <= NK
        mats = sc[:, :, :].rearrange("p a n -> p (a n)")[:, 0:H * P]
        mats3 = mats.rearrange("p (h n) -> p h n", h=H)
        matsT = arena[:, 0:H * P]
        matsT3 = matsT.rearrange("p (h n) -> p h n", h=H)
        oT = arena[:, 2048:2048 + D].rearrange("p (k n) -> p k n", k=KD)
        halfT = arena[:, 2304:2304 + D].rearrange("p (k n) -> p k n", k=KD)
        vaug = arena[:, 2560:2560 + H * (DH + 1)].rearrange("p (h n) -> p h n", h=H)
        num = arena[:, 2832:2832 + H * (DH + 1)].rearrange("p (h n) -> p h n", h=H)
        hid = arena[:, 0:1024]
        hidT = arena[:, 1024:2048].rearrange("p (t n) -> p t n", t=E)
        gated = arena[:, 3200:4224]
        yacc = arena[:, 4224:4480]

        at = 0
        C = {}
        for name, w in CONSTS.items():
            C[name] = consts[:, at:at + w]
            at += w
        ident = C["ident"]

        def pk(layer, name, k=None):
            at = 0
            for n, w in PACKS[layer].items():
                if n == name:
                    break
                at += w
            piece = packs[LAYERS.index(layer) % 2][:, at:at + w]
            return piece.rearrange("p (k n) -> p k n", k=k) if k else piece

        cols = [0]

        def take(w):
            cols[0] += w
            assert cols[0] <= 512
            return small[:, cols[0] - w:cols[0]]

        stats, mv, rstd, half = take(6), take(2), take(1), take(64)
        vsum, head_a, head_b, lam = take(32), take(32), take(32), take(16)
        n_old, n_half, n_new, l_new = take(16), take(16), take(16), take(16)
        alpha, l_sum, wts, wcur = take(16), take(16), take(8), take(2)
        maxes, sums, row, row_max = take(14), take(14), take(1), take(1)
        gmax, bat, rec, prob = take(1), take(1), take(1), take(8)
        rank, one0, one1 = take(8), take(8), take(8)
        eye_a, mean, tick = take(64), take(2), take(1)
        parts4 = sb("parts", [P, NC, 2, KD])
        oc = work[:, 0:256]
        acc = work[:, 256:512]

        minus_half = sb("minus_half", [P, 2 * H])
        filled = sem("minus_half_filled")

        STAGES = stage_lists(layers)
        stages = {e: sem(f"{e}_stages") for e in STAGES}
        counted = {e: 0 for e in STAGES}

        def done(e, ins, name):
            assert STAGES[e][counted[e]] == name, (e, name, STAGES[e][counted[e]])
            counted[e] += 1
            ins.then_inc(stages[e], 1)

        def need(eng, e, name):
            eng.wait_ge(stages[e], STAGES[e].index(name) + 1)

        consts_in = sem("consts_in")
        x_in = sem("x_in")
        pack_in = [sem(f"pack{n}_in") for n in range(2)]
        stored = sem("stored")
        own = {e: sem(f"{e}_own") for e in ("dve", "act")}
        owned = {"dve": 0, "act": 0}

        def packed(eng, layer):
            eng.wait_ge(pack_in[LAYERS.index(layer) % 2], 16 * (layers.index(layer) // 2 + 1))

        L = {}

        def sems(layer, *names):
            L[layer] = {n: sem(f"{layer}_{n}") for n in names}

        for layer in layers:
            if layer == "L0x":
                sems(layer, "ctx_in0", "ctx_in1", "ctx_in2", "summed")
            elif layer == "L1x":
                sems(layer, "ctx_in0", "ctx_in1", "s_ready", "s_taken", "p_ready", "nat_in0", "nat_in1", "t_ready", "t_dve", "t_act",
                     "pv_ready", "pv_taken")
            elif layer in ("L2x", "L3x"):
                sems(layer, "ctx_in0", "ctx_in1", "mask_in", "mask_taken", "kp_ready", "up_taken", "low_taken",
                     "acc_taken", "half_read", "keys_in0", "keys_in1", "vp_ready", "vp_taken",
                     "s_ready", "s_taken", "p_ready", "t_ready", "t_dve", "t_act", "pv_done", "o_taken",
                     "delta", "alpha", "finished")
            elif layer == "L1f":
                sems(layer, "q_in")
            elif layer in FF:
                sems(layer, "w_in0", "w_in1", "g_ready", "act_done", "h_ready", "t_ready", "t_dve", "t_act", "y_ready",
                     "y_taken")

        block = ctx.enter_context(nc.Block())

        @block.sync
        def _(sp):
            def load_pack(layer):
                n = layers.index(layer)
                if n >= 2:
                    need(sp, "dve", f"{layers[n - 2]}.end")
                w = sum(PACKS[layer].values())
                slot = LAYERS.index(layer) % 2
                sp.dma_start(packs[slot][:, 0:w], a[f"pack_{layer}"]).then_inc(pack_in[slot], 16)

            sp.dma_start(x[:, :], a["x"]).then_inc(x_in, 16)
            sp.dma_start(consts[:, :], a["consts"]).then_inc(consts_in, 16)
            for layer in layers[:2]:
                load_pack(layer)

            def load_ctx(s, n, half):
                sp.dma_start(ctx_in[:, half], a["ctx_cols"][bass.ds(n, 1)].rearrange(
                    "a p k n -> p (a k) n")).then_inc(s, 16)

            def load_expert(layer, e, b):
                F = FF[layer]
                m = KD * (2 if layer in GATED else 1) * F
                s = L[layer][f"w_in{b}"]
                sp.dma_start(fb[:, b, 0:m], a[f"up_{layer}"][bass.ds(e, 1)].rearrange(
                    "a p n -> p (a n)")).then_inc(s, 16)
                sp.dma_start(fb[0:F // E, b, m:m + E * D], a[f"down_{layer}"][bass.ds(e, 1)].rearrange(
                    "a p n -> p (a n)")).then_inc(s, 16)

            for i, layer in enumerate(layers):
                prev = layers[i - 1] if i else None
                if layer == "L0x":
                    s = L[layer]
                    bufs = [ctx_in[:, :, :, :].rearrange("p h k n -> p (h k n)"),
                            sc[:, 0:2, :].rearrange("p a n -> p (a n)"), arena[:, 0:KD * CH]]
                    for c in range(NC):
                        if c >= 3:
                            sp.wait_ge(s["summed"], c - 2)
                        for half in range(2):
                            dst = bufs[c % 3].rearrange("p (h n) -> p h n", h=2)[:, half]
                            sp.dma_start(dst, a["ctx_cols"][2 * c + half].rearrange("p k n -> p (k n)")) \
                                .then_inc(s[f"ctx_in{c % 3}"], 16)
                elif layer == "L1x":
                    s = L[layer]
                    if prev:
                        need(sp, "dve", f"{prev}.end")
                    for half in range(2):
                        load_ctx(s[f"ctx_in{half}"], half, half)
                    with sp.Fori(1, NC) as c:
                        for half in range(2):
                            sp.wait_ge(s["s_ready"], 2 * c - 1 + half)
                            load_ctx(s[f"ctx_in{half}"], 2 * c + half, half)
                    def load_nat(n, half):
                        sp.dma_start(fb[0:TK, half, 0:TH * D], a["ctx_rows"][bass.ds(n, 1)].rearrange(
                            "a p n -> p (a n)")).then_inc(s[f"nat_in{half}"], 16)
                    for half in range(2):
                        load_nat(half, half)
                    with sp.Fori(1, NC) as c:
                        for half in range(2):
                            sp.wait_ge(s["pv_ready"], 2 * c - 1 + half)
                            load_nat(2 * c + half, half)
                elif layer in ("L2x", "L3x"):
                    s = L[layer]
                    if prev:
                        need(sp, "dve", f"{prev}.end")

                    def load_mask(c):
                        dst = mask_in.bitcast(I32) if layer == "L2x" else mask_in
                        sp.dma_start(dst, a[f"mask_{layer}"][bass.ds(c, 1)].rearrange("a p n -> p (a n)")) \
                            .then_inc(s["mask_in"], 16)

                    for half in range(2):
                        load_ctx(s[f"ctx_in{half}"], half, half)
                    load_mask(0)
                    if i + 1 < len(layers):
                        load_pack(layers[i + 1])

                    def load_keys(c, hf, before=None):
                        sp.wait_ge(s["low_taken"], 8 * c + 4 * (hf + 1))
                        if before is not None:
                            sp.wait_ge(s["delta" if hf else "half_read"], before)
                        for j in range(HH // 2):
                            for r in range(4):
                                sp.dma_start(keys4[QR * r:QR * (r + 1), hf * HH // 2 + j, :].bitcast(F32),
                                             keys_hl[QR * j:QR * (j + 1), r % 2, :].bitcast(F32)) \
                                    .then_inc(s[f"keys_in{hf}"], 16)

                    for hf in range(KD):
                        load_keys(0, hf)
                    with sp.Fori(1, NC) as c:
                        sp.wait_ge(s["mask_taken"], c)
                        load_mask(c)
                        sp.wait_ge(s["vp_ready"], 8 * c)
                        for half in range(2):
                            load_ctx(s[f"ctx_in{half}"], 2 * c + half, half)
                        for hf in range(KD):
                            load_keys(c, hf, c)
                elif layer == "L1f":
                    s = L[layer]
                    if prev:
                        need(sp, "dve", f"{prev}.end")
                    for b in range(2):
                        sp.dma_start(fb[:, b, 0:2048].bitcast(I32), a[f"fc{b + 1}_q"]).then_inc(s["q_in"], 16)
                        sp.dma_start(fb[:, b, 2048:4096], a[f"fc{b + 1}_scales"]).then_inc(s["q_in"], 16)
                elif layer in FF:
                    s = L[layer]
                    if i == 0:
                        for e in range(2):
                            load_expert(layer, e, e)
                    with sp.Fori(1, E // 2) as n:
                        for b in range(2):
                            sp.wait_ge(s["y_ready"], 2 * n + (b - 1))
                            load_expert(layer, 2 * n + b, b)
                if i + 1 < len(layers) and layers[i + 1] in FF:
                    if prev:
                        need(sp, "dve", f"{prev}.end")
                    for e in range(2):
                        load_expert(layers[i + 1], e, e)
                if i + 2 < len(layers) and layers[i + 1] not in ("L2x", "L3x"):
                    load_pack(layers[i + 2])

            need(sp, "dve", f"{layers[-1]}.end")
            sp.dma_start(a["out"], x[:, :]).then_inc(stored, 16)
            sp.wait_ge(stored, 16)

        @block.gpsimd
        def _(pool):
            def power(layer, stage, of, t, out):
                need(pool, "dve", f"{layer}.{of}")
                done("pool", nc.gpsimd.tensor_tensor(out, t, minus_half[:, 0:t.shape[1]], ALU.pow), f"{layer}.{stage}")

            nc.gpsimd.memset(minus_half[:, :], -0.5).then_inc(filled, 1)
            pool.wait_ge(filled, 1)
            for layer in layers:
                power(layer, "rstd", "var", mv[:, 1:2], rstd)
                if layer in ("L0a", "L1f"):
                    power(layer, "rstd2", "var2", mv[:, 1:2], rstd)
                elif layer == "L1a":
                    power(layer, "rstd2", "var2", head_a, head_b)
                elif layer == "L3a":
                    power(layer, "rstd2", "var2", mv[:, 1:2], rstd)
                elif layer == "L2f":
                    power(layer, "rstd3", "var3", mv[:, 1:2], rstd)
                elif layer == "L1x":
                    need(pool, "dve", f"{layer}.max")
                    done("pool", nc.gpsimd.partition_all_reduce(gmax, row_max, P, bass.bass_isa.ReduceOp.max),
                         f"{layer}.gmax")

        @block.tensor
        def _(pe):
            mm = nc.tensor.matmul

            def transposes(out, src, n, w=P):
                for t in range(n):
                    last = nc.tensor.transpose(out[0:w, t * P:(t + 1) * P], src[:, t * w:(t + 1) * w], ident)
                return last

            def product(out, lhsT, rhs, n=KD):
                for k in range(n):
                    last = mm(out, lhsT[:, k, :], rhs[:, k, :], start=(k == 0), stop=(k == n - 1))
                return last

            def norm(layer):
                need(pe, "dve", f"{layer}.xn")
                done("pe", transposes(T2[:, 0], xn, KD), f"{layer}.xnT")

            def norm2(layer):
                need(pe, "dve", f"{layer}.x2")
                done("pe", transposes(T2[:, 1], x2, KD), f"{layer}.x2T_ps")

            def tail(layer):
                need(pe, "dve", f"{layer}.o")
                done("pe", transposes(T2[:, 1], x2, KD), f"{layer}.oT_ps")
                need(pe, "dve", f"{layer}.oT")
                done("pe", product(O2[:, 0, 0:D], oT, pk(layer, "proj", KD)), f"{layer}.out")

            def qkv(layer, src):
                w = pk(layer, "qkv", KD)
                product(S4[:, 0], src, w[:, :, 0:2 * D])
                done("pe", product(S4[:, 1, 0:D], src, w[:, :, 2 * D:3 * D]), f"{layer}.qkv_ps")
                need(pe, "dve", f"{layer}.qk")
                done("pe", transposes(T2[:, 0], work, 2 * KD), f"{layer}.qkT_ps")

            def heads_products(stat, rhs):
                for b in range(4):
                    last = mm(S4[:, b], stat[:, b // 2, :], rhs[:, 4 * b:4 * b + 4, :], start=True, stop=True)
                return last

            def cross(layer):
                s = L[layer]
                wq, wk, wv = (pk(layer, n, KD) for n in ("wq", "wk", "wv"))
                need(pe, "dve", f"{layer}.xT")
                done("pe", product(O2[:, 0, 0:D], xT, wq), f"{layer}.q_ps")
                need(pe, "dve", f"{layer}.q")
                for half in range(2):
                    last = transposes(T2[:, half], work[:, BANK * (half + 1):BANK * (half + 2)], 4)
                done("pe", last, f"{layer}.qT_ps")

                def key_block(n):
                    hf, nb = divmod(n, 4)
                    for k in range(KD):
                        last = mm(S4[:, n % 4, 0:HC // 2], wk[:, k, hf * P:(hf + 1) * P],
                                  ctx_in[:, nb // 2, k, (nb % 2) * (HC // 2):(nb % 2 + 1) * (HC // 2)],
                                  start=(k == 0), stop=(k == KD - 1))
                    last.then_inc(s["kp_ready"], 1)

                def keys_ahead(c, hf):
                    for half in range(2):
                        pe.wait_ge(s["s_taken"], 32 * c + (2 * KEYS_AT[hf] + 3 + half))
                        for n in (2 * half, 2 * half + 1):
                            key_block(4 * hf + n)

                def scores(c, h):
                    if h % HH == 0:
                        pe.wait_ge(s[f"keys_in{h // HH % KD}"], 256 * c + 256 * (h // H + 1))
                    for half in range(2):
                        if h > 1:
                            pe.wait_ge(s["s_taken"], 32 * c + (2 * h - 1 + half))
                        for n0, n1 in ((0, BANK), (BANK, HC)):
                            last = mm(S4f[:, half * 2 * BANK + n0:half * 2 * BANK + n1], q4[:, h % H, :],
                                      keys4[:, h % H // 2, half * HC + n0:half * HC + n1], start=True, stop=True)
                        last.then_inc(s["s_ready"], 1)

                for half in range(2):
                    pe.wait_ge(s[f"ctx_in{half}"], 16)
                for n in range(8):
                    if n >= 4:
                        pe.wait_ge(s["up_taken"], n - 3)
                        pe.wait_ge(s["low_taken"], n - 3)
                    key_block(n)
                for part in ("up_taken", "low_taken"):
                    pe.wait_ge(s[part], 8)
                need(pe, "dve", f"{layer}.q4")
                scores(0, 0)

                def chunk(c, last_chunk):
                    for b in range(8):
                        if b in (0, 2):
                            pe.wait_ge(s["s_taken"], 32 * c + (b // 2 + 1))
                        if b >= 4:
                            pe.wait_ge(s["vp_taken"], 8 * c + (b - 3))
                        for t in (2 * b, 2 * b + 1):
                            for k in range(KD):
                                last = mm(S4[0:TK, b % 4, (t % 2) * D:(t % 2 + 1) * D],
                                          ctx_in[:, t // TH, k, (t % TH) * TK:(t % TH + 1) * TK], wv[:, k, :],
                                          start=(k == 0), stop=(k == KD - 1))
                        last.then_inc(s["vp_ready"], 1)
                    pe.wait_ge(s["vp_taken"], 8 * c + 8)
                    scores(c, 1)

                    def values(h, g):
                        e = GROUPS[GROUP_AT["T", h, g]][3]
                        pe.wait_ge(s[f"t_{e}"], TAKEN[e][-1] * c + TAKEN[e][GROUP_AT["T", h, g]])
                        quad = h // 4
                        if h % 4 == 0 and g == 0 and quad >= 2:
                            pe.wait_ge(s["o_taken"], 4 * c + (quad - 1))
                        for i in range(4):
                            last = mm(O2[32 * i:32 * i + 32, quad % 2, (h % 4) * P:(h % 4 + 1) * P],
                                      vv[:, 4 * g + i, (h // 2) * 32:(h // 2 + 1) * 32],
                                      pT[0:TK, g, i * P:(i + 1) * P], start=(g == 0), stop=(g == 3))
                        last.then_inc(s["pv_done"], 1)

                    waiting = None
                    for n, (kind, h, g, _) in enumerate(GROUPS):
                        if kind == "T" and g == 0 and h in KEYS_AT and not last_chunk:
                            hf = KEYS_AT.index(h)
                            if hf == 0:
                                for half in range(2):
                                    pe.wait_ge(s[f"ctx_in{half}"], 16 * c + 32)
                            keys_ahead(c, hf)
                        if kind == "T" and g == (2 if h in LATE else 0):
                            if h in KEYS_AT and not last_chunk:
                                for part in ("up_taken", "low_taken"):
                                    pe.wait_ge(s[part], 8 * c + (8 + 4 * (KEYS_AT.index(h) + 1)))
                            if h < H - 2:
                                scores(c, h + 2)
                            elif h == H - 1 and not last_chunk:
                                scores(c, H)
                        if kind == "T" and g == 0:
                            pe.wait_ge(s["p_ready"], 16 * c + (h + 1))
                        if kind == "O":
                            if n == NG - 1:
                                values(*waiting)
                                waiting = None
                            pe.wait_ge(s["o_taken"], 4 * c + (h + 1))
                        if n >= 2:
                            e = GROUPS[n - 2][3]
                            pe.wait_ge(s[f"t_{e}"], TAKEN[e][-1] * c + TAKEN[e][n - 2])
                        if kind == "T":
                            last = transposes(T2[:, n % 2], sc[:, h % 3, 4 * g * TK:(4 * g + 4) * TK], 4, TK)
                        else:
                            last = transposes(T2[:, n % 2], o_sb[:, h % 2], 4)
                        last.then_inc(s["t_ready"], 1)
                        if waiting:
                            values(*waiting)
                            waiting = None
                        if kind == "T":
                            waiting = (h, g)
                    for e in ("act", "dve"):
                        pe.wait_ge(s[f"t_{e}"], TAKEN[e][-1] * c + TAKEN[e][-1])

                with pe.Fori(0, NC - 1) as c:
                    chunk(c, False)
                chunk(NC - 1, True)
                tail(layer)

            def experts(layer):
                s = L[layer]
                F = FF[layer]
                m = KD * F
                need(pe, "dve", f"{layer}.weights")

                def expert(e, b, n):
                    pe.wait_ge(s[f"w_in{b}"], 32 * n + 32)
                    for j in range(2 if layer in GATED else 1):
                        w = fb[:, b, j * m:(j + 1) * m].rearrange("p (k n) -> p k n", k=KD)
                        for i in range(2):
                            last = product(S4[:, 2 * j + i, 0:F // 2], xT, w[:, :, i * F // 2:(i + 1) * F // 2])
                        last.then_inc(s["g_ready"], 1)
                    w = fb[0:F // E, b, (m * (2 if layer in GATED else 1)):][:, 0:E * D] \
                        .rearrange("p (t n) -> p t n", t=E)
                    pe.wait_ge(s["h_ready"], e + 1)
                    for j in range(2):
                        last = transposes(T2[:, j], hid[:, j * F // 2:(j + 1) * F // 2], 4, F // E)
                        last.then_inc(s["t_ready"], 1)
                    pe.wait_ge(s["t_dve"], e + 1)
                    pe.wait_ge(s["t_act"], e + 1)
                    for t in range(E):
                        last = mm(O2[:, b, 0:D], hidT[0:F // E, t, :], w[:, t, :], start=(t == 0), stop=(t == E - 1))
                    last.then_inc(s["y_ready"], 1)

                with pe.Fori(0, E // 2) as n:
                    for b in range(2):
                        expert(2 * n + b, b, n)

            pe.wait_ge(consts_in, 16)
            for layer in layers:
                norm(layer)
                packed(pe, layer)
                if layer == "L0x":
                    need(pe, "dve", f"{layer}.xT")
                    for k in range(KD):
                        mm(O2[:, 0, 0:D], xT[:, k, :], pk(layer, "w1", KD)[:, k, :], start=(k == 0), stop=False)
                    need(pe, "dve", f"{layer}.mean")
                    for k in range(KD):
                        last = mm(O2[:, 0, 0:D], x2T[:, k, :], pk(layer, "w2", KD)[:, k, :], start=False,
                                  stop=(k == KD - 1))
                    done("pe", last, f"{layer}.out")
                elif layer == "L0a":
                    norm2(layer)
                    need(pe, "dve", f"{layer}.xT")
                    done("pe", product(O2[:, 0, 0:D], xT, pk(layer, "gate", KD)), f"{layer}.gate_ps")
                    need(pe, "dve", f"{layer}.x2T")
                    qkv(layer, x2T)
                elif layer in ("L1a", "L2a"):
                    need(pe, "dve", f"{layer}.xT")
                    qkv(layer, xT)
                if layer in ("L0a", "L2a"):
                    need(pe, "dve", f"{layer}.qblk")
                    done("pe", heads_products(halfT, blk), f"{layer}.A_ps")
                    need(pe, "dve", f"{layer}.AT")
                    for h in range(H):
                        last = mm(O2[:, 1, h * (DH + 1):(h + 1) * (DH + 1)], mats3[:, h, :], vaug[:, h, :],
                                  start=True, stop=True)
                    done("pe", last, f"{layer}.num_ps")
                    tail(layer)
                elif layer == "L1a":
                    need(pe, "dve", f"{layer}.kblk")
                    done("pe", heads_products(halfT, blk), f"{layer}.S_ps")
                    need(pe, "act", f"{layer}.p")
                    for b in range(4):
                        last = transposes(S4[:, b], mats[:, b * BANK:(b + 1) * BANK], 4)
                    done("pe", last, f"{layer}.pT_ps")
                    need(pe, "dve", f"{layer}.pT")
                    for h in range(H):
                        last = mm(O2[:, 1, h * DH:(h + 1) * DH], matsT3[:, h, :], vaug[:, h, 0:DH],
                                  start=True, stop=True)
                    done("pe", last, f"{layer}.num_ps")
                    tail(layer)
                elif layer == "L3a":
                    need(pe, "dve", f"{layer}.V")
                    for h in range(H):
                        last = mm(O2[:, 1, h * DH:(h + 1) * DH], mats3[:, h, :], vaug[:, h, 0:DH],
                                  start=True, stop=True)
                    done("pe", last, f"{layer}.num_ps")
                    tail(layer)
                elif layer == "L1f":
                    norm2(layer)
                    need(pe, "dve", f"{layer}.x2T")
                    need(pe, "dve", f"{layer}.w")
                    w1 = fb[:, 0, 0:2048].rearrange("p (k n) -> p k n", k=KD)
                    w2 = fb[:, 1, 0:2048].rearrange("p (t n) -> p t n", t=8)
                    for i in range(2):
                        last = product(S4[:, i], x2T, w1[:, :, i * BANK:(i + 1) * BANK])
                    done("pe", last, f"{layer}.z_ps")
                    need(pe, "act", f"{layer}.y")
                    for i in range(2):
                        last = transposes(S4[:, 2 + i], hid[:, i * BANK:(i + 1) * BANK], 4)
                    done("pe", last, f"{layer}.yT_ps")
                    need(pe, "dve", f"{layer}.yT")
                    done("pe", product(O2[:, 0, 0:D], hidT, w2, 8), f"{layer}.out")
                elif layer in ("L2x", "L3x"):
                    cross(layer)
                elif layer in FF:
                    need(pe, "dve", f"{layer}.xT")
                    done("pe", product(O2[:, 0, 0:E], xT, pk(layer, "gate", KD)), f"{layer}.logit")
                    if layer == "L3f":
                        need(pe, "dve", f"{layer}.onehot")
                        mm(O2[:, 1, 0:E], C["causal"], one0, start=True, stop=True)
                        done("pe", mm(O2[:, 1, E:2 * E], C["causal"], one1, start=True, stop=True), f"{layer}.pos")
                    experts(layer)
                elif layer == "L1x":
                    s = L[layer]
                    need(pe, "dve", f"{layer}.A")
                    done("pe", transposes(T2[:, 1], x2, KD), f"{layer}.AT_ps")
                    need(pe, "dve", f"{layer}.AT")

                    def sim(c, first):
                        for half in range(2):
                            pe.wait_ge(s[f"ctx_in{half}"], 16 * c + 16)
                            if not first:
                                pe.wait_ge(s["s_taken"], 2 * c - 1 + half)
                            for n0, n1 in ((0, BANK), (BANK, HC)):
                                for k in range(KD):
                                    last = mm(S4f[:, half * 2 * BANK + n0:half * 2 * BANK + n1], x2T[:, k, :],
                                              ctx_in[:, half, k, n0:n1], start=(k == 0), stop=(k == KD - 1))
                            last.then_inc(s["s_ready"], 1)

                    sim(0, True)
                    with pe.Fori(1, NC) as c:
                        sim(c, False)

                    def attend(c, first):
                        for half in range(2):
                            pe.wait_ge(s["p_ready"], 2 * c + half + 1)
                            if half or not first:
                                pe.wait_ge(s["t_dve"], 2 * c + half)
                                pe.wait_ge(s["t_act"], 2 * c + half)
                            for g in range(2):
                                last = transposes(T2[:, g], sc[:, half, 4 * g * TK:(4 * g + 4) * TK], 4, TK)
                                last.then_inc(s["t_ready"], 1)
                            pe.wait_ge(s[f"nat_in{half}"], 16 * c + 16)
                            if not first:
                                pe.wait_ge(s["pv_taken"], 2 * c - 1 + half)
                            for g in range(2):
                                pe.wait_ge(s["t_act" if g else "t_dve"], 2 * c + half + 1)
                                for i in range(4):
                                    t = 4 * g + i
                                    last = mm(O2[:, half, 0:D], pT[0:TK, 2 * half + g, i * P:(i + 1) * P],
                                              fb[0:TK, half, t * D:(t + 1) * D], start=(t == 0), stop=(t == TH - 1))
                            last.then_inc(s["pv_ready"], 1)

                    attend(0, True)
                    with pe.Fori(1, NC) as c:
                        attend(c, False)
                    need(pe, "dve", f"{layer}.bat")
                    done("pe", mm(O2[:, 0, 0:D + 1], mats3[:, 0, :], work[:, 512:512 + D + 1], start=True, stop=True),
                         f"{layer}.hc_ps")
                    need(pe, "dve", f"{layer}.f")
                    transposes(S4[:, 0], arena[:, 0:512], 4)
                    done("pe", transposes(S4[:, 1], arena[:, 512:768], 2), f"{layer}.fT_ps")
                    need(pe, "dve", f"{layer}.fT")
                    w = pk(layer, "w_qv", 8)
                    fT = arena[:, 1024:1024 + 768].rearrange("p (k n) -> p k n", k=6)
                    for k in range(8):
                        last = mm(O2[:, 1, 0:D], xT[:, k, :] if k < 2 else fT[:, k - 2, :], w[:, k, :],
                                  start=(k == 0), stop=(k == 7))
                    done("pe", last, f"{layer}.out")

        @block.scalar
        def _(act):
            def cross(layer):
                s = L[layer]
                bias = pk(layer, "bk") if layer == "L2x" else None

                def keys(hf, c, first=False):
                    for nb in range(4):
                        act.wait_ge(s["kp_ready"], 8 * c + (4 * hf + nb + 1))
                        if nb == 0 and hf:
                            act.wait_ge(s["keys_in0"], 256 * c + 256)
                        elif nb == 0 and not first:
                            act.wait_ge(s["keys_in1"], 256 * c)
                        dst = keys_hl[:, 0, nb * (HC // 2):(nb + 1) * (HC // 2)]
                        src = S4[:, nb, 0:HC // 2]
                        if bias is None:
                            ins = nc.scalar.activation(dst, src, ACT.Copy)
                        else:
                            ins = nc.scalar.activation(dst, src, ACT.Identity, bias=bias[:, hf:hf + 1])
                        ins.then_inc(s["up_taken"], 1)

                def take_group(c, n):
                    kind, h, g, _ = GROUPS[n]
                    act.wait_ge(s["t_ready"], NG * c + (n + 1))
                    if h >= 1:
                        act.wait_ge(s["pv_done"], 64 * c + (4 * (h - 1) + g + 1))
                    nc.scalar.activation(pT[0:TK, g, :], T2[0:TK, n % 2, :], ACT.Copy).then_inc(s["t_act"], 1)

                def take_quad(c, quad):
                    act.wait_ge(s["pv_done"], 64 * c + 16 * (quad + 1))
                    if quad >= 2:
                        act.wait_ge(s["t_ready"], NG * c + (GROUP_AT["O", quad - 2, 0] + 1))
                    nc.scalar.activation(o_sb[:, quad % 2, :], O2[:, quad % 2, :], ACT.Copy).then_inc(s["o_taken"], 1)

                if bias is not None:
                    packed(act, layer)
                for hf in range(KD):
                    keys(hf, 0, True)

                def soften(c, h):
                    act.wait_ge(s["s_taken"], 32 * c + (2 * h + 2))
                    nc.scalar.activation(sc[:, h % 3, :], sc[:, h % 3, :], ACT.Exp, bias=n_new[:, h:h + 1],
                                         scale=-1.0, accum_out=l_new[:, h:h + 1]).then_inc(s["p_ready"], 1)

                def chunk(c, last_chunk):
                    soften(c, 0)
                    for h in range(H):
                        if h in KEYS_AT and not last_chunk:
                            keys(KEYS_AT.index(h), c + 1)
                        take_group(c, GROUP_AT["T", h, 0])
                        if h == 0:
                            soften(c, 1)
                        take_group(c, GROUP_AT["T", h, 2])
                        if h % 4 == 0 and h:
                            take_quad(c, h // 4 - 1)
                        if h < H - 2:
                            soften(c, h + 2)
                        elif h == H - 2:
                            act.wait_ge(s["delta"], c + 1)
                            nc.scalar.activation(alpha, alpha, ACT.Exp).then_inc(s["alpha"], 1)
                    take_quad(c, 3)

                with act.Fori(0, NC - 1) as c:
                    chunk(c, False)
                chunk(NC - 1, True)

            def experts(layer):
                s = L[layer]
                F = FF[layer]
                per = 2 if layer in GATED else 1
                fn = ACT.Silu if layer in GATED else ACT.Gelu

                def expert(e):
                    act.wait_ge(s["g_ready"], per * e + 1)
                    nc.scalar.activation(gated[:, 0:F].rearrange("p (i n) -> p i n", i=2), S4[:, 0:2, 0:F // 2], fn) \
                        .then_inc(s["act_done"], 1)
                    act.wait_ge(s["t_ready"], 2 * e + 2)
                    nc.scalar.activation(hidT[0:F // E, 4:8, :].rearrange("p t n -> p (t n)"), T2[0:F // E, 1, :],
                                         ACT.Copy).then_inc(s["t_act"], 1)

                with act.Fori(0, E // 2) as n:
                    for b in range(2):
                        expert(2 * n + b)

            for layer in layers:
                if layer == "L0a":
                    need(act, "dve", f"{layer}.g")
                    done("act", nc.scalar.activation(x2[:, :], x2[:, :], ACT.Sigmoid, accum_out=row), f"{layer}.sig")
                elif layer == "L2a":
                    need(act, "dve", f"{layer}.neg")
                    done("act", nc.scalar.activation(work[:, 512:1024], work[:, 512:1024], ACT.Exp), f"{layer}.elu")
                elif layer == "L1a":
                    need(act, "dve", f"{layer}.sm")
                    done("act", nc.scalar.activation(mats, mats, ACT.Exp), f"{layer}.p")
                elif layer == "L3a":
                    need(act, "dve", f"{layer}.abs")
                    done("act", nc.scalar.activation(head_a[:, 0:H], head_b[:, 0:H], ACT.Exp, scale=-1.0),
                         f"{layer}.e")
                    need(act, "dve", f"{layer}.onep")
                    done("act", nc.scalar.activation(head_b[:, 0:H], head_a[:, 0:H], ACT.Ln), f"{layer}.ln1p")
                    need(act, "dve", f"{layer}.ln")
                    for h in range(H):
                        last = nc.scalar.activation(mats3[:, h, :], C["steps"], ACT.Exp, scale=lam[:, h:h + 1])
                    done("act", last, f"{layer}.decay")
                elif layer == "L1f":
                    need(act, "dve", f"{layer}.z")
                    done("act", nc.scalar.activation(hid, hid, ACT.Silu), f"{layer}.y")
                elif layer in ("L2x", "L3x"):
                    cross(layer)
                elif layer in FF:
                    if layer != "L0f":
                        need(act, "dve", f"{layer}.logit")
                        done("act", nc.scalar.activation(prob, prob, ACT.Exp, accum_out=row), f"{layer}.prob")
                    experts(layer)
                elif layer == "L1x":
                    s = L[layer]
                    need(act, "pool", f"{layer}.gmax")
                    need(act, "dve", f"{layer}.max")

                    def soften(c, first):
                        for half in range(2):
                            if not first:
                                act.wait_ge(s["t_ready"], 4 * c + (2 * half - 2))
                            nc.scalar.activation(sc[:, half, 0:HC], arena[:, bass.ds(c * CH + half * HC, HC)], ACT.Exp,
                                                 bias=rec, accum_out=sums[:, bass.ds(2 * c + half, 1)]) \
                                .then_inc(s["p_ready"], 1)
                            act.wait_ge(s["t_ready"], 4 * c + (2 * half + 2))
                            if not first:
                                act.wait_ge(s["pv_ready"], 2 * c + half - 1)
                            nc.scalar.activation(pT[0:TK, 2 * half + 1, :], T2[0:TK, 1, :], ACT.Copy) \
                                .then_inc(s["t_act"], 1)

                    soften(0, True)
                    with act.Fori(1, NC) as c:
                        soften(c, False)
                    done("act", nc.scalar.activation(bat, row_max, ACT.Exp, bias=gmax, scale=1.0), f"{layer}.bat")

        @block.vector
        def _(dve):
            V = nc.vector

            def link(ins):
                owned["dve"] += 1
                ins.then_inc(own["dve"], 1)
                dve.wait_ge(own["dve"], owned["dve"])

            def bcast(ap, n, inner=True):
                m = ap.shape[1]
                if inner:
                    return ap.unsqueeze(2).to_broadcast([P, m, n])
                return ap.unsqueeze(1).to_broadcast([P, n, m])

            def variance(src, layer, stage):
                link(V.bn_stats(stats, src))
                link(V.bn_aggr(mv, stats))
                done("dve", V.tensor_scalar(mv[:, 1:2], mv[:, 1:2], 1e-5, None, ALU.add), f"{layer}.{stage}")

            def scaled(out, src):
                return V.tensor_scalar(out, src, mv[:, 0:1], rstd, ALU.subtract, ALU.mult)

            def norm(layer):
                variance(x[:, :], layer, "var")
                need(dve, "pool", f"{layer}.rstd")
                done("dve", scaled(xn[:, :], x[:, :]), f"{layer}.xn")
                need(dve, "pe", f"{layer}.xnT")
                done("dve", V.tensor_copy(xT[:, :, :].rearrange("p k n -> p (k n)"), T2[:, 0, 0:D]), f"{layer}.xT")

            def norm2(layer):
                packed(dve, layer)
                variance(xn[:, :], layer, "var2")
                need(dve, "pool", f"{layer}.rstd2")
                link(scaled(x2[:, :], xn[:, :]))
                link(V.tensor_tensor(x2[:, :], x2[:, :], pk(layer, "ln_g"), ALU.mult))
                done("dve", V.tensor_tensor(x2[:, :], x2[:, :], pk(layer, "ln_b"), ALU.add), f"{layer}.x2")
                need(dve, "pe", f"{layer}.x2T_ps")
                done("dve", V.tensor_copy(x2T[:, :, :].rearrange("p k n -> p (k n)"), T2[:, 1, 0:D]), f"{layer}.x2T")

            def tail(layer):
                need(dve, "pe", f"{layer}.oT_ps")
                done("dve", V.tensor_copy(oT.rearrange("p k n -> p (k n)"), T2[:, 1, 0:D]), f"{layer}.oT")
                need(dve, "pe", f"{layer}.out")
                residual(layer, O2[:, 0, 0:D])

            def residual(layer, out):
                if "b_out" in PACKS[layer] or "b" in PACKS[layer]:
                    link(V.tensor_tensor(x[:, :], x[:, :], pk(layer, "b_out" if "b_out" in PACKS[layer] else "b"),
                                         ALU.add))
                done("dve", V.tensor_tensor(x[:, :], out, x[:, :], ALU.add), f"{layer}.end")
                need(dve, "dve", f"{layer}.end")

            def spread(psum, stage):
                for k in range(KD):
                    last = V.tensor_tensor(blk[:, k * HH:(k + 1) * HH, :], bcast(psum[:, k * P:(k + 1) * P], HH, False),
                                           bcast(C["head"], P), ALU.mult)
                done("dve", last, stage)

            def ranks(src):
                a3 = half.rearrange("p (e j) -> p e j", e=E)
                b3 = eye_a.rearrange("p (e j) -> p e j", e=E)
                link(V.tensor_tensor(b3, bcast(src, E, False), bcast(src, E), ALU.is_equal))
                link(V.tensor_tensor(eye_a, eye_a, C["before"], ALU.mult))
                link(V.tensor_tensor(a3, bcast(src, E, False), bcast(src, E), ALU.is_gt))
                link(V.tensor_tensor(half, half, eye_a, ALU.add))
                link(V.tensor_reduce(rank, a3, X, ALU.add))

            def softmax_gate(layer, bias):
                need(dve, "pe", f"{layer}.logit")
                if bias is None:
                    link(V.tensor_copy(prob, O2[:, 0, 0:E]))
                else:
                    link(V.tensor_tensor(prob, O2[:, 0, 0:E], bias, ALU.add))
                link(V.tensor_reduce(rec, prob, X, ALU.max))
                done("dve", V.tensor_scalar(prob, prob, rec, None, ALU.subtract), f"{layer}.logit")
                need(dve, "act", f"{layer}.prob")
                link(V.reciprocal(rec, row))
                link(V.tensor_scalar(prob, prob, rec, None, ALU.mult))

            def experts(layer):
                s = L[layer]
                F = FF[layer]
                per = 2 if layer in GATED else 1

                def expert(e, b):
                    V.tensor_copy(wcur[:, b:b + 1], wts[:, bass.ds(e, 1)]).then_inc(s["y_taken"], 1)
                    dve.wait_ge(s["y_taken"], 3 * e + 1)
                    dve.wait_ge(s["act_done"], e + 1)
                    if layer in GATED:
                        dve.wait_ge(s["g_ready"], per * e + per)
                        V.scalar_tensor_tensor(
                            hid[:, 0:F].rearrange("p (i n) -> p i n", i=2), S4[:, 2:4, 0:F // 2], wcur[:, b:b + 1],
                            gated[:, 0:F].rearrange("p (i n) -> p i n", i=2), ALU.mult, ALU.mult) \
                            .then_inc(s["h_ready"], 1)
                    else:
                        V.tensor_scalar(hid[:, 0:F], gated[:, 0:F], wcur[:, b:b + 1], None, ALU.mult) \
                            .then_inc(s["h_ready"], 1)
                    dve.wait_ge(s["t_ready"], 2 * e + 1)
                    V.tensor_copy(hidT[0:F // E, 0:4, :].rearrange("p t n -> p (t n)"), T2[0:F // E, 0, :]) \
                        .then_inc(s["t_dve"], 1)
                    dve.wait_ge(s["y_ready"], e + 1)
                    V.tensor_tensor(yacc, O2[:, b, 0:D], yacc, ALU.add).then_inc(s["y_taken"], 2)
                    dve.wait_ge(s["y_taken"], 3 * e + 3)

                with dve.Fori(0, E // 2) as n:
                    for b in range(2):
                        expert(2 * n + b, b)

            def cross(layer):
                s = L[layer]
                packed(dve, layer)
                need(dve, "pe", f"{layer}.q_ps")
                rep4 = work[:, BANK:3 * BANK].rearrange("p (j r d) -> p j r d", r=4, d=QR)
                q_ps = O2[:, 0, 0:D]
                if layer == "L2x":
                    link(V.tensor_tensor(x2[:, :], q_ps, pk(layer, "bq"), ALU.add))
                    q_ps = x2[:, :]
                done("dve", V.tensor_scalar(rep4, q_ps.rearrange("p (j d) -> p j d", d=QR).unsqueeze(2)
                                            .to_broadcast([P, NP, 4, QR]), -DH ** -0.5, None, ALU.mult), f"{layer}.q")
                V.memset(n_old, BIG)
                V.memset(acc, 0.0)
                link(V.memset(l_sum, 0.0))

                def keys(hf, c):
                    for nb in range(4):
                        dve.wait_ge(s["up_taken"], 8 * c + (4 * hf + nb + 1))
                        up, low = (keys_hl[:, i, nb * (HC // 2):(nb + 1) * (HC // 2)] for i in range(2))
                        src = S4[:, nb, 0:HC // 2]
                        if layer == "L2x":
                            ins = V.scalar_tensor_tensor(low, src, pk(layer, "bk")[:, hf:hf + 1], up.bitcast(F32),
                                                         ALU.add, ALU.subtract)
                        else:
                            ins = V.tensor_tensor(low, src, up.bitcast(F32), ALU.subtract)
                        ins.then_inc(s["low_taken"], 1)

                need(dve, "pe", f"{layer}.qT_ps")

                def queries(ap, rows):
                    n = rows.stop - rows.start
                    return ap.rearrange("p (j n) -> p j n", n=P).unsqueeze(2).to_broadcast([n, NP, 2, P])

                def own_rows(rows):
                    n = rows.stop - rows.start
                    return C["pair"][rows, :].unsqueeze(1).unsqueeze(3).to_broadcast([n, NP, 2, P])

                upper, lower = slice(0, P // 2), slice(P // 2, P)
                qT = T2[:, :, :].rearrange("p b n -> p (b n)")
                V.tensor_tensor(q4[upper].rearrange("p (j a) n -> p j a n", a=2), queries(qT[upper], upper),
                                own_rows(upper), ALU.mult)
                link(V.tensor_copy(q_up[lower], qT[lower]))
                link(V.tensor_tensor(q_low[lower], qT[lower], q_up[lower].bitcast(F32), ALU.subtract))
                done("dve", V.tensor_tensor(q4[lower].rearrange("p (j a) n -> p j a n", a=2),
                                            queries(q_low[lower], lower), own_rows(lower), ALU.mult), f"{layer}.q4")
                for hf in range(KD):
                    keys(hf, 0)

                def take_group(c, n):
                    kind, h, g, _ = GROUPS[n]
                    dve.wait_ge(s["t_ready"], NG * c + (n + 1))
                    if kind == "T":
                        if h >= 1:
                            dve.wait_ge(s["pv_done"], 64 * c + (4 * (h - 1) + g + 1))
                        V.tensor_copy(pT[0:TK, g, :], T2[0:TK, n % 2, :]).then_inc(s["t_dve"], 1)
                        return
                    src = T2[:, n % 2, :].rearrange("p (a b g m d) -> p a b m d g", a=2, b=2, g=4, m=2)
                    dst = oc[:, h * 4 * DH:(h + 1) * 4 * DH].rearrange("p (a b d) -> p a b d", a=2, b=2)
                    for b in range(2):
                        last = V.tensor_reduce(dst[:, :, b], src[:, :, b, b], X, ALU.add)
                    last.then_inc(s["t_dve"], 1)

                def take_mask(c):
                    dve.wait_ge(s["mask_in"], 16 * c + 16)
                    if layer == "L2x":
                        ins = V.tensor_scalar(mask_bias[:, :], mask_in.bitcast(I32), 0.0, MASKED, ALU.is_equal, ALU.mult)
                    else:
                        ins = V.tensor_scalar(mask_bias[:, :], mask_in, 1.0e9, None, ALU.mult)
                    ins.then_inc(s["mask_taken"], 1)
                    dve.wait_ge(s["mask_taken"], c + 1)

                def take_scores(c, h, i, first=False):
                    dve.wait_ge(s["s_ready"], 32 * c + (2 * h + i + 1))
                    if h >= 3 and i == 0:
                        dve.wait_ge(s["t_ready"], NG * c + (GROUP_AT["T", h - 3, 3] + 1))
                    elif h == 0 and i == 0 and not first:
                        dve.wait_ge(s["t_ready"], NG * c + (GROUP_AT["T", H - 1, 3] + 1 - NG))
                    ins = V.memset(tick, 0.0)
                    if h == HH and i == 0:
                        ins.then_inc(s["half_read"], 1)
                    V.tensor_tensor_reduce(
                        sc[:, h % 3, i * HC:(i + 1) * HC], S4f[:, i * 2 * BANK:i * 2 * BANK + HC],
                        mask_bias[:, i * HC:(i + 1) * HC], 1.0, (n_half if i else n_old)[:, h:h + 1],
                        ALU.add, ALU.min, (n_new if i else n_half)[:, h:h + 1]).then_inc(s["s_taken"], 1)
                    dve.wait_ge(s["s_taken"], 32 * c + (2 * h + i + 1))

                def chunk(c, last_chunk):
                    for b in range(8):
                        dve.wait_ge(s["vp_ready"], 8 * c + (b + 1))
                        V.tensor_copy(vv[:, 2 * b:2 * b + 2, :].rearrange("p t n -> p (t n)"), S4[0:TK, b % 4, :]) \
                            .then_inc(s["vp_taken"], 1)
                    for i in range(2):
                        take_scores(c, 1, i)
                    for h in range(H):
                        if h in KEYS_AT and not last_chunk:
                            keys(KEYS_AT.index(h), c + 1)
                        ahead = h < H - 2
                        if ahead and h not in LATE:
                            take_scores(c, h + 2, 0)
                        if h % 4 == 1 and h > 1:
                            take_group(c, GROUP_AT["O", (h - 5) // 4, 0])
                        take_group(c, GROUP_AT["T", h, 1])
                        if ahead:
                            if h in LATE:
                                take_scores(c, h + 2, 0)
                            take_scores(c, h + 2, 1)
                        if h == H - 3:
                            V.tensor_tensor(alpha, n_new, n_old, ALU.subtract).then_inc(s["delta"], 1)
                            dve.wait_ge(s["delta"], c + 1)
                            V.tensor_copy(n_old, n_new).then_inc(s["finished"], 1)
                            dve.wait_ge(s["finished"], 4 * c + 1)
                        if h == H - 2 and not last_chunk:
                            take_mask(c + 1)
                        take_group(c, GROUP_AT["T", h, 3])
                    dve.wait_ge(s["alpha"], c + 1)
                    V.tensor_tensor(l_sum, l_sum, alpha, ALU.mult).then_inc(s["finished"], 1)
                    dve.wait_ge(s["finished"], 4 * c + 2)
                    V.tensor_tensor(l_sum, l_sum, l_new, ALU.add).then_inc(s["finished"], 1)
                    if not last_chunk:
                        for i in range(2):
                            take_scores(c + 1, 0, i)
                    take_group(c, GROUP_AT["O", 3, 0])
                    dve.wait_ge(s["t_dve"], TAKEN["dve"][-1] * c + TAKEN["dve"][-1])
                    acc3 = acc.rearrange("p (h d) -> p h d", h=H)
                    V.tensor_tensor(acc3, acc3, bcast(alpha, DH), ALU.mult).then_inc(s["acc_taken"], 1)
                    dve.wait_ge(s["acc_taken"], c + 1)
                    V.tensor_tensor(acc, acc, oc, ALU.add).then_inc(s["finished"], 1)
                    dve.wait_ge(s["finished"], 4 * c + 4)

                take_mask(0)
                for i in range(2):
                    take_scores(0, 0, i, True)
                with dve.Fori(0, NC - 1) as c:
                    chunk(c, False)
                chunk(NC - 1, True)
                link(V.reciprocal(l_sum, l_sum))
                ins = V.tensor_tensor(x2[:, :].rearrange("p (h d) -> p h d", h=H),
                                      acc.rearrange("p (h d) -> p h d", h=H), bcast(l_sum, DH), ALU.mult)
                if layer == "L2x":
                    link(ins)
                    ins = V.tensor_tensor(x2[:, :], x2[:, :], pk(layer, "bv"), ALU.add)
                done("dve", ins, f"{layer}.o")
                tail(layer)

            dve.wait_ge(x_in, 16)
            dve.wait_ge(consts_in, 16)
            for layer in layers:
                norm(layer)
                packed(dve, layer)
                x2h = x2[:, :].rearrange("p (h d) -> p h d", h=H)
                if layer == "L0x":
                    s = L[layer]
                    bufs = [ctx_in[:, :, :, :].rearrange("p h k n -> p (h k n)"),
                            sc[:, 0:2, :].rearrange("p a n -> p (a n)"), arena[:, 0:KD * CH]]
                    for c in range(NC):
                        dve.wait_ge(s[f"ctx_in{c % 3}"], 32 * (c // 3 + 1))
                        V.tensor_reduce(parts4[:, c], bufs[c % 3].rearrange("p (h k n) -> p h k n", h=2, k=KD),
                                        X, ALU.add).then_inc(s["summed"], 1)
                    dve.wait_ge(s["summed"], NC)
                    link(V.tensor_reduce(mean, parts4.rearrange("p c h k -> p k (c h)"), X, ALU.add))
                    link(V.tensor_scalar(mean, mean, 1.0 / NK, None, ALU.mult))
                    done("dve", V.tensor_copy(x2T[:, :, :], bcast(mean, P)), f"{layer}.mean")
                    need(dve, "pe", f"{layer}.out")
                    residual(layer, O2[:, 0, 0:D])
                elif layer == "L0a":
                    norm2(layer)
                    need(dve, "pe", f"{layer}.gate_ps")
                    done("dve", V.tensor_tensor(x2[:, :], O2[:, 0, 0:D], pk(layer, "b_gate"), ALU.add), f"{layer}.g")
                    need(dve, "pe", f"{layer}.qkv_ps")
                    qk = work[:, 0:2 * D]
                    link(V.tensor_tensor(qk, S4[:, 0], pk(layer, "b_qkv")[:, 0:2 * D], ALU.add))
                    link(V.memset(vaug, 1.0))
                    V.tensor_tensor(vaug[:, :, 0:DH], S4[:, 1, 0:D].rearrange("p (h d) -> p h d", h=H),
                                    pk(layer, "b_qkv")[:, 2 * D:3 * D].rearrange("p (h d) -> p h d", h=H), ALU.add)
                    need(dve, "act", f"{layer}.sig")
                    link(V.tensor_scalar(rec, row, 1.0 / D, 1e-5, ALU.mult, ALU.add))
                    link(V.reciprocal(rec, rec))
                    link(V.tensor_scalar(x2[:, :], x2[:, :], rec, None, ALU.mult))
                    q3 = qk.rearrange("p (a n) -> p a n", a=2)
                    link(V.tensor_tensor(q3, q3, bcast(x2[:, :], 2, False), ALU.mult))
                    link(V.tensor_scalar(qk, qk, 0.0, None, ALU.max))
                    link(V.tensor_tensor(qk, qk, qk, ALU.mult))
                    done("dve", V.tensor_scalar(qk, qk, 1e-5, None, ALU.add), f"{layer}.qk")
                elif layer == "L2a":
                    need(dve, "pe", f"{layer}.qkv_ps")
                    qk = work[:, 0:2 * D]
                    done("dve", V.tensor_scalar(work[:, 512:1024], S4[:, 0], 0.0, None, ALU.min), f"{layer}.neg")
                    link(V.memset(vaug, 1.0))
                    V.tensor_copy(vaug[:, :, 0:DH], S4[:, 1, 0:D].rearrange("p (h d) -> p h d", h=H))
                    link(V.tensor_scalar(qk, S4[:, 0], 0.0, None, ALU.max))
                    need(dve, "act", f"{layer}.elu")
                    done("dve", V.tensor_tensor(qk, qk, work[:, 512:1024], ALU.add), f"{layer}.qk")
                if layer in ("L0a", "L2a"):
                    need(dve, "pe", f"{layer}.qkT_ps")
                    V.tensor_copy(halfT.rearrange("p k n -> p (k n)"), T2[:, 0, D:2 * D])
                    spread(T2[:, 0], f"{layer}.qblk")
                    need(dve, "pe", f"{layer}.A_ps")
                    done("dve", V.tensor_tensor(mats3, S4f.rearrange("p (h n) -> p h n", h=H),
                                                bcast(C["causal"], H, False), ALU.mult), f"{layer}.AT")
                    need(dve, "pe", f"{layer}.num_ps")
                    link(V.tensor_copy(num, O2[:, 1, 0:H * (DH + 1)].rearrange("p (h n) -> p h n", h=H)))
                    den = head_a[:, 0:H]
                    if layer == "L0a":
                        link(V.tensor_scalar(den, num[:, :, DH], 1e-5, None, ALU.add))
                    else:
                        link(V.tensor_scalar(den, num[:, :, DH], 1e-6, None, ALU.max))
                    link(V.reciprocal(den, den))
                    done("dve", V.tensor_tensor(x2h, num[:, :, 0:DH], bcast(den, DH), ALU.mult), f"{layer}.o")
                    tail(layer)
                elif layer == "L1a":
                    need(dve, "pe", f"{layer}.qkv_ps")
                    qk, q3 = work[:, 0:2 * D], work[:, 0:2 * D].rearrange("p (h d) -> p h d", d=DH)
                    sq, s3 = work[:, 512:1024], work[:, 512:1024].rearrange("p (h d) -> p h d", d=DH)
                    V.tensor_copy(vaug[:, :, 0:DH], S4[:, 1, 0:D].rearrange("p (h d) -> p h d", h=H))
                    link(V.tensor_copy(qk, S4[:, 0]))
                    link(V.tensor_reduce(vsum, q3, X, ALU.add))
                    link(V.tensor_scalar(vsum, vsum, 1.0 / DH, None, ALU.mult))
                    link(V.tensor_tensor(q3, q3, bcast(vsum, DH), ALU.subtract))
                    link(V.tensor_tensor(sq, qk, qk, ALU.mult))
                    link(V.tensor_reduce(vsum, s3, X, ALU.add))
                    done("dve", V.tensor_scalar(head_a, vsum, 1.0 / DH, 1e-5, ALU.mult, ALU.add), f"{layer}.var2")
                    need(dve, "pool", f"{layer}.rstd2")
                    link(V.tensor_tensor(q3, q3, bcast(head_b, DH), ALU.mult))
                    link(V.tensor_tensor(qk, qk, pk(layer, "ln_w"), ALU.mult))
                    link(V.tensor_tensor(qk, qk, pk(layer, "ln_b"), ALU.add))
                    done("dve", V.tensor_scalar(qk[:, 0:D], qk[:, 0:D], DH ** -0.5, None, ALU.mult), f"{layer}.qk")
                    need(dve, "pe", f"{layer}.qkT_ps")
                    V.tensor_copy(halfT.rearrange("p k n -> p (k n)"), T2[:, 0, 0:D])
                    spread(T2[:, 0, D:2 * D], f"{layer}.kblk")
                    need(dve, "pe", f"{layer}.S_ps")
                    link(V.tensor_tensor(mats3, S4f.rearrange("p (h n) -> p h n", h=H),
                                         bcast(C["causal_bias"], H, False), ALU.add))
                    link(V.tensor_reduce(head_a[:, 0:H], mats3, X, ALU.max))
                    done("dve", V.tensor_tensor(mats3, mats3, bcast(head_a[:, 0:H], P), ALU.subtract), f"{layer}.sm")
                    need(dve, "act", f"{layer}.p")
                    link(V.tensor_reduce(head_a[:, 0:H], mats3, X, ALU.add))
                    link(V.reciprocal(head_a[:, 0:H], head_a[:, 0:H]))
                    need(dve, "pe", f"{layer}.pT_ps")
                    done("dve", V.tensor_copy(matsT, S4f), f"{layer}.pT")
                    need(dve, "pe", f"{layer}.num_ps")
                    done("dve", V.tensor_tensor(x2h, O2[:, 1, 0:D].rearrange("p (h d) -> p h d", h=H),
                                                bcast(head_a[:, 0:H], DH), ALU.mult), f"{layer}.o")
                    tail(layer)
                elif layer == "L3a":
                    ld = pk(layer, "log_decay")
                    link(V.tensor_scalar(head_a[:, 0:H], ld, -1.0, None, ALU.mult))
                    done("dve", V.tensor_tensor(head_b[:, 0:H], head_a[:, 0:H], ld, ALU.max), f"{layer}.abs")
                    link(V.tensor_scalar(lam, ld, 0.0, None, ALU.min))
                    need(dve, "act", f"{layer}.e")
                    done("dve", V.tensor_scalar(head_a[:, 0:H], head_a[:, 0:H], 1.0, None, ALU.add), f"{layer}.onep")
                    need(dve, "act", f"{layer}.ln1p")
                    done("dve", V.tensor_tensor(lam, lam, head_b[:, 0:H], ALU.subtract), f"{layer}.ln")
                    link(V.tensor_tensor(work[:, 0:D], pk(layer, "q"), pk(layer, "k"), ALU.mult))
                    link(V.tensor_reduce(vsum[:, 0:H], work[:, 0:D].rearrange("p (h d) -> p h d", h=H), X, ALU.add))
                    V.tensor_tensor(vaug[:, :, 0:DH], xn[:, :].rearrange("p (h d) -> p h d", h=H),
                                    bcast(vsum[:, 0:H], DH), ALU.mult)
                    need(dve, "act", f"{layer}.decay")
                    done("dve", V.tensor_tensor(mats3, mats3, bcast(C["causal"], H, False), ALU.mult), f"{layer}.V")
                    need(dve, "pe", f"{layer}.num_ps")
                    link(V.tensor_copy(x2[:, :], O2[:, 1, 0:D]))
                    link(V.tensor_tensor(work[:, 0:D], x2[:, :], x2[:, :], ALU.mult))
                    link(V.tensor_reduce(rec, work[:, 0:D], X, ALU.add))
                    done("dve", V.tensor_scalar(mv[:, 1:2], rec, 1.0 / D, 1e-6, ALU.mult, ALU.add), f"{layer}.var2")
                    need(dve, "pool", f"{layer}.rstd2")
                    link(V.tensor_scalar(x2[:, :], x2[:, :], rstd, None, ALU.mult))
                    done("dve", V.tensor_tensor(x2[:, :], x2[:, :], pk(layer, "norm"), ALU.mult), f"{layer}.o")
                    tail(layer)
                elif layer == "L1f":
                    norm2(layer)
                    dve.wait_ge(L[layer]["q_in"], 64)
                    for b in range(2):
                        link(V.tensor_scalar(fb[:, b, 0:2048], fb[:, b, 0:2048].bitcast(I32), 128.0, None, ALU.subtract))
                    link(V.tensor_tensor(fb[:, 0, 0:2048], fb[:, 0, 0:2048], fb[:, 0, 2048:4096], ALU.mult))
                    done("dve", V.tensor_tensor(fb[:, 1, 0:2048], fb[:, 1, 0:2048], fb[:, 1, 2048:4096], ALU.mult),
                         f"{layer}.w")
                    need(dve, "pe", f"{layer}.z_ps")
                    done("dve", V.tensor_tensor(hid, S4f[:, 0:1024], pk(layer, "b1"), ALU.add), f"{layer}.z")
                    need(dve, "pe", f"{layer}.yT_ps")
                    done("dve", V.tensor_copy(hidT.rearrange("p t n -> p (t n)"), S4f[:, 1024:2048]), f"{layer}.yT")
                    link(V.tensor_tensor(x[:, :], x[:, :], xn[:, :], ALU.add))
                    need(dve, "pe", f"{layer}.out")
                    link(V.tensor_tensor(x2[:, :], O2[:, 0, 0:D], pk(layer, "b2"), ALU.add))
                    done("dve", V.scalar_tensor_tensor(x[:, :], x2[:, :], 0.5, x[:, :], ALU.mult, ALU.add),
                         f"{layer}.end")
                    need(dve, "dve", f"{layer}.end")
                elif layer in ("L2x", "L3x"):
                    cross(layer)
                elif layer in FF:
                    V.memset(yacc, 0.0)
                    if layer == "L0f":
                        need(dve, "pe", f"{layer}.logit")
                        link(V.tensor_copy(prob, O2[:, 0, 0:E]))
                        ranks(prob)
                        link(V.tensor_scalar(rank, rank, 2.0, None, ALU.is_lt))
                        done("dve", V.tensor_tensor(wts, rank, prob, ALU.mult), f"{layer}.weights")
                    elif layer == "L2f":
                        softmax_gate(layer, pk(layer, "bias"))
                        ranks(prob)
                        link(V.tensor_scalar(rank, rank, 2.0, None, ALU.is_lt))
                        link(V.tensor_tensor(wts, rank, prob, ALU.mult))
                        link(V.tensor_reduce(row, wts, X, ALU.add))
                        link(V.tensor_scalar(row, row, 1e-6, None, ALU.add))
                        link(V.reciprocal(row, row))
                        done("dve", V.tensor_scalar(wts, wts, row, None, ALU.mult), f"{layer}.weights")
                    else:
                        softmax_gate(layer, None)
                        ranks(prob)
                        link(V.tensor_scalar(one0, rank, 0.0, None, ALU.is_equal))
                        link(V.tensor_scalar(one1, rank, 1.0, None, ALU.is_equal))
                        done("dve", V.tensor_tensor(wts, one0, one1, ALU.add), f"{layer}.onehot")
                        need(dve, "dve", f"{layer}.onehot")
                        link(V.tensor_tensor(wts, wts, prob, ALU.mult))
                        link(V.tensor_reduce(row, wts, X, ALU.add))
                        link(V.reciprocal(row, row))
                        link(V.tensor_scalar(prob, prob, row, None, ALU.mult))
                        need(dve, "pe", f"{layer}.pos")
                        link(V.tensor_scalar(half[:, 0:2 * E], O2[:, 1, 0:2 * E], float(CAPACITY), None, ALU.is_le))
                        link(V.tensor_tensor(one0, one0, half[:, 0:E], ALU.mult))
                        link(V.tensor_tensor(one1, one1, half[:, E:2 * E], ALU.mult))
                        link(V.tensor_tensor(wts, one0, one1, ALU.add))
                        done("dve", V.tensor_tensor(wts, wts, prob, ALU.mult), f"{layer}.weights")
                    need(dve, "dve", f"{layer}.weights")
                    experts(layer)
                    if layer == "L2f":
                        variance(yacc, layer, "var3")
                        link(V.tensor_tensor(x[:, :], x[:, :], xn[:, :], ALU.add))
                        need(dve, "pool", f"{layer}.rstd3")
                        link(scaled(yacc, yacc))
                    residual(layer, yacc)
                elif layer == "L1x":
                    s = L[layer]
                    w = pk(layer, "w_sim")
                    link(V.tensor_tensor(x2[:, :], xn[:, :], w[:, 0:D], ALU.mult))
                    link(V.tensor_reduce(row, x2[:, :], X, ALU.add))
                    link(V.tensor_tensor(row, row, pk(layer, "b_sim"), ALU.add))
                    link(V.tensor_tensor(x2[:, :], xn[:, :], w[:, 2 * D:3 * D], ALU.mult))
                    done("dve", V.tensor_tensor(x2[:, :], x2[:, :], w[:, D:2 * D], ALU.add), f"{layer}.A")
                    need(dve, "pe", f"{layer}.AT_ps")
                    done("dve", V.tensor_copy(x2T[:, :, :].rearrange("p k n -> p (k n)"), T2[:, 1, 0:D]), f"{layer}.AT")
                    with dve.Fori(0, NC) as c:
                        for i in range(2):
                            dve.wait_ge(s["s_ready"], 2 * c + (i + 1))
                            V.tensor_scalar(arena[:, bass.ds(c * CH + i * HC, HC)],
                                            S4f[:, i * 2 * BANK:i * 2 * BANK + HC], row, None, ALU.add, ALU.max,
                                            accum_out=maxes[:, bass.ds(2 * c + i, 1)]).then_inc(s["s_taken"], 1)
                    dve.wait_ge(s["s_taken"], 2 * NC)
                    link(V.memset(acc, 0.0))
                    link(V.tensor_reduce(row_max, maxes, X, ALU.max))
                    done("dve", V.tensor_scalar(rec, row_max, -1.0, None, ALU.mult), f"{layer}.max")
                    need(dve, "pool", f"{layer}.gmax")
                    link(V.tensor_scalar(gmax, gmax, -1.0, None, ALU.mult))

                    def attend(c, first):
                        for i in range(2):
                            dve.wait_ge(s["t_ready"], 4 * c + (2 * i + 1))
                            if not first:
                                dve.wait_ge(s["pv_ready"], 2 * c + i - 1)
                            V.tensor_copy(pT[0:TK, 2 * i, :], T2[0:TK, 0, :]).then_inc(s["t_dve"], 1)
                            dve.wait_ge(s["pv_ready"], 2 * c + i + 1)
                            V.tensor_tensor(acc, O2[:, i, 0:D], acc, ALU.add).then_inc(s["pv_taken"], 1)
                            dve.wait_ge(s["pv_taken"], 2 * c + i + 1)

                    attend(0, True)
                    with dve.Fori(1, NC) as c:
                        attend(c, False)
                    dve.wait_ge(s["p_ready"], 2 * NC)
                    need(dve, "act", f"{layer}.bat")
                    V.tensor_copy(work[:, 512:512 + D], xn[:, :])
                    V.memset(work[:, 512 + D:512 + D + 1], 1.0)
                    done("dve", V.tensor_copy(mats3[:, 0, :], bat.to_broadcast([P, P])), f"{layer}.bat")
                    f = [arena[:, k * D:(k + 1) * D] for k in range(3)]
                    link(V.tensor_reduce(rec, sums, X, ALU.add))
                    link(V.reciprocal(rec, rec))
                    link(V.tensor_scalar(f[0], acc, rec, None, ALU.mult))
                    link(V.tensor_tensor(f[1], xn[:, :], f[0], ALU.mult))
                    need(dve, "pe", f"{layer}.hc_ps")
                    link(V.reciprocal(rec, O2[:, 0, D:D + 1]))
                    link(V.tensor_scalar(f[2], O2[:, 0, 0:D], rec, None, ALU.mult))
                    done("dve", V.tensor_tensor(f[2], f[2], xn[:, :], ALU.mult), f"{layer}.f")
                    need(dve, "pe", f"{layer}.fT_ps")
                    done("dve", V.tensor_copy(arena[:, 1024:1024 + 768], S4f[:, 0:768]), f"{layer}.fT")
                    need(dve, "pe", f"{layer}.out")
                    residual(layer, O2[:, 1, 0:D])


def blocks(w):
    k = w.shape[0] // P
    return w.reshape(k, P, w.shape[1]).transpose(1, 0, 2).reshape(P, k * w.shape[1])


def rows(*vs):
    return [np.broadcast_to(np.reshape(v, (1, -1)), (P, np.size(v))) for v in vs]


def pack(*parts):
    return np.ascontiguousarray(np.concatenate(parts, axis=1))


def constants():
    i = np.arange(P)
    e = np.arange(E)
    parts = [np.eye(P), i[:, None] <= i[None, :], np.where(i[None, :] <= i[:, None], 0.0, -MASKED),
             np.maximum(i[None, :] - i[:, None], 0), (i[:, None] // DH) == np.arange(HH)[None, :],
             (i[:, None] % QR // DH) == np.arange(2)[None, :],
             np.broadcast_to((e[None, :] < e[:, None]).reshape(1, -1), (P, E * E))]
    return np.ascontiguousarray(np.concatenate([np.asarray(p, np.float32) for p in parts], axis=1))


def layout(i):
    c = i["ctx_1024"][0]
    L0W = i["L0_xattn_W"]
    out = {
        "x": i["x"][0],
        "consts": constants(),
        "ctx_cols": c.reshape(2 * NC, HC, KD, P).transpose(0, 3, 2, 1),
        "ctx_rows": c.reshape(2 * NC, TH, TK, D).transpose(0, 2, 1, 3).reshape(2 * NC, TK, TH * D),
        "mask_L2x": i["mask_SxS2_ik0"].reshape(P, NC, CH).transpose(1, 0, 2),
        "mask_L3x": i["mask_BxSxS2_ff0"][0].reshape(P, NC, CH).transpose(1, 0, 2),
        "fc1_q": blocks(i["L1_ffn_fc1_q"]),
        "fc2_q": blocks(i["L1_ffn_fc2_q"]),
        "fc1_scales": pack(*rows(i["L1_ffn_fc1_scales"])),
        "fc2_scales": pack(*rows(i["L1_ffn_fc2_scales"])),
        "pack_L0x": pack(blocks(L0W[:, :D].T), blocks(L0W[:, D:].T), *rows(i["L0_xattn_b"])),
        "pack_L0a": pack(blocks(i["L0_attn_W_qkv"]), blocks(i["L0_attn_W_gate"]), blocks(i["L0_attn_W_proj"]),
                         *rows(i["L0_attn_ln_g"], i["L0_attn_ln_b"], i["L0_attn_b_qkv"], i["L0_attn_b_gate"],
                               i["L0_attn_b_proj"])),
        "pack_L0f": pack(blocks(i["L0_ffn_Wg"].T)),
        "pack_L1x": pack(blocks(i["L1_xattn_W_qv"]),
                         *rows(i["L1_xattn_w_sim"], i["L1_xattn_b_sim"], i["L1_xattn_b_qv"])),
        "pack_L1a": pack(blocks(np.concatenate([i["L1_attn_Wq"].T, i["L1_attn_Wk"].T, i["L1_attn_Wv"].T], axis=1)),
                         blocks(i["L1_attn_Wu"].T),
                         *rows(np.tile(i["L1_attn_qln_w"], H), np.tile(i["L1_attn_kln_w"], H),
                               np.tile(i["L1_attn_qln_b"], H), np.tile(i["L1_attn_kln_b"], H))),
        "pack_L1f": pack(*rows(i["L1_ffn_ln_gamma"], i["L1_ffn_ln_beta"], i["L1_ffn_fc1_bias"], i["L1_ffn_fc2_bias"])),
        "pack_L2x": pack(*[blocks(i[f"L2_xattn_W{n}"].T) for n in "qkvo"], *rows(i["L2_xattn_bq"]),
                         i["L2_xattn_bk"].reshape(KD, P).T, *rows(i["L2_xattn_bv"], i["L2_xattn_bo"])),
        "pack_L2a": pack(blocks(np.concatenate([i[f"L2_attn_W{n}"].T for n in "qkv"], axis=1)),
                         blocks(i["L2_attn_Wo"].T)),
        "pack_L2f": pack(blocks(i["L2_ffn_gate_w"].T), *rows(i["L2_ffn_expert_bias"])),
        "pack_L3x": pack(*[blocks(i[f"L3_xattn_W{n}"]) for n in "qkvo"]),
        "pack_L3a": pack(blocks(i["L3_attn_o_w"].T), *rows(i["L3_attn_q"], i["L3_attn_k"], i["L3_attn_log_decay"],
                                                          i["L3_attn_norm_weight"])),
        "pack_L3f": pack(blocks(i["L3_ffn_gate_w"].T)),
    }
    ups = {"L0f": ["L0_ffn_W1", "L0_ffn_W2"], "L2f": ["L2_ffn_w_up"], "L3f": ["L3_ffn_wi_gate", "L3_ffn_wi_up"]}
    downs = {"L0f": "L0_ffn_W3", "L2f": "L2_ffn_w_down", "L3f": "L3_ffn_wo"}
    for layer, names in ups.items():
        F = FF[layer]
        out[f"up_{layer}"] = np.concatenate(
            [i[n].reshape(E, F, KD, P).transpose(0, 3, 2, 1).reshape(E, P, KD * F) for n in names], axis=2)
        out[f"down_{layer}"] = i[downs[layer]].reshape(E, D, E, F // E).transpose(0, 3, 2, 1).reshape(E, F // E, E * D)
    return {k: np.ascontiguousarray(v) for k, v in out.items()}


def kernel(**inputs):
    import concourse.bacc as bacc
    from concourse.bass_utils import run_bass_kernel_spmd

    arrays = layout({k: np.asarray(v) for k, v in inputs.items()})
    nc = bacc.Bacc("TRN2", target_bir_lowering=False, num_devices=1)
    args = {k: nc.dram_tensor(f"in_{k}", v.shape, mybir.dt.from_np(v.dtype), kind="ExternalInput").ap()
            for k, v in arrays.items()}
    args["out"] = nc.dram_tensor("out_x", (P, D), F32, kind="ExternalOutput").ap()
    build(nc, args)
    r = run_bass_kernel_spmd(nc, [{f"in_{k}": v for k, v in arrays.items()}], core_ids=[0])
    return r.results[0]["out_x"].reshape(1, P, D)
```

```python
from contextlib import ExitStack

import numpy as np

import concourse.bass as bass
import concourse.mybir as mybir

F32 = mybir.dt.float32
F32R = mybir.dt.float32r
I32 = mybir.dt.int32
ALU = mybir.AluOpType
ACT = mybir.ActivationFunctionType
X = mybir.AxisListType.X

P = 128
D = 256
KD = D // P
H = 16
DH = D // H
HH = H // KD
QR = 32
NP = H // 2
NK = 12544
TK = 112
HC = 896
CH = 2 * HC
NC = NK // CH
TC = CH // TK
TH = HC // TK
BANK = 512
E = 8
BIG = 3.0e38
MASKED = 1.0e30
CAPACITY = int(P / E * 1.25)

LAYERS = ["L0x", "L0a", "L0f", "L1x", "L1a", "L1f", "L2x", "L2a", "L2f", "L3x", "L3a", "L3f"]
FF = {"L0f": 704, "L2f": 1024, "L3f": 1024}
GATED = ("L0f", "L3f")

PACKS = {
    "L0x": dict(w1=512, w2=512, b=256),
    "L0a": dict(qkv=1536, gate=512, proj=512, ln_g=256, ln_b=256, b_qkv=768, b_gate=256, b_out=256),
    "L0f": dict(gate=16),
    "L1x": dict(w_qv=2048, w_sim=768, b_sim=1, b_out=256),
    "L1a": dict(qkv=1536, proj=512, ln_w=512, ln_b=512),
    "L1f": dict(ln_g=256, ln_b=256, b1=1024, b2=256),
    "L2x": dict(wq=512, wk=512, wv=512, proj=512, bq=256, bk=2, bv=256, b_out=256),
    "L2a": dict(qkv=1536, proj=512),
    "L2f": dict(gate=16, bias=8),
    "L3x": dict(wq=512, wk=512, wv=512, proj=512),
    "L3a": dict(proj=512, q=256, k=256, log_decay=16, norm=256),
    "L3f": dict(gate=16),
}
CONSTS = dict(ident=128, causal=128, causal_bias=128, steps=128, head=8, pair=2, before=64)

NORM = {"dve": ["var", "xn", "xT"], "pool": ["rstd"], "pe": ["xnT"], "act": []}
NORM2 = {"dve": ["var2", "x2", "x2T"], "pool": ["rstd2"], "pe": ["x2T_ps"], "act": []}
TAIL = {"dve": ["o", "oT"], "pool": [], "pe": ["oT_ps", "out"], "act": []}


def stage_lists(layers):
    lists = {e: [] for e in ("pe", "dve", "act", "pool")}

    def add(layer, **stages):
        for e, names in stages.items():
            lists[e] += [f"{layer}.{n}" for n in names]

    for layer in layers:
        add(layer, **NORM)
        if layer == "L0x":
            add(layer, dve=["mean"], pe=["out"])
        elif layer == "L0a":
            add(layer, **NORM2)
            add(layer, pe=["gate_ps", "qkv_ps", "qkT_ps", "A_ps", "num_ps"],
                dve=["g", "qk", "qblk", "AT"], act=["sig"])
            add(layer, **TAIL)
        elif layer == "L2a":
            add(layer, pe=["qkv_ps", "qkT_ps", "A_ps", "num_ps"], dve=["neg", "qk", "qblk", "AT"], act=["elu"])
            add(layer, **TAIL)
        elif layer == "L1a":
            add(layer, pe=["qkv_ps", "qkT_ps", "S_ps", "pT_ps", "num_ps"],
                dve=["var2", "qk", "kblk", "sm", "pT"], act=["p"], pool=["rstd2"])
            add(layer, **TAIL)
        elif layer == "L3a":
            add(layer, pe=["num_ps"], dve=["abs", "onep", "ln", "V", "var2"], act=["e", "ln1p", "decay"],
                pool=["rstd2"])
            add(layer, **TAIL)
        elif layer == "L1x":
            add(layer, dve=["A", "AT", "max", "bat", "f", "fT"], pe=["AT_ps", "hc_ps", "fT_ps", "out"],
                pool=["gmax"], act=["bat"])
        elif layer == "L1f":
            add(layer, **NORM2)
            add(layer, pe=["z_ps", "yT_ps", "out"], dve=["w", "z", "yT"], act=["y"])
        elif layer in ("L2x", "L3x"):
            add(layer, pe=["q_ps", "qT_ps"], dve=["q", "q4"])
            add(layer, **TAIL)
        elif layer == "L0f":
            add(layer, pe=["logit"], dve=["weights"])
        elif layer == "L2f":
            add(layer, pe=["logit"], dve=["logit", "weights", "var3"], act=["prob"], pool=["rstd3"])
        elif layer == "L3f":
            add(layer, pe=["logit", "pos"], dve=["logit", "onehot", "weights"], act=["prob"])
        add(layer, dve=["end"])
    return lists


def unit_groups():
    seq = []
    for h in range(H):
        if h % 4 == 1 and h > 1:
            seq.append(("O", (h - 5) // 4, 0, "dve"))
        seq += [("T", h, g, "act" if g % 2 == 0 else "dve") for g in range(4)]
    seq.append(("O", 3, 0, "dve"))
    return seq


GROUPS = unit_groups()
GROUP_AT = {g[:3]: n for n, g in enumerate(GROUPS)}
TAKEN = {e: [sum(g[3] == e for g in GROUPS[:n + 1]) for n in range(len(GROUPS))] for e in ("act", "dve")}
NG = len(GROUPS)
KEYS_AT = (3, 9)
VALUE_BANK = (1, 0, 0, 1, 0, 1, 0, 1)


def build(nc, a, layers=LAYERS):
    ctx = ExitStack()
    with ctx:
        def sb(name, shape, dt=F32):
            return ctx.enter_context(nc.sbuf_tensor(name, shape, dt))

        def sem(name):
            return ctx.enter_context(nc.semaphore(name))

        S4 = ctx.enter_context(nc.psum_tensor("S4", [P, 4, BANK], F32))
        T2 = ctx.enter_context(nc.psum_tensor("T2", [P, 2, BANK], F32))
        O2 = ctx.enter_context(nc.psum_tensor("O2", [P, 2, BANK], F32))
        S4f = S4[:, :, :].rearrange("p b n -> p (b n)")

        x = sb("x", [P, D])
        xn = sb("xn", [P, D])
        x2 = sb("x2", [P, D])
        xT = sb("xT", [P, KD, P])
        x2T = sb("x2T", [P, KD, P])
        consts = sb("consts", [P, sum(CONSTS.values())])
        slots = [max(sum(PACKS[n].values()) for n in LAYERS[i::2]) for i in range(2)]
        packs = [sb(f"packs{i}", [P, slots[i]]) for i in range(2)]
        arena_at = nc.sbuf_base
        arena = sb("arena", [P, NK])
        ctx_in = sb("ctx_in", [P, 2, KD, HC])
        sc = sb("sc", [P, 3, CH])
        pT = sb("pT", [P, 4, BANK])
        o_sb = sb("o_sb", [P, 2, BANK])
        mask_bias = sb("mask_bias", [P, CH])
        wide_at = nc.sbuf_base
        wide = sb("wide", [P, NP * CH])
        fb = wide[:, 0:2 * 3 * KD * 1024].rearrange("p (b n) -> p b n", b=2)
        work = sb("work", [P, 1536])
        small = sb("small", [P, 512])

        vv = arena[0:TK, KD * CH:KD * CH + TC * D].rearrange("p (t d) -> p t d", t=TC)
        at = KD * CH + TC * D
        blk = arena[:, at:at + H * P].rearrange("p (h n) -> p h n", h=H)
        mask_in = arena[:, at + H * P:at + H * P + CH]
        keys_hl = nc.alloc_sbuf_tensor_at("keys_hl", [P, 2, CH], F32R, offset=arena_at)
        keys4 = nc.alloc_sbuf_tensor_at("keys4", [P, NP, CH], F32R, offset=wide_at)
        q4 = nc.alloc_sbuf_tensor_at("q4", [P, H, P], F32R, offset=arena_at + 4 * at)
        q_up = nc.alloc_sbuf_tensor_at("q_up", [P, NP * P], F32R, offset=arena_at + 4 * (at + H * P + CH))
        q_low = arena[:, at + H * P + CH:at + H * P + CH + NP * P]
        assert at + H * P + CH + NP * P <= NK
        mats = sc[:, :, :].rearrange("p a n -> p (a n)")[:, 0:H * P]
        mats3 = mats.rearrange("p (h n) -> p h n", h=H)
        matsT = arena[:, 0:H * P]
        matsT3 = matsT.rearrange("p (h n) -> p h n", h=H)
        oT = arena[:, 2048:2048 + D].rearrange("p (k n) -> p k n", k=KD)
        halfT = arena[:, 2304:2304 + D].rearrange("p (k n) -> p k n", k=KD)
        vaug = arena[:, 2560:2560 + H * (DH + 1)].rearrange("p (h n) -> p h n", h=H)
        num = arena[:, 2832:2832 + H * (DH + 1)].rearrange("p (h n) -> p h n", h=H)
        hid = arena[:, 0:1024]
        hidT = arena[:, 1024:2048].rearrange("p (t n) -> p t n", t=E)
        gated = arena[:, 3200:4224]
        yacc = arena[:, 4224:4480]

        at = 0
        C = {}
        for name, w in CONSTS.items():
            C[name] = consts[:, at:at + w]
            at += w
        ident = C["ident"]

        def pk(layer, name, k=None):
            at = 0
            for n, w in PACKS[layer].items():
                if n == name:
                    break
                at += w
            piece = packs[LAYERS.index(layer) % 2][:, at:at + w]
            return piece.rearrange("p (k n) -> p k n", k=k) if k else piece

        def half_in(q):
            return ctx_in[:, q] if q < 2 else sc[:, q - 2, :].rearrange("p (k n) -> p k n", k=KD)

        cols = [0]

        def take(w):
            cols[0] += w
            assert cols[0] <= 512
            return small[:, cols[0] - w:cols[0]]

        stats, mv, rstd, half = take(6), take(2), take(1), take(64)
        vsum, head_a, head_b, lam = take(32), take(32), take(32), take(16)
        n_old, n_half, n_new, l_new = take(16), take(16), take(16), take(16)
        alpha, l_sum, wts, wcur = take(16), take(16), take(8), take(2)
        maxes, sums, row, row_max = take(14), take(14), take(1), take(1)
        gmax, bat, rec, prob = take(1), take(1), take(1), take(8)
        rank, one0, one1 = take(8), take(8), take(8)
        eye_a, mean, tick = take(64), take(2), take(1)
        parts4 = sb("parts", [P, NC, 2, KD])
        oc = work[:, 0:256]
        acc = work[:, 256:512]

        minus_half = sb("minus_half", [P, 2 * H])
        filled = sem("minus_half_filled")

        STAGES = stage_lists(layers)
        stages = {e: sem(f"{e}_stages") for e in STAGES}
        counted = {e: 0 for e in STAGES}

        def done(e, ins, name):
            assert STAGES[e][counted[e]] == name, (e, name, STAGES[e][counted[e]])
            counted[e] += 1
            ins.then_inc(stages[e], 1)

        def need(eng, e, name):
            eng.wait_ge(stages[e], STAGES[e].index(name) + 1)

        consts_in = sem("consts_in")
        x_in = sem("x_in")
        pack_in = [sem(f"pack{n}_in") for n in range(2)]
        stored = sem("stored")
        own = {e: sem(f"{e}_own") for e in ("dve", "act")}
        owned = {"dve": 0, "act": 0}

        def packed(eng, layer):
            eng.wait_ge(pack_in[LAYERS.index(layer) % 2], 16 * (layers.index(layer) // 2 + 1))

        L = {}

        def sems(layer, *names):
            L[layer] = {n: sem(f"{layer}_{n}") for n in names}

        for layer in layers:
            if layer == "L0x":
                sems(layer, "ctx_in0", "ctx_in1", "ctx_in2", "summed")
            elif layer == "L1x":
                sems(layer, "ctx_in0", "ctx_in1", "ctx_in2", "ctx_in3", "s_ready", "s_taken", "p_ready", "nat_in0", "nat_in1", "t_ready", "t_dve", "t_act",
                     "pv_ready", "pv_taken")
            elif layer in ("L2x", "L3x"):
                sems(layer, "ctx_in0", "ctx_in1", "mask_in", "mask_taken", "kp_ready", "up_taken", "low_taken",
                     "acc_taken", "half_read", "keys_in0", "keys_in1", "vp_ready", "vp_taken",
                     "s_ready", "s_taken", "p_ready", "t_ready", "t_dve", "t_act", "pv_done", "o_taken",
                     "delta", "alpha", "finished")
            elif layer == "L1f":
                sems(layer, "q_in")
            elif layer in FF:
                sems(layer, "up_in0", "up_in1", "down_in0", "down_in1", "picked", "g_ready", "act_done", "h_ready", "t_ready", "t_dve", "t_act", "y_ready",
                     "y_taken")

        block = ctx.enter_context(nc.Block())

        @block.sync
        def _(sp):
            def load_pack(layer):
                n = layers.index(layer)
                if n >= 2:
                    need(sp, "dve", f"{layers[n - 2]}.end")
                w = sum(PACKS[layer].values())
                slot = LAYERS.index(layer) % 2
                sp.dma_start(packs[slot][:, 0:w], a[f"pack_{layer}"]).then_inc(pack_in[slot], 16)

            sp.dma_start(x[:, :], a["x"]).then_inc(x_in, 16)
            sp.dma_start(consts[:, :], a["consts"]).then_inc(consts_in, 16)
            for layer in layers[:2]:
                load_pack(layer)

            def load_ctx(s, n, half):
                sp.dma_start(ctx_in[:, half], a["ctx_cols"][bass.ds(n, 1)].rearrange(
                    "a p k n -> p (a k) n")).then_inc(s, 16)

            def load_up(layer, e, b):
                m = KD * (2 if layer in GATED else 1) * FF[layer]
                sp.dma_start(fb[:, b, 0:m], a[f"up_{layer}"][bass.ds(e, 1)].rearrange(
                    "a p n -> p (a n)")).then_inc(L[layer][f"up_in{b}"], 16)

            def load_down(layer, e, b):
                F = FF[layer]
                m = KD * (2 if layer in GATED else 1) * F
                sp.dma_start(fb[0:F // E, b, m:m + E * D], a[f"down_{layer}"][bass.ds(e, 1)].rearrange(
                    "a p n -> p (a n)")).then_inc(L[layer][f"down_in{b}"], 16)

            def load_first(layer):
                for e in range(2):
                    load_up(layer, e, e)
                    load_down(layer, e, e)

            def load_quantised(layer):
                for b in range(2):
                    sp.dma_start(fb[:, b, 0:2048].bitcast(I32), a[f"fc{b + 1}_q"]).then_inc(L[layer]["q_in"], 16)
                    sp.dma_start(fb[:, b, 2048:4096], a[f"fc{b + 1}_scales"]).then_inc(L[layer]["q_in"], 16)

            for i, layer in enumerate(layers):
                prev = layers[i - 1] if i else None
                if layer == "L0x":
                    s = L[layer]
                    bufs = [ctx_in[:, :, :, :].rearrange("p h k n -> p (h k n)"),
                            sc[:, 0:2, :].rearrange("p a n -> p (a n)"), arena[:, 0:KD * CH]]
                    for c in range(NC):
                        if c >= 3:
                            sp.wait_ge(s["summed"], c - 2)
                        for half in range(2):
                            dst = bufs[c % 3].rearrange("p (h n) -> p h n", h=2)[:, half]
                            sp.dma_start(dst, a["ctx_cols"][2 * c + half].rearrange("p k n -> p (k n)")) \
                                .then_inc(s[f"ctx_in{c % 3}"], 16)
                elif layer == "L1x":
                    s = L[layer]

                    def load_half(n, q):
                        if q < 2:
                            load_ctx(s[f"ctx_in{q}"], n, q)
                        else:
                            sp.dma_start(half_in(q), a["ctx_cols"][bass.ds(n, 1)].rearrange(
                                "a p k n -> p (a k) n")).then_inc(s[f"ctx_in{q}"], 16)

                    for q in range(4):
                        if q == 2 and prev:
                            need(sp, "dve", f"{prev}.end")
                        load_half(q, q)
                    with sp.Fori(1, NC // 2) as n:
                        for q in range(4):
                            sp.wait_ge(s["s_ready"], 4 * n + (q - 3))
                            load_half(4 * n + q, q)
                    for q in range(2):
                        sp.wait_ge(s["s_ready"], 2 * NC - 5 + q)
                        load_half(2 * NC - 2 + q, q)
                    def load_nat(n, half):
                        sp.dma_start(fb[0:TK, half, 0:TH * D], a["ctx_rows"][bass.ds(n, 1)].rearrange(
                            "a p n -> p (a n)")).then_inc(s[f"nat_in{half}"], 16)
                    for half in range(2):
                        load_nat(half, half)
                    with sp.Fori(1, NC) as c:
                        for half in range(2):
                            sp.wait_ge(s["pv_ready"], 2 * c - 1 + half)
                            load_nat(2 * c + half, half)
                elif layer in ("L2x", "L3x"):
                    s = L[layer]

                    def load_mask(c):
                        dst = mask_in.bitcast(I32) if layer == "L2x" else mask_in
                        sp.dma_start(dst, a[f"mask_{layer}"][bass.ds(c, 1)].rearrange("a p n -> p (a n)")) \
                            .then_inc(s["mask_in"], 16)

                    for half in range(2):
                        load_ctx(s[f"ctx_in{half}"], half, half)
                    if prev:
                        need(sp, "dve", f"{prev}.end")
                    load_mask(0)
                    if i + 1 < len(layers):
                        load_pack(layers[i + 1])

                    def load_keys(c, hf, before=None):
                        sp.wait_ge(s["low_taken"], 8 * c + 4 * (hf + 1))
                        if before is not None:
                            sp.wait_ge(s["delta" if hf else "half_read"], before)
                        for j in range(HH // 2):
                            for r in range(4):
                                sp.dma_start(keys4[QR * r:QR * (r + 1), hf * HH // 2 + j, :].bitcast(F32),
                                             keys_hl[QR * j:QR * (j + 1), r % 2, :].bitcast(F32)) \
                                    .then_inc(s[f"keys_in{hf}"], 16)

                    for hf in range(KD):
                        load_keys(0, hf)
                    with sp.Fori(1, NC) as c:
                        sp.wait_ge(s["mask_taken"], c)
                        load_mask(c)
                        sp.wait_ge(s["vp_ready"], 8 * c)
                        for half in range(2):
                            load_ctx(s[f"ctx_in{half}"], 2 * c + half, half)
                        for hf in range(KD):
                            load_keys(c, hf, c)
                elif layer == "L1f" and i == 0:
                    load_quantised(layer)
                elif layer in FF:
                    s = L[layer]
                    per = 2 if layer in GATED else 1
                    if i == 0:
                        load_first(layer)
                    with sp.Fori(1, E // 2) as n:
                        for b in range(2):
                            sp.wait_ge(s["g_ready"], 2 * per * n + per * (b - 1))
                            load_up(layer, 2 * n + b, b)
                            sp.wait_ge(s["y_ready"], 2 * n + (b - 1))
                            load_down(layer, 2 * n + b, b)
                if i + 1 < len(layers) and (layers[i + 1] in FF or layers[i + 1] == "L1f"):
                    if prev:
                        need(sp, "dve", f"{prev}.end")
                    (load_first if layers[i + 1] in FF else load_quantised)(layers[i + 1])
                if i + 2 < len(layers) and layers[i + 1] not in ("L2x", "L3x"):
                    load_pack(layers[i + 2])

            need(sp, "dve", f"{layers[-1]}.end")
            sp.dma_start(a["out"], x[:, :]).then_inc(stored, 16)
            sp.wait_ge(stored, 16)

        @block.gpsimd
        def _(pool):
            def power(layer, stage, of, t, out):
                need(pool, "dve", f"{layer}.{of}")
                done("pool", nc.gpsimd.tensor_tensor(out, t, minus_half[:, 0:t.shape[1]], ALU.pow), f"{layer}.{stage}")

            nc.gpsimd.memset(minus_half[:, :], -0.5).then_inc(filled, 1)
            pool.wait_ge(filled, 1)
            for layer in layers:
                power(layer, "rstd", "var", mv[:, 1:2], rstd)
                if layer in ("L0a", "L1f"):
                    power(layer, "rstd2", "var2", mv[:, 1:2], rstd)
                elif layer == "L1a":
                    power(layer, "rstd2", "var2", head_a, head_b)
                elif layer == "L3a":
                    power(layer, "rstd2", "var2", mv[:, 1:2], rstd)
                elif layer == "L2f":
                    power(layer, "rstd3", "var3", mv[:, 1:2], rstd)
                elif layer == "L1x":
                    need(pool, "dve", f"{layer}.max")
                    done("pool", nc.gpsimd.partition_all_reduce(gmax, row_max, P, bass.bass_isa.ReduceOp.max),
                         f"{layer}.gmax")

        @block.tensor
        def _(pe):
            mm = nc.tensor.matmul

            def transposes(out, src, n, w=P):
                for t in range(n):
                    last = nc.tensor.transpose(out[0:w, t * P:(t + 1) * P], src[:, t * w:(t + 1) * w], ident)
                return last

            def product(out, lhsT, rhs, n=KD):
                for k in range(n):
                    last = mm(out, lhsT[:, k, :], rhs[:, k, :], start=(k == 0), stop=(k == n - 1))
                return last

            def norm(layer):
                need(pe, "dve", f"{layer}.xn")
                done("pe", transposes(T2[:, 0], xn, KD), f"{layer}.xnT")

            def norm2(layer):
                need(pe, "dve", f"{layer}.x2")
                done("pe", transposes(T2[:, 1], x2, KD), f"{layer}.x2T_ps")

            def tail(layer):
                need(pe, "dve", f"{layer}.o")
                done("pe", transposes(T2[:, 1], x2, KD), f"{layer}.oT_ps")
                need(pe, "dve", f"{layer}.oT")
                done("pe", product(O2[:, 0, 0:D], oT, pk(layer, "proj", KD)), f"{layer}.out")

            def qkv(layer, src):
                w = pk(layer, "qkv", KD)
                product(S4[:, 0], src, w[:, :, 0:2 * D])
                done("pe", product(S4[:, 1, 0:D], src, w[:, :, 2 * D:3 * D]), f"{layer}.qkv_ps")
                need(pe, "dve", f"{layer}.qk")
                done("pe", transposes(T2[:, 0], work, 2 * KD), f"{layer}.qkT_ps")

            def heads_products(stat, rhs):
                for b in range(4):
                    last = mm(S4[:, b], stat[:, b // 2, :], rhs[:, 4 * b:4 * b + 4, :], start=True, stop=True)
                return last

            def cross(layer):
                s = L[layer]
                wq, wk, wv = (pk(layer, n, KD) for n in ("wq", "wk", "wv"))
                def key_block(n):
                    hf, nb = divmod(n, 4)
                    for k in range(KD):
                        last = mm(S4[:, n % 4, 0:HC // 2], wk[:, k, hf * P:(hf + 1) * P],
                                  ctx_in[:, nb // 2, k, (nb % 2) * (HC // 2):(nb % 2 + 1) * (HC // 2)],
                                  start=(k == 0), stop=(k == KD - 1))
                    last.then_inc(s["kp_ready"], 1)

                def keys_ahead(c, hf):
                    for half in range(2):
                        pe.wait_ge(s["s_taken"], 32 * c + (2 * KEYS_AT[hf] + 3 + half))
                        for n in (2 * half, 2 * half + 1):
                            key_block(4 * hf + n)

                def scores(c, h, keys_too=False):
                    if h % HH == 0:
                        pe.wait_ge(s[f"keys_in{h // HH % KD}"], 256 * c + 256 * (h // H + 1))
                    for half in range(2):
                        if h:
                            pe.wait_ge(s["s_taken"], 32 * c + (2 * h - 1 + half))
                        if h - 2 in KEYS_AT and keys_too:
                            pe.wait_ge(s["low_taken"], 8 * c + (8 + 4 * KEYS_AT.index(h - 2) + 2 * half + 2))
                        for n0, n1 in ((0, BANK), (BANK, HC)):
                            last = mm(S4f[:, half * 2 * BANK + n0:half * 2 * BANK + n1], q4[:, h % H, :],
                                      keys4[:, h % H // 2, half * HC + n0:half * HC + n1], start=True, stop=True)
                        last.then_inc(s["s_ready"], 1)

                def value_block(c, b, of=None):
                    if of is not None and b in (0, 1, 3):
                        n = {0: NG - 3, 1: NG - 2, 3: NG - 1}[b]
                        e = GROUPS[n][3]
                        pe.wait_ge(s[f"t_{e}"], TAKEN[e][-1] * of + TAKEN[e][n])
                    elif b >= 2:
                        pe.wait_ge(s["vp_taken"], 8 * c + {2: 2, 3: 1}.get(b, b - 1))
                    for t in (2 * b, 2 * b + 1):
                        for k in range(KD):
                            last = mm(T2[0:TK, VALUE_BANK[b], (t % 2) * D:(t % 2 + 1) * D],
                                      ctx_in[:, t // TH, k, (t % TH) * TK:(t % TH + 1) * TK], wv[:, k, :],
                                      start=(k == 0), stop=(k == KD - 1))
                    last.then_inc(s["vp_ready"], 1)

                for half in range(2):
                    pe.wait_ge(s[f"ctx_in{half}"], 16)
                for n in range(4):
                    key_block(n)
                need(pe, "dve", f"{layer}.xT")
                done("pe", product(O2[:, 0, 0:D], xT, wq), f"{layer}.q_ps")
                need(pe, "dve", f"{layer}.q")
                pe.wait_ge(s["low_taken"], 4)
                for half in range(2):
                    last = transposes(S4[:, half], work[:, BANK * (half + 1):BANK * (half + 2)], 4)
                done("pe", last, f"{layer}.qT_ps")
                for b in range(4):
                    value_block(0, b)
                need(pe, "dve", f"{layer}.q4")
                for n in range(4, 8):
                    key_block(n)
                value_block(0, 4)
                pe.wait_ge(s["low_taken"], 8)
                for h in range(3):
                    scores(0, h)
                    value_block(0, h + 5)

                def chunk(c, last_chunk):
                    def values(h, g):
                        e = GROUPS[GROUP_AT["T", h, g]][3]
                        pe.wait_ge(s[f"t_{e}"], TAKEN[e][-1] * c + TAKEN[e][GROUP_AT["T", h, g]])
                        quad = h // 4
                        if h % 4 == 0 and g == 0 and quad >= 2:
                            pe.wait_ge(s["o_taken"], 4 * c + (quad - 1))
                        for i in range(4):
                            last = mm(O2[32 * i:32 * i + 32, quad % 2, (h % 4) * P:(h % 4 + 1) * P],
                                      vv[:, 4 * g + i, (h // 2) * 32:(h // 2 + 1) * 32],
                                      pT[0:TK, g, i * P:(i + 1) * P], start=(g == 0), stop=(g == 3))
                        last.then_inc(s["pv_done"], 1)

                    waiting = []
                    for n, (kind, h, g, _) in enumerate(GROUPS):
                        if kind == "T" and g == 0 and h in KEYS_AT and not last_chunk:
                            hf = KEYS_AT.index(h)
                            if hf == 0:
                                for half in range(2):
                                    pe.wait_ge(s[f"ctx_in{half}"], 16 * c + 32)
                            keys_ahead(c, hf)
                        if kind == "T" and g == (2 if h in KEYS_AT else 0):
                            if 0 < h < H - 2:
                                scores(c, h + 2, not last_chunk)
                            elif h == H - 1 and not last_chunk:
                                scores(c, H)
                        if kind == "T" and g == 0:
                            pe.wait_ge(s["p_ready"], 16 * c + (h + 1))
                        if n == NG - 1:
                            if not last_chunk:
                                value_block(c + 1, 0, c)
                            for group in waiting:
                                values(*group)
                            waiting = []
                            if not last_chunk:
                                value_block(c + 1, 1, c)
                                scores(c, H + 1)
                        if kind == "O":
                            pe.wait_ge(s["o_taken"], 4 * c + (h + 1))
                        if n == NG - 1 and not last_chunk:
                            pe.wait_ge(s["vp_taken"], 8 * c + 9)
                        elif n >= 2:
                            e = GROUPS[n - 2][3]
                            pe.wait_ge(s[f"t_{e}"], TAKEN[e][-1] * c + TAKEN[e][n - 2])
                        else:
                            pe.wait_ge(s["vp_taken"], 8 * c + (n + 7))
                        if kind == "T":
                            last = transposes(T2[:, n % 2], sc[:, h % 3, 4 * g * TK:(4 * g + 4) * TK], 4, TK)
                        else:
                            last = transposes(T2[:, n % 2], o_sb[:, h % 2], 4)
                        last.then_inc(s["t_ready"], 1)
                        if kind == "T":
                            waiting.append((h, g))
                        if len(waiting) > 2:
                            values(*waiting.pop(0))
                    if not last_chunk:
                        for b in range(2, 8):
                            value_block(c + 1, b, c)
                            if b == 3:
                                scores(c, H + 2)

                with pe.Fori(0, NC - 1) as c:
                    chunk(c, False)
                chunk(NC - 1, True)
                tail(layer)

            def experts(layer):
                s = L[layer]
                F = FF[layer]
                m = KD * F
                per = 2 if layer in GATED else 1

                def down(e, b, n):
                    w = fb[0:F // E, b, per * m:][:, 0:E * D].rearrange("p (t n) -> p t n", t=E)
                    pe.wait_ge(s[f"down_in{b}"], 16 * n + 16)
                    pe.wait_ge(s["t_dve"], e + 1)
                    pe.wait_ge(s["t_act"], e + 1)
                    for t in range(E):
                        last = mm(O2[:, b, 0:D], hidT[0:F // E, t, :], w[:, t, :], start=(t == 0), stop=(t == E - 1))
                    last.then_inc(s["y_ready"], 1)

                def expert(e, b, n, first=False):
                    pe.wait_ge(s[f"up_in{b}"], 16 * n + 16)
                    for j in range(per):
                        w = fb[:, b, j * m:(j + 1) * m].rearrange("p (k n) -> p k n", k=KD)
                        for i in range(2):
                            last = product(S4[:, 2 * j + i, 0:F // 2], xT, w[:, :, i * F // 2:(i + 1) * F // 2])
                        last.then_inc(s["g_ready"], 1)
                    if not first:
                        down(e - 1, 1 - b, n - (1 - b))
                    pe.wait_ge(s["h_ready"], e + 1)
                    for j in range(2):
                        last = transposes(T2[:, j], hid[:, j * F // 2:(j + 1) * F // 2], 4, F // E)
                        last.then_inc(s["t_ready"], 1)

                expert(0, 0, 0, True)
                expert(1, 1, 0)
                with pe.Fori(1, E // 2) as n:
                    for b in range(2):
                        expert(2 * n + b, b, n)
                down(E - 1, 1, E // 2 - 1)

            pe.wait_ge(consts_in, 16)
            for layer in layers:
                norm(layer)
                packed(pe, layer)
                if layer == "L0x":
                    need(pe, "dve", f"{layer}.xT")
                    for k in range(KD):
                        mm(O2[:, 0, 0:D], xT[:, k, :], pk(layer, "w1", KD)[:, k, :], start=(k == 0), stop=False)
                    need(pe, "dve", f"{layer}.mean")
                    for k in range(KD):
                        last = mm(O2[:, 0, 0:D], x2T[:, k, :], pk(layer, "w2", KD)[:, k, :], start=False,
                                  stop=(k == KD - 1))
                    done("pe", last, f"{layer}.out")
                elif layer == "L0a":
                    norm2(layer)
                    need(pe, "dve", f"{layer}.xT")
                    done("pe", product(O2[:, 0, 0:D], xT, pk(layer, "gate", KD)), f"{layer}.gate_ps")
                    need(pe, "dve", f"{layer}.x2T")
                    qkv(layer, x2T)
                elif layer in ("L1a", "L2a"):
                    need(pe, "dve", f"{layer}.xT")
                    qkv(layer, xT)
                if layer in ("L0a", "L2a"):
                    need(pe, "dve", f"{layer}.qblk")
                    done("pe", heads_products(halfT, blk), f"{layer}.A_ps")
                    need(pe, "dve", f"{layer}.AT")
                    for h in range(H):
                        last = mm(O2[:, 1, h * (DH + 1):(h + 1) * (DH + 1)], mats3[:, h, :], vaug[:, h, :],
                                  start=True, stop=True)
                    done("pe", last, f"{layer}.num_ps")
                    tail(layer)
                elif layer == "L1a":
                    need(pe, "dve", f"{layer}.kblk")
                    done("pe", heads_products(halfT, blk), f"{layer}.S_ps")
                    need(pe, "act", f"{layer}.p")
                    for b in range(4):
                        last = transposes(S4[:, b], mats[:, b * BANK:(b + 1) * BANK], 4)
                    done("pe", last, f"{layer}.pT_ps")
                    need(pe, "dve", f"{layer}.pT")
                    for h in range(H):
                        last = mm(O2[:, 1, h * DH:(h + 1) * DH], matsT3[:, h, :], vaug[:, h, 0:DH],
                                  start=True, stop=True)
                    done("pe", last, f"{layer}.num_ps")
                    tail(layer)
                elif layer == "L3a":
                    need(pe, "dve", f"{layer}.V")
                    for h in range(H):
                        last = mm(O2[:, 1, h * DH:(h + 1) * DH], mats3[:, h, :], vaug[:, h, 0:DH],
                                  start=True, stop=True)
                    done("pe", last, f"{layer}.num_ps")
                    tail(layer)
                elif layer == "L1f":
                    norm2(layer)
                    need(pe, "dve", f"{layer}.x2T")
                    need(pe, "dve", f"{layer}.w")
                    w1 = fb[:, 0, 0:2048].rearrange("p (k n) -> p k n", k=KD)
                    w2 = fb[:, 1, 0:2048].rearrange("p (t n) -> p t n", t=8)
                    for i in range(2):
                        last = product(S4[:, i], x2T, w1[:, :, i * BANK:(i + 1) * BANK])
                    done("pe", last, f"{layer}.z_ps")
                    need(pe, "act", f"{layer}.y")
                    for i in range(2):
                        last = transposes(S4[:, 2 + i], hid[:, i * BANK:(i + 1) * BANK], 4)
                    done("pe", last, f"{layer}.yT_ps")
                    need(pe, "dve", f"{layer}.yT")
                    done("pe", product(O2[:, 0, 0:D], hidT, w2, 8), f"{layer}.out")
                elif layer in ("L2x", "L3x"):
                    cross(layer)
                elif layer in FF:
                    need(pe, "dve", f"{layer}.xT")
                    done("pe", product(O2[:, 0, 0:E], xT, pk(layer, "gate", KD)), f"{layer}.logit")
                    if layer == "L3f":
                        need(pe, "dve", f"{layer}.onehot")
                        mm(O2[:, 1, 0:E], C["causal"], one0, start=True, stop=True)
                        done("pe", mm(O2[:, 1, E:2 * E], C["causal"], one1, start=True, stop=True), f"{layer}.pos")
                    experts(layer)
                elif layer == "L1x":
                    s = L[layer]
                    need(pe, "dve", f"{layer}.A")
                    done("pe", transposes(T2[:, 1], x2, KD), f"{layer}.AT_ps")
                    need(pe, "dve", f"{layer}.AT")

                    def sim(n, q, first=False):
                        pe.wait_ge(s[f"ctx_in{q}"], 16 * n + 16)
                        if q >= 2 or not first:
                            pe.wait_ge(s["s_taken"], 4 * n + (q - 1))
                        for n0, n1 in ((0, BANK), (BANK, HC)):
                            for k in range(KD):
                                last = mm(S4f[:, q % 2 * 2 * BANK + n0:q % 2 * 2 * BANK + n1], x2T[:, k, :],
                                          half_in(q)[:, k, n0:n1], start=(k == 0), stop=(k == KD - 1))
                        last.then_inc(s["s_ready"], 1)

                    for q in range(4):
                        sim(0, q, True)
                    with pe.Fori(1, NC // 2) as n:
                        for q in range(4):
                            sim(n, q)
                    for q in range(2):
                        sim(NC // 2, q)

                    def turn(c, half, first=False):
                        pe.wait_ge(s["p_ready"], 2 * c + half + 1)
                        if half or not first:
                            pe.wait_ge(s["t_dve"], 2 * c + half)
                            pe.wait_ge(s["t_act"], 2 * c + half)
                        for g in range(2):
                            last = transposes(T2[:, g], sc[:, half, 4 * g * TK:(4 * g + 4) * TK], 4, TK)
                            last.then_inc(s["t_ready"], 1)

                    def multiply(c, half, first=False):
                        pe.wait_ge(s[f"nat_in{half}"], 16 * c + 16)
                        if not first:
                            pe.wait_ge(s["pv_taken"], 2 * c - 1 + half)
                        for g in range(2):
                            pe.wait_ge(s["t_act" if g else "t_dve"], 2 * c + half + 1)
                            for i in range(4):
                                t = 4 * g + i
                                last = mm(O2[:, half, 0:D], pT[0:TK, 2 * half + g, i * P:(i + 1) * P],
                                          fb[0:TK, half, t * D:(t + 1) * D], start=(t == 0), stop=(t == TH - 1))
                        last.then_inc(s["pv_ready"], 1)

                    turn(0, 0, True)
                    turn(0, 1)
                    multiply(0, 0, True)
                    turn(1, 0)
                    multiply(0, 1, True)
                    turn(1, 1)
                    multiply(1, 0)
                    with pe.Fori(2, NC) as c:
                        turn(c, 0)
                        multiply(c - 1, 1)
                        turn(c, 1)
                        multiply(c, 0)
                    multiply(NC - 1, 1)
                    need(pe, "dve", f"{layer}.bat")
                    done("pe", mm(O2[:, 0, 0:D + 1], mats3[:, 0, :], work[:, 512:512 + D + 1], start=True, stop=True),
                         f"{layer}.hc_ps")
                    need(pe, "dve", f"{layer}.f")
                    transposes(S4[:, 0], arena[:, 0:512], 4)
                    done("pe", transposes(S4[:, 1], arena[:, 512:768], 2), f"{layer}.fT_ps")
                    need(pe, "dve", f"{layer}.fT")
                    w = pk(layer, "w_qv", 8)
                    fT = arena[:, 1024:1024 + 768].rearrange("p (k n) -> p k n", k=6)
                    for k in range(8):
                        last = mm(O2[:, 1, 0:D], xT[:, k, :] if k < 2 else fT[:, k - 2, :], w[:, k, :],
                                  start=(k == 0), stop=(k == 7))
                    done("pe", last, f"{layer}.out")

        @block.scalar
        def _(act):
            def cross(layer):
                s = L[layer]
                bias = pk(layer, "bk") if layer == "L2x" else None

                def keys(hf, c, first=False):
                    for nb in range(4):
                        act.wait_ge(s["kp_ready"], 8 * c + (4 * hf + nb + 1))
                        if nb == 0 and hf:
                            act.wait_ge(s["keys_in0"], 256 * c + 256)
                        elif nb == 0 and not first:
                            act.wait_ge(s["keys_in1"], 256 * c)
                        dst = keys_hl[:, 0, nb * (HC // 2):(nb + 1) * (HC // 2)]
                        src = S4[:, nb, 0:HC // 2]
                        if bias is None:
                            ins = nc.scalar.activation(dst, src, ACT.Copy)
                        else:
                            ins = nc.scalar.activation(dst, src, ACT.Identity, bias=bias[:, hf:hf + 1])
                        ins.then_inc(s["up_taken"], 1)

                def take_group(c, n):
                    kind, h, g, _ = GROUPS[n]
                    act.wait_ge(s["t_ready"], NG * c + (n + 1))
                    if h >= 1:
                        act.wait_ge(s["pv_done"], 64 * c + (4 * (h - 1) + g + 1))
                    nc.scalar.activation(pT[0:TK, g, :], T2[0:TK, n % 2, :], ACT.Copy).then_inc(s["t_act"], 1)

                def take_quad(c, quad):
                    act.wait_ge(s["pv_done"], 64 * c + 16 * (quad + 1))
                    if quad >= 2:
                        act.wait_ge(s["t_ready"], NG * c + (GROUP_AT["O", quad - 2, 0] + 1))
                    nc.scalar.activation(o_sb[:, quad % 2, :], O2[:, quad % 2, :], ACT.Copy).then_inc(s["o_taken"], 1)

                if bias is not None:
                    packed(act, layer)
                for hf in range(KD):
                    keys(hf, 0, True)

                def soften(c, h):
                    act.wait_ge(s["s_taken"], 32 * c + (2 * h + 2))
                    nc.scalar.activation(sc[:, h % 3, :], sc[:, h % 3, :], ACT.Exp, bias=n_new[:, h:h + 1],
                                         scale=-1.0, accum_out=l_new[:, h:h + 1]).then_inc(s["p_ready"], 1)

                def chunk(c, last_chunk):
                    for h in range(3):
                        soften(c, h)
                    for h in range(H):
                        if h in KEYS_AT and not last_chunk:
                            keys(KEYS_AT.index(h), c + 1)
                        take_group(c, GROUP_AT["T", h, 0])
                        take_group(c, GROUP_AT["T", h, 2])
                        if h % 4 == 0 and h:
                            take_quad(c, h // 4 - 1)
                        if 0 < h < H - 2:
                            soften(c, h + 2)
                        elif h == H - 2:
                            act.wait_ge(s["delta"], c + 1)
                            nc.scalar.activation(alpha, alpha, ACT.Exp).then_inc(s["alpha"], 1)
                    take_quad(c, 3)

                with act.Fori(0, NC - 1) as c:
                    chunk(c, False)
                chunk(NC - 1, True)

            def experts(layer):
                s = L[layer]
                F = FF[layer]
                per = 2 if layer in GATED else 1
                fn = ACT.Silu if layer in GATED else ACT.Gelu

                def expert(e):
                    act.wait_ge(s["g_ready"], per * e + 1)
                    nc.scalar.activation(gated[:, 0:F].rearrange("p (i n) -> p i n", i=2), S4[:, 0:2, 0:F // 2], fn) \
                        .then_inc(s["act_done"], 1)
                    act.wait_ge(s["t_ready"], 2 * e + 2)
                    nc.scalar.activation(hidT[0:F // E, 4:8, :].rearrange("p t n -> p (t n)"), T2[0:F // E, 1, :],
                                         ACT.Copy).then_inc(s["t_act"], 1)

                with act.Fori(0, E // 2) as n:
                    for b in range(2):
                        expert(2 * n + b)

            for layer in layers:
                if layer == "L0a":
                    need(act, "dve", f"{layer}.g")
                    done("act", nc.scalar.activation(x2[:, :], x2[:, :], ACT.Sigmoid, accum_out=row), f"{layer}.sig")
                elif layer == "L2a":
                    need(act, "dve", f"{layer}.neg")
                    done("act", nc.scalar.activation(work[:, 512:1024], work[:, 512:1024], ACT.Exp), f"{layer}.elu")
                elif layer == "L1a":
                    need(act, "dve", f"{layer}.sm")
                    done("act", nc.scalar.activation(mats, mats, ACT.Exp), f"{layer}.p")
                elif layer == "L3a":
                    need(act, "dve", f"{layer}.abs")
                    done("act", nc.scalar.activation(head_a[:, 0:H], head_b[:, 0:H], ACT.Exp, scale=-1.0),
                         f"{layer}.e")
                    need(act, "dve", f"{layer}.onep")
                    done("act", nc.scalar.activation(head_b[:, 0:H], head_a[:, 0:H], ACT.Ln), f"{layer}.ln1p")
                    need(act, "dve", f"{layer}.ln")
                    for h in range(H):
                        last = nc.scalar.activation(mats3[:, h, :], C["steps"], ACT.Exp, scale=lam[:, h:h + 1])
                    done("act", last, f"{layer}.decay")
                elif layer == "L1f":
                    need(act, "dve", f"{layer}.z")
                    done("act", nc.scalar.activation(hid, hid, ACT.Silu), f"{layer}.y")
                elif layer in ("L2x", "L3x"):
                    cross(layer)
                elif layer in FF:
                    if layer != "L0f":
                        need(act, "dve", f"{layer}.logit")
                        done("act", nc.scalar.activation(prob, prob, ACT.Exp, accum_out=row), f"{layer}.prob")
                    experts(layer)
                elif layer == "L1x":
                    s = L[layer]
                    need(act, "pool", f"{layer}.gmax")
                    need(act, "dve", f"{layer}.max")

                    def soften(c, first):
                        for half in range(2):
                            if not first:
                                act.wait_ge(s["t_ready"], 4 * c + (2 * half - 2))
                            nc.scalar.activation(sc[:, half, 0:HC], arena[:, bass.ds(c * CH + half * HC, HC)], ACT.Exp,
                                                 bias=rec, accum_out=sums[:, bass.ds(2 * c + half, 1)]) \
                                .then_inc(s["p_ready"], 1)
                            act.wait_ge(s["t_ready"], 4 * c + (2 * half + 2))
                            if not first:
                                act.wait_ge(s["pv_ready"], 2 * c + half - 1)
                            nc.scalar.activation(pT[0:TK, 2 * half + 1, :], T2[0:TK, 1, :], ACT.Copy) \
                                .then_inc(s["t_act"], 1)

                    soften(0, True)
                    with act.Fori(1, NC) as c:
                        soften(c, False)
                    done("act", nc.scalar.activation(bat, row_max, ACT.Exp, bias=gmax, scale=1.0), f"{layer}.bat")

        @block.vector
        def _(dve):
            V = nc.vector

            def link(ins):
                owned["dve"] += 1
                ins.then_inc(own["dve"], 1)
                dve.wait_ge(own["dve"], owned["dve"])

            def bcast(ap, n, inner=True):
                m = ap.shape[1]
                if inner:
                    return ap.unsqueeze(2).to_broadcast([P, m, n])
                return ap.unsqueeze(1).to_broadcast([P, n, m])

            def variance(src, layer, stage):
                link(V.bn_stats(stats, src))
                link(V.bn_aggr(mv, stats))
                done("dve", V.tensor_scalar(mv[:, 1:2], mv[:, 1:2], 1e-5, None, ALU.add), f"{layer}.{stage}")

            def scaled(out, src):
                return V.tensor_scalar(out, src, mv[:, 0:1], rstd, ALU.subtract, ALU.mult)

            def norm(layer):
                variance(x[:, :], layer, "var")
                need(dve, "pool", f"{layer}.rstd")
                done("dve", scaled(xn[:, :], x[:, :]), f"{layer}.xn")
                need(dve, "pe", f"{layer}.xnT")
                done("dve", V.tensor_copy(xT[:, :, :].rearrange("p k n -> p (k n)"), T2[:, 0, 0:D]), f"{layer}.xT")

            def norm2(layer):
                packed(dve, layer)
                variance(xn[:, :], layer, "var2")
                need(dve, "pool", f"{layer}.rstd2")
                link(scaled(x2[:, :], xn[:, :]))
                link(V.tensor_tensor(x2[:, :], x2[:, :], pk(layer, "ln_g"), ALU.mult))
                done("dve", V.tensor_tensor(x2[:, :], x2[:, :], pk(layer, "ln_b"), ALU.add), f"{layer}.x2")
                need(dve, "pe", f"{layer}.x2T_ps")
                done("dve", V.tensor_copy(x2T[:, :, :].rearrange("p k n -> p (k n)"), T2[:, 1, 0:D]), f"{layer}.x2T")

            def tail(layer):
                need(dve, "pe", f"{layer}.oT_ps")
                done("dve", V.tensor_copy(oT.rearrange("p k n -> p (k n)"), T2[:, 1, 0:D]), f"{layer}.oT")
                need(dve, "pe", f"{layer}.out")
                residual(layer, O2[:, 0, 0:D])

            def residual(layer, out):
                if "b_out" in PACKS[layer] or "b" in PACKS[layer]:
                    link(V.tensor_tensor(x[:, :], x[:, :], pk(layer, "b_out" if "b_out" in PACKS[layer] else "b"),
                                         ALU.add))
                done("dve", V.tensor_tensor(x[:, :], out, x[:, :], ALU.add), f"{layer}.end")
                need(dve, "dve", f"{layer}.end")

            def spread(psum, stage):
                for k in range(KD):
                    last = V.tensor_tensor(blk[:, k * HH:(k + 1) * HH, :], bcast(psum[:, k * P:(k + 1) * P], HH, False),
                                           bcast(C["head"], P), ALU.mult)
                done("dve", last, stage)

            def ranks(src):
                a3 = half.rearrange("p (e j) -> p e j", e=E)
                b3 = eye_a.rearrange("p (e j) -> p e j", e=E)
                link(V.tensor_tensor(b3, bcast(src, E, False), bcast(src, E), ALU.is_equal))
                link(V.tensor_tensor(eye_a, eye_a, C["before"], ALU.mult))
                link(V.tensor_tensor(a3, bcast(src, E, False), bcast(src, E), ALU.is_gt))
                link(V.tensor_tensor(half, half, eye_a, ALU.add))
                link(V.tensor_reduce(rank, a3, X, ALU.add))

            def softmax_gate(layer, bias):
                need(dve, "pe", f"{layer}.logit")
                if bias is None:
                    link(V.tensor_copy(prob, O2[:, 0, 0:E]))
                else:
                    link(V.tensor_tensor(prob, O2[:, 0, 0:E], bias, ALU.add))
                link(V.tensor_reduce(rec, prob, X, ALU.max))
                done("dve", V.tensor_scalar(prob, prob, rec, None, ALU.subtract), f"{layer}.logit")
                need(dve, "act", f"{layer}.prob")
                link(V.reciprocal(rec, row))
                link(V.tensor_scalar(prob, prob, rec, None, ALU.mult))

            def experts(layer):
                s = L[layer]
                F = FF[layer]
                per = 2 if layer in GATED else 1

                def add_up(e, b):
                    dve.wait_ge(s["y_ready"], e + 1)
                    V.tensor_tensor(yacc, O2[:, b, 0:D], yacc, ALU.add).then_inc(s["y_taken"], 1)
                    dve.wait_ge(s["y_taken"], e + 1)

                def expert(e, b, first=False):
                    V.tensor_copy(wcur[:, b:b + 1], wts[:, bass.ds(e, 1)]).then_inc(s["picked"], 1)
                    dve.wait_ge(s["picked"], e + 1)
                    dve.wait_ge(s["act_done"], e + 1)
                    if layer in GATED:
                        dve.wait_ge(s["g_ready"], per * e + per)
                        V.scalar_tensor_tensor(
                            hid[:, 0:F].rearrange("p (i n) -> p i n", i=2), S4[:, 2:4, 0:F // 2], wcur[:, b:b + 1],
                            gated[:, 0:F].rearrange("p (i n) -> p i n", i=2), ALU.mult, ALU.mult) \
                            .then_inc(s["h_ready"], 1)
                    else:
                        V.tensor_scalar(hid[:, 0:F], gated[:, 0:F], wcur[:, b:b + 1], None, ALU.mult) \
                            .then_inc(s["h_ready"], 1)
                    if not first:
                        add_up(e - 1, 1 - b)
                    dve.wait_ge(s["t_ready"], 2 * e + 1)
                    V.tensor_copy(hidT[0:F // E, 0:4, :].rearrange("p t n -> p (t n)"), T2[0:F // E, 0, :]) \
                        .then_inc(s["t_dve"], 1)

                expert(0, 0, True)
                expert(1, 1)
                with dve.Fori(1, E // 2) as n:
                    for b in range(2):
                        expert(2 * n + b, b)
                add_up(E - 1, 1)

            def cross(layer):
                s = L[layer]
                packed(dve, layer)
                def keys(hf, c):
                    for nb in range(4):
                        dve.wait_ge(s["up_taken"], 8 * c + (4 * hf + nb + 1))
                        up, low = (keys_hl[:, i, nb * (HC // 2):(nb + 1) * (HC // 2)] for i in range(2))
                        src = S4[:, nb, 0:HC // 2]
                        if layer == "L2x":
                            ins = V.scalar_tensor_tensor(low, src, pk(layer, "bk")[:, hf:hf + 1], up.bitcast(F32),
                                                         ALU.add, ALU.subtract)
                        else:
                            ins = V.tensor_tensor(low, src, up.bitcast(F32), ALU.subtract)
                        ins.then_inc(s["low_taken"], 1)

                def take_values(c, b):
                    dve.wait_ge(s["vp_ready"], 8 * c + (b + 1))
                    V.tensor_copy(vv[:, 2 * b:2 * b + 2, :].rearrange("p t n -> p (t n)"),
                                  T2[0:TK, VALUE_BANK[b], :]).then_inc(s["vp_taken"], 1)

                keys(0, 0)
                need(dve, "pe", f"{layer}.q_ps")
                rep4 = work[:, BANK:3 * BANK].rearrange("p (j r d) -> p j r d", r=4, d=QR)
                q_ps = O2[:, 0, 0:D]
                if layer == "L2x":
                    link(V.tensor_tensor(x2[:, :], q_ps, pk(layer, "bq"), ALU.add))
                    q_ps = x2[:, :]
                done("dve", V.tensor_scalar(rep4, q_ps.rearrange("p (j d) -> p j d", d=QR).unsqueeze(2)
                                            .to_broadcast([P, NP, 4, QR]), -DH ** -0.5, None, ALU.mult), f"{layer}.q")
                V.memset(n_old, BIG)
                V.memset(acc, 0.0)
                link(V.memset(l_sum, 0.0))

                need(dve, "pe", f"{layer}.qT_ps")

                def queries(ap, rows):
                    n = rows.stop - rows.start
                    return ap.rearrange("p (j n) -> p j n", n=P).unsqueeze(2).to_broadcast([n, NP, 2, P])

                def own_rows(rows):
                    n = rows.stop - rows.start
                    return C["pair"][rows, :].unsqueeze(1).unsqueeze(3).to_broadcast([n, NP, 2, P])

                upper, lower = slice(0, P // 2), slice(P // 2, P)
                qT = S4f[:, 0:2 * BANK]
                V.tensor_tensor(q4[upper].rearrange("p (j a) n -> p j a n", a=2), queries(qT[upper], upper),
                                own_rows(upper), ALU.mult)
                link(V.tensor_copy(q_up[lower], qT[lower]))
                for b in range(2):
                    take_values(0, b)
                link(V.tensor_tensor(q_low[lower], qT[lower], q_up[lower].bitcast(F32), ALU.subtract))
                take_values(0, 2)
                done("dve", V.tensor_tensor(q4[lower].rearrange("p (j a) n -> p j a n", a=2),
                                            queries(q_low[lower], lower), own_rows(lower), ALU.mult), f"{layer}.q4")
                take_values(0, 3)

                def take_group(c, n):
                    kind, h, g, _ = GROUPS[n]
                    dve.wait_ge(s["t_ready"], NG * c + (n + 1))
                    if kind == "T":
                        if h >= 1:
                            dve.wait_ge(s["pv_done"], 64 * c + (4 * (h - 1) + g + 1))
                        V.tensor_copy(pT[0:TK, g, :], T2[0:TK, n % 2, :]).then_inc(s["t_dve"], 1)
                        return
                    src = T2[:, n % 2, :].rearrange("p (a b g m d) -> p a b m d g", a=2, b=2, g=4, m=2)
                    dst = oc[:, h * 4 * DH:(h + 1) * 4 * DH].rearrange("p (a b d) -> p a b d", a=2, b=2)
                    for b in range(2):
                        last = V.tensor_reduce(dst[:, :, b], src[:, :, b, b], X, ALU.add)
                    last.then_inc(s["t_dve"], 1)

                def take_mask(c):
                    dve.wait_ge(s["mask_in"], 16 * c + 16)
                    if layer == "L2x":
                        ins = V.tensor_scalar(mask_bias[:, :], mask_in.bitcast(I32), 0.0, MASKED, ALU.is_equal, ALU.mult)
                    else:
                        ins = V.tensor_scalar(mask_bias[:, :], mask_in, 1.0e9, None, ALU.mult)
                    ins.then_inc(s["mask_taken"], 1)
                    dve.wait_ge(s["mask_taken"], c + 1)

                def take_scores(c, h, i, first=False):
                    dve.wait_ge(s["s_ready"], 32 * c + (2 * h + i + 1))
                    if h >= 3 and i == 0:
                        dve.wait_ge(s["t_ready"], NG * c + (GROUP_AT["T", h - 3, 3] + 1))
                    elif h < 3 and i == 0 and not first:
                        back = GROUP_AT["T", (H - 1, H - 3, H - 2)[h], 3]
                        dve.wait_ge(s["t_ready"], NG * c + (back + 1 - NG))
                    ins = V.memset(tick, 0.0)
                    if h == HH and i == 0:
                        ins.then_inc(s["half_read"], 1)
                    V.tensor_tensor_reduce(
                        sc[:, h % 3, i * HC:(i + 1) * HC], S4f[:, i * 2 * BANK:i * 2 * BANK + HC],
                        mask_bias[:, i * HC:(i + 1) * HC], 1.0, (n_half if i else n_old)[:, h:h + 1],
                        ALU.add, ALU.min, (n_new if i else n_half)[:, h:h + 1]).then_inc(s["s_taken"], 1)
                    dve.wait_ge(s["s_taken"], 32 * c + (2 * h + i + 1))

                def chunk(c, last_chunk):
                    for h in range(H):
                        if h in KEYS_AT and not last_chunk:
                            keys(KEYS_AT.index(h), c + 1)
                        if h % 4 == 1 and h > 1:
                            take_group(c, GROUP_AT["O", (h - 5) // 4, 0])
                        ahead = 0 < h < H - 2
                        if ahead and h not in KEYS_AT:
                            take_scores(c, h + 2, 0)
                        take_group(c, GROUP_AT["T", h, 1])
                        if ahead:
                            if h in KEYS_AT:
                                take_scores(c, h + 2, 0)
                            take_scores(c, h + 2, 1)
                        if h == H - 2 and not last_chunk:
                            take_mask(c + 1)
                        if h == H - 1:
                            dve.wait_ge(s["alpha"], c + 1)
                            V.tensor_tensor(l_sum, l_sum, alpha, ALU.mult).then_inc(s["finished"], 1)
                            dve.wait_ge(s["finished"], 4 * c + 2)
                            V.tensor_tensor(l_sum, l_sum, l_new, ALU.add).then_inc(s["finished"], 1)
                        take_group(c, GROUP_AT["T", h, 3])
                        if h == H - 3:
                            V.tensor_tensor(alpha, n_new, n_old, ALU.subtract).then_inc(s["delta"], 1)
                            dve.wait_ge(s["delta"], c + 1)
                            V.tensor_copy(n_old, n_new).then_inc(s["finished"], 1)
                            dve.wait_ge(s["finished"], 4 * c + 1)
                    if not last_chunk:
                        for i in range(2):
                            take_scores(c + 1, 0, i)
                        for b in range(2):
                            take_values(c + 1, b)
                        take_scores(c + 1, 1, 0)
                    take_group(c, GROUP_AT["O", 3, 0])
                    if not last_chunk:
                        take_scores(c + 1, 1, 1)
                        for b in range(2, 4):
                            take_values(c + 1, b)
                        for i in range(2):
                            take_scores(c + 1, 2, i)
                        take_values(c + 1, 4)
                    dve.wait_ge(s["t_dve"], TAKEN["dve"][-1] * c + TAKEN["dve"][-1])
                    acc3 = acc.rearrange("p (h d) -> p h d", h=H)
                    V.tensor_tensor(acc3, acc3, bcast(alpha, DH), ALU.mult).then_inc(s["acc_taken"], 1)
                    dve.wait_ge(s["acc_taken"], c + 1)
                    V.tensor_tensor(acc, acc, oc, ALU.add).then_inc(s["finished"], 1)
                    if not last_chunk:
                        for b in range(5, 8):
                            take_values(c + 1, b)
                    dve.wait_ge(s["finished"], 4 * c + 4)

                keys(1, 0)
                take_mask(0)
                take_values(0, 4)
                for h in range(3):
                    for i in range(2):
                        take_scores(0, h, i, True)
                    take_values(0, h + 5)
                with dve.Fori(0, NC - 1) as c:
                    chunk(c, False)
                chunk(NC - 1, True)
                link(V.reciprocal(l_sum, l_sum))
                ins = V.tensor_tensor(x2[:, :].rearrange("p (h d) -> p h d", h=H),
                                      acc.rearrange("p (h d) -> p h d", h=H), bcast(l_sum, DH), ALU.mult)
                if layer == "L2x":
                    link(ins)
                    ins = V.tensor_tensor(x2[:, :], x2[:, :], pk(layer, "bv"), ALU.add)
                done("dve", ins, f"{layer}.o")
                tail(layer)

            dve.wait_ge(x_in, 16)
            dve.wait_ge(consts_in, 16)
            for layer in layers:
                norm(layer)
                packed(dve, layer)
                x2h = x2[:, :].rearrange("p (h d) -> p h d", h=H)
                if layer == "L0x":
                    s = L[layer]
                    bufs = [ctx_in[:, :, :, :].rearrange("p h k n -> p (h k n)"),
                            sc[:, 0:2, :].rearrange("p a n -> p (a n)"), arena[:, 0:KD * CH]]
                    for c in range(NC):
                        dve.wait_ge(s[f"ctx_in{c % 3}"], 32 * (c // 3 + 1))
                        V.tensor_reduce(parts4[:, c], bufs[c % 3].rearrange("p (h k n) -> p h k n", h=2, k=KD),
                                        X, ALU.add).then_inc(s["summed"], 1)
                    dve.wait_ge(s["summed"], NC)
                    link(V.tensor_reduce(mean, parts4.rearrange("p c h k -> p k (c h)"), X, ALU.add))
                    link(V.tensor_scalar(mean, mean, 1.0 / NK, None, ALU.mult))
                    done("dve", V.tensor_copy(x2T[:, :, :], bcast(mean, P)), f"{layer}.mean")
                    need(dve, "pe", f"{layer}.out")
                    residual(layer, O2[:, 0, 0:D])
                elif layer == "L0a":
                    norm2(layer)
                    need(dve, "pe", f"{layer}.gate_ps")
                    done("dve", V.tensor_tensor(x2[:, :], O2[:, 0, 0:D], pk(layer, "b_gate"), ALU.add), f"{layer}.g")
                    need(dve, "pe", f"{layer}.qkv_ps")
                    qk = work[:, 0:2 * D]
                    link(V.tensor_tensor(qk, S4[:, 0], pk(layer, "b_qkv")[:, 0:2 * D], ALU.add))
                    link(V.memset(vaug, 1.0))
                    V.tensor_tensor(vaug[:, :, 0:DH], S4[:, 1, 0:D].rearrange("p (h d) -> p h d", h=H),
                                    pk(layer, "b_qkv")[:, 2 * D:3 * D].rearrange("p (h d) -> p h d", h=H), ALU.add)
                    need(dve, "act", f"{layer}.sig")
                    link(V.tensor_scalar(rec, row, 1.0 / D, 1e-5, ALU.mult, ALU.add))
                    link(V.reciprocal(rec, rec))
                    link(V.tensor_scalar(x2[:, :], x2[:, :], rec, None, ALU.mult))
                    q3 = qk.rearrange("p (a n) -> p a n", a=2)
                    link(V.tensor_tensor(q3, q3, bcast(x2[:, :], 2, False), ALU.mult))
                    link(V.tensor_scalar(qk, qk, 0.0, None, ALU.max))
                    link(V.tensor_tensor(qk, qk, qk, ALU.mult))
                    done("dve", V.tensor_scalar(qk, qk, 1e-5, None, ALU.add), f"{layer}.qk")
                elif layer == "L2a":
                    need(dve, "pe", f"{layer}.qkv_ps")
                    qk = work[:, 0:2 * D]
                    done("dve", V.tensor_scalar(work[:, 512:1024], S4[:, 0], 0.0, None, ALU.min), f"{layer}.neg")
                    link(V.memset(vaug, 1.0))
                    V.tensor_copy(vaug[:, :, 0:DH], S4[:, 1, 0:D].rearrange("p (h d) -> p h d", h=H))
                    link(V.tensor_scalar(qk, S4[:, 0], 0.0, None, ALU.max))
                    need(dve, "act", f"{layer}.elu")
                    done("dve", V.tensor_tensor(qk, qk, work[:, 512:1024], ALU.add), f"{layer}.qk")
                if layer in ("L0a", "L2a"):
                    need(dve, "pe", f"{layer}.qkT_ps")
                    V.tensor_copy(halfT.rearrange("p k n -> p (k n)"), T2[:, 0, D:2 * D])
                    spread(T2[:, 0], f"{layer}.qblk")
                    need(dve, "pe", f"{layer}.A_ps")
                    done("dve", V.tensor_tensor(mats3, S4f.rearrange("p (h n) -> p h n", h=H),
                                                bcast(C["causal"], H, False), ALU.mult), f"{layer}.AT")
                    need(dve, "pe", f"{layer}.num_ps")
                    link(V.tensor_copy(num, O2[:, 1, 0:H * (DH + 1)].rearrange("p (h n) -> p h n", h=H)))
                    den = head_a[:, 0:H]
                    if layer == "L0a":
                        link(V.tensor_scalar(den, num[:, :, DH], 1e-5, None, ALU.add))
                    else:
                        link(V.tensor_scalar(den, num[:, :, DH], 1e-6, None, ALU.max))
                    link(V.reciprocal(den, den))
                    done("dve", V.tensor_tensor(x2h, num[:, :, 0:DH], bcast(den, DH), ALU.mult), f"{layer}.o")
                    tail(layer)
                elif layer == "L1a":
                    need(dve, "pe", f"{layer}.qkv_ps")
                    qk, q3 = work[:, 0:2 * D], work[:, 0:2 * D].rearrange("p (h d) -> p h d", d=DH)
                    sq, s3 = work[:, 512:1024], work[:, 512:1024].rearrange("p (h d) -> p h d", d=DH)
                    V.tensor_copy(vaug[:, :, 0:DH], S4[:, 1, 0:D].rearrange("p (h d) -> p h d", h=H))
                    link(V.tensor_copy(qk, S4[:, 0]))
                    link(V.tensor_reduce(vsum, q3, X, ALU.add))
                    link(V.tensor_scalar(vsum, vsum, 1.0 / DH, None, ALU.mult))
                    link(V.tensor_tensor(q3, q3, bcast(vsum, DH), ALU.subtract))
                    link(V.tensor_tensor(sq, qk, qk, ALU.mult))
                    link(V.tensor_reduce(vsum, s3, X, ALU.add))
                    done("dve", V.tensor_scalar(head_a, vsum, 1.0 / DH, 1e-5, ALU.mult, ALU.add), f"{layer}.var2")
                    need(dve, "pool", f"{layer}.rstd2")
                    link(V.tensor_tensor(q3, q3, bcast(head_b, DH), ALU.mult))
                    link(V.tensor_tensor(qk, qk, pk(layer, "ln_w"), ALU.mult))
                    link(V.tensor_tensor(qk, qk, pk(layer, "ln_b"), ALU.add))
                    done("dve", V.tensor_scalar(qk[:, 0:D], qk[:, 0:D], DH ** -0.5, None, ALU.mult), f"{layer}.qk")
                    need(dve, "pe", f"{layer}.qkT_ps")
                    V.tensor_copy(halfT.rearrange("p k n -> p (k n)"), T2[:, 0, 0:D])
                    spread(T2[:, 0, D:2 * D], f"{layer}.kblk")
                    need(dve, "pe", f"{layer}.S_ps")
                    link(V.tensor_tensor(mats3, S4f.rearrange("p (h n) -> p h n", h=H),
                                         bcast(C["causal_bias"], H, False), ALU.add))
                    link(V.tensor_reduce(head_a[:, 0:H], mats3, X, ALU.max))
                    done("dve", V.tensor_tensor(mats3, mats3, bcast(head_a[:, 0:H], P), ALU.subtract), f"{layer}.sm")
                    need(dve, "act", f"{layer}.p")
                    link(V.tensor_reduce(head_a[:, 0:H], mats3, X, ALU.add))
                    link(V.reciprocal(head_a[:, 0:H], head_a[:, 0:H]))
                    need(dve, "pe", f"{layer}.pT_ps")
                    done("dve", V.tensor_copy(matsT, S4f), f"{layer}.pT")
                    need(dve, "pe", f"{layer}.num_ps")
                    done("dve", V.tensor_tensor(x2h, O2[:, 1, 0:D].rearrange("p (h d) -> p h d", h=H),
                                                bcast(head_a[:, 0:H], DH), ALU.mult), f"{layer}.o")
                    tail(layer)
                elif layer == "L3a":
                    ld = pk(layer, "log_decay")
                    link(V.tensor_scalar(head_a[:, 0:H], ld, -1.0, None, ALU.mult))
                    done("dve", V.tensor_tensor(head_b[:, 0:H], head_a[:, 0:H], ld, ALU.max), f"{layer}.abs")
                    link(V.tensor_scalar(lam, ld, 0.0, None, ALU.min))
                    need(dve, "act", f"{layer}.e")
                    done("dve", V.tensor_scalar(head_a[:, 0:H], head_a[:, 0:H], 1.0, None, ALU.add), f"{layer}.onep")
                    need(dve, "act", f"{layer}.ln1p")
                    done("dve", V.tensor_tensor(lam, lam, head_b[:, 0:H], ALU.subtract), f"{layer}.ln")
                    link(V.tensor_tensor(work[:, 0:D], pk(layer, "q"), pk(layer, "k"), ALU.mult))
                    link(V.tensor_reduce(vsum[:, 0:H], work[:, 0:D].rearrange("p (h d) -> p h d", h=H), X, ALU.add))
                    V.tensor_tensor(vaug[:, :, 0:DH], xn[:, :].rearrange("p (h d) -> p h d", h=H),
                                    bcast(vsum[:, 0:H], DH), ALU.mult)
                    need(dve, "act", f"{layer}.decay")
                    done("dve", V.tensor_tensor(mats3, mats3, bcast(C["causal"], H, False), ALU.mult), f"{layer}.V")
                    need(dve, "pe", f"{layer}.num_ps")
                    link(V.tensor_copy(x2[:, :], O2[:, 1, 0:D]))
                    link(V.tensor_tensor(work[:, 0:D], x2[:, :], x2[:, :], ALU.mult))
                    link(V.tensor_reduce(rec, work[:, 0:D], X, ALU.add))
                    done("dve", V.tensor_scalar(mv[:, 1:2], rec, 1.0 / D, 1e-6, ALU.mult, ALU.add), f"{layer}.var2")
                    need(dve, "pool", f"{layer}.rstd2")
                    link(V.tensor_scalar(x2[:, :], x2[:, :], rstd, None, ALU.mult))
                    done("dve", V.tensor_tensor(x2[:, :], x2[:, :], pk(layer, "norm"), ALU.mult), f"{layer}.o")
                    tail(layer)
                elif layer == "L1f":
                    norm2(layer)
                    dve.wait_ge(L[layer]["q_in"], 64)
                    for b in range(2):
                        link(V.tensor_scalar(fb[:, b, 0:2048], fb[:, b, 0:2048].bitcast(I32), 128.0, None, ALU.subtract))
                    link(V.tensor_tensor(fb[:, 0, 0:2048], fb[:, 0, 0:2048], fb[:, 0, 2048:4096], ALU.mult))
                    done("dve", V.tensor_tensor(fb[:, 1, 0:2048], fb[:, 1, 0:2048], fb[:, 1, 2048:4096], ALU.mult),
                         f"{layer}.w")
                    need(dve, "pe", f"{layer}.z_ps")
                    done("dve", V.tensor_tensor(hid, S4f[:, 0:1024], pk(layer, "b1"), ALU.add), f"{layer}.z")
                    need(dve, "pe", f"{layer}.yT_ps")
                    done("dve", V.tensor_copy(hidT.rearrange("p t n -> p (t n)"), S4f[:, 1024:2048]), f"{layer}.yT")
                    link(V.tensor_tensor(x[:, :], x[:, :], xn[:, :], ALU.add))
                    need(dve, "pe", f"{layer}.out")
                    link(V.tensor_tensor(x2[:, :], O2[:, 0, 0:D], pk(layer, "b2"), ALU.add))
                    done("dve", V.scalar_tensor_tensor(x[:, :], x2[:, :], 0.5, x[:, :], ALU.mult, ALU.add),
                         f"{layer}.end")
                    need(dve, "dve", f"{layer}.end")
                elif layer in ("L2x", "L3x"):
                    cross(layer)
                elif layer in FF:
                    V.memset(yacc, 0.0)
                    if layer == "L0f":
                        need(dve, "pe", f"{layer}.logit")
                        link(V.tensor_copy(prob, O2[:, 0, 0:E]))
                        ranks(prob)
                        link(V.tensor_scalar(rank, rank, 2.0, None, ALU.is_lt))
                        done("dve", V.tensor_tensor(wts, rank, prob, ALU.mult), f"{layer}.weights")
                    elif layer == "L2f":
                        softmax_gate(layer, pk(layer, "bias"))
                        ranks(prob)
                        link(V.tensor_scalar(rank, rank, 2.0, None, ALU.is_lt))
                        link(V.tensor_tensor(wts, rank, prob, ALU.mult))
                        link(V.tensor_reduce(row, wts, X, ALU.add))
                        link(V.tensor_scalar(row, row, 1e-6, None, ALU.add))
                        link(V.reciprocal(row, row))
                        done("dve", V.tensor_scalar(wts, wts, row, None, ALU.mult), f"{layer}.weights")
                    else:
                        softmax_gate(layer, None)
                        ranks(prob)
                        link(V.tensor_scalar(one0, rank, 0.0, None, ALU.is_equal))
                        link(V.tensor_scalar(one1, rank, 1.0, None, ALU.is_equal))
                        done("dve", V.tensor_tensor(wts, one0, one1, ALU.add), f"{layer}.onehot")
                        need(dve, "dve", f"{layer}.onehot")
                        link(V.tensor_tensor(wts, wts, prob, ALU.mult))
                        link(V.tensor_reduce(row, wts, X, ALU.add))
                        link(V.reciprocal(row, row))
                        link(V.tensor_scalar(prob, prob, row, None, ALU.mult))
                        need(dve, "pe", f"{layer}.pos")
                        link(V.tensor_scalar(half[:, 0:2 * E], O2[:, 1, 0:2 * E], float(CAPACITY), None, ALU.is_le))
                        link(V.tensor_tensor(one0, one0, half[:, 0:E], ALU.mult))
                        link(V.tensor_tensor(one1, one1, half[:, E:2 * E], ALU.mult))
                        link(V.tensor_tensor(wts, one0, one1, ALU.add))
                        done("dve", V.tensor_tensor(wts, wts, prob, ALU.mult), f"{layer}.weights")
                    need(dve, "dve", f"{layer}.weights")
                    experts(layer)
                    if layer == "L2f":
                        variance(yacc, layer, "var3")
                        link(V.tensor_tensor(x[:, :], x[:, :], xn[:, :], ALU.add))
                        need(dve, "pool", f"{layer}.rstd3")
                        link(scaled(yacc, yacc))
                    residual(layer, yacc)
                elif layer == "L1x":
                    s = L[layer]
                    w = pk(layer, "w_sim")
                    link(V.tensor_tensor(x2[:, :], xn[:, :], w[:, 0:D], ALU.mult))
                    link(V.tensor_reduce(row, x2[:, :], X, ALU.add))
                    link(V.tensor_tensor(row, row, pk(layer, "b_sim"), ALU.add))
                    link(V.tensor_tensor(x2[:, :], xn[:, :], w[:, 2 * D:3 * D], ALU.mult))
                    done("dve", V.tensor_tensor(x2[:, :], x2[:, :], w[:, D:2 * D], ALU.add), f"{layer}.A")
                    need(dve, "pe", f"{layer}.AT_ps")
                    done("dve", V.tensor_copy(x2T[:, :, :].rearrange("p k n -> p (k n)"), T2[:, 1, 0:D]), f"{layer}.AT")
                    with dve.Fori(0, NC) as c:
                        for i in range(2):
                            dve.wait_ge(s["s_ready"], 2 * c + (i + 1))
                            V.tensor_scalar(arena[:, bass.ds(c * CH + i * HC, HC)],
                                            S4f[:, i * 2 * BANK:i * 2 * BANK + HC], row, None, ALU.add, ALU.max,
                                            accum_out=maxes[:, bass.ds(2 * c + i, 1)]).then_inc(s["s_taken"], 1)
                    dve.wait_ge(s["s_taken"], 2 * NC)
                    link(V.memset(acc, 0.0))
                    link(V.tensor_reduce(row_max, maxes, X, ALU.max))
                    done("dve", V.tensor_scalar(rec, row_max, -1.0, None, ALU.mult), f"{layer}.max")
                    need(dve, "pool", f"{layer}.gmax")
                    link(V.tensor_scalar(gmax, gmax, -1.0, None, ALU.mult))

                    def turned(c, i, first):
                        dve.wait_ge(s["t_ready"], 4 * c + (2 * i + 1))
                        if not first:
                            dve.wait_ge(s["pv_ready"], 2 * c + i - 1)
                        V.tensor_copy(pT[0:TK, 2 * i, :], T2[0:TK, 0, :]).then_inc(s["t_dve"], 1)

                    def multiplied(c, i):
                        dve.wait_ge(s["pv_ready"], 2 * c + i + 1)
                        V.tensor_tensor(acc, O2[:, i, 0:D], acc, ALU.add).then_inc(s["pv_taken"], 1)
                        dve.wait_ge(s["pv_taken"], 2 * c + i + 1)

                    turned(0, 0, True)
                    turned(0, 1, True)
                    multiplied(0, 0)
                    with dve.Fori(1, NC) as c:
                        turned(c, 0, False)
                        multiplied(c - 1, 1)
                        turned(c, 1, False)
                        multiplied(c, 0)
                    multiplied(NC - 1, 1)
                    dve.wait_ge(s["p_ready"], 2 * NC)
                    need(dve, "act", f"{layer}.bat")
                    V.tensor_copy(work[:, 512:512 + D], xn[:, :])
                    V.memset(work[:, 512 + D:512 + D + 1], 1.0)
                    done("dve", V.tensor_copy(mats3[:, 0, :], bat.to_broadcast([P, P])), f"{layer}.bat")
                    f = [arena[:, k * D:(k + 1) * D] for k in range(3)]
                    link(V.tensor_reduce(rec, sums, X, ALU.add))
                    link(V.reciprocal(rec, rec))
                    link(V.tensor_scalar(f[0], acc, rec, None, ALU.mult))
                    link(V.tensor_tensor(f[1], xn[:, :], f[0], ALU.mult))
                    need(dve, "pe", f"{layer}.hc_ps")
                    link(V.reciprocal(rec, O2[:, 0, D:D + 1]))
                    link(V.tensor_scalar(f[2], O2[:, 0, 0:D], rec, None, ALU.mult))
                    done("dve", V.tensor_tensor(f[2], f[2], xn[:, :], ALU.mult), f"{layer}.f")
                    need(dve, "pe", f"{layer}.fT_ps")
                    done("dve", V.tensor_copy(arena[:, 1024:1024 + 768], S4f[:, 0:768]), f"{layer}.fT")
                    need(dve, "pe", f"{layer}.out")
                    residual(layer, O2[:, 1, 0:D])


def blocks(w):
    k = w.shape[0] // P
    return w.reshape(k, P, w.shape[1]).transpose(1, 0, 2).reshape(P, k * w.shape[1])


def rows(*vs):
    return [np.broadcast_to(np.reshape(v, (1, -1)), (P, np.size(v))) for v in vs]


def pack(*parts):
    return np.ascontiguousarray(np.concatenate(parts, axis=1))


def constants():
    i = np.arange(P)
    e = np.arange(E)
    parts = [np.eye(P), i[:, None] <= i[None, :], np.where(i[None, :] <= i[:, None], 0.0, -MASKED),
             np.maximum(i[None, :] - i[:, None], 0), (i[:, None] // DH) == np.arange(HH)[None, :],
             (i[:, None] % QR // DH) == np.arange(2)[None, :],
             np.broadcast_to((e[None, :] < e[:, None]).reshape(1, -1), (P, E * E))]
    return np.ascontiguousarray(np.concatenate([np.asarray(p, np.float32) for p in parts], axis=1))


def layout(i):
    c = i["ctx_1024"][0]
    L0W = i["L0_xattn_W"]
    out = {
        "x": i["x"][0],
        "consts": constants(),
        "ctx_cols": c.reshape(2 * NC, HC, KD, P).transpose(0, 3, 2, 1),
        "ctx_rows": c.reshape(2 * NC, TH, TK, D).transpose(0, 2, 1, 3).reshape(2 * NC, TK, TH * D),
        "mask_L2x": i["mask_SxS2_ik0"].reshape(P, NC, CH).transpose(1, 0, 2),
        "mask_L3x": i["mask_BxSxS2_ff0"][0].reshape(P, NC, CH).transpose(1, 0, 2),
        "fc1_q": blocks(i["L1_ffn_fc1_q"]),
        "fc2_q": blocks(i["L1_ffn_fc2_q"]),
        "fc1_scales": pack(*rows(i["L1_ffn_fc1_scales"])),
        "fc2_scales": pack(*rows(i["L1_ffn_fc2_scales"])),
        "pack_L0x": pack(blocks(L0W[:, :D].T), blocks(L0W[:, D:].T), *rows(i["L0_xattn_b"])),
        "pack_L0a": pack(blocks(i["L0_attn_W_qkv"]), blocks(i["L0_attn_W_gate"]), blocks(i["L0_attn_W_proj"]),
                         *rows(i["L0_attn_ln_g"], i["L0_attn_ln_b"], i["L0_attn_b_qkv"], i["L0_attn_b_gate"],
                               i["L0_attn_b_proj"])),
        "pack_L0f": pack(blocks(i["L0_ffn_Wg"].T)),
        "pack_L1x": pack(blocks(i["L1_xattn_W_qv"]),
                         *rows(i["L1_xattn_w_sim"], i["L1_xattn_b_sim"], i["L1_xattn_b_qv"])),
        "pack_L1a": pack(blocks(np.concatenate([i["L1_attn_Wq"].T, i["L1_attn_Wk"].T, i["L1_attn_Wv"].T], axis=1)),
                         blocks(i["L1_attn_Wu"].T),
                         *rows(np.tile(i["L1_attn_qln_w"], H), np.tile(i["L1_attn_kln_w"], H),
                               np.tile(i["L1_attn_qln_b"], H), np.tile(i["L1_attn_kln_b"], H))),
        "pack_L1f": pack(*rows(i["L1_ffn_ln_gamma"], i["L1_ffn_ln_beta"], i["L1_ffn_fc1_bias"], i["L1_ffn_fc2_bias"])),
        "pack_L2x": pack(*[blocks(i[f"L2_xattn_W{n}"].T) for n in "qkvo"], *rows(i["L2_xattn_bq"]),
                         i["L2_xattn_bk"].reshape(KD, P).T, *rows(i["L2_xattn_bv"], i["L2_xattn_bo"])),
        "pack_L2a": pack(blocks(np.concatenate([i[f"L2_attn_W{n}"].T for n in "qkv"], axis=1)),
                         blocks(i["L2_attn_Wo"].T)),
        "pack_L2f": pack(blocks(i["L2_ffn_gate_w"].T), *rows(i["L2_ffn_expert_bias"])),
        "pack_L3x": pack(*[blocks(i[f"L3_xattn_W{n}"]) for n in "qkvo"]),
        "pack_L3a": pack(blocks(i["L3_attn_o_w"].T), *rows(i["L3_attn_q"], i["L3_attn_k"], i["L3_attn_log_decay"],
                                                          i["L3_attn_norm_weight"])),
        "pack_L3f": pack(blocks(i["L3_ffn_gate_w"].T)),
    }
    ups = {"L0f": ["L0_ffn_W1", "L0_ffn_W2"], "L2f": ["L2_ffn_w_up"], "L3f": ["L3_ffn_wi_gate", "L3_ffn_wi_up"]}
    downs = {"L0f": "L0_ffn_W3", "L2f": "L2_ffn_w_down", "L3f": "L3_ffn_wo"}
    for layer, names in ups.items():
        F = FF[layer]
        out[f"up_{layer}"] = np.concatenate(
            [i[n].reshape(E, F, KD, P).transpose(0, 3, 2, 1).reshape(E, P, KD * F) for n in names], axis=2)
        out[f"down_{layer}"] = i[downs[layer]].reshape(E, D, E, F // E).transpose(0, 3, 2, 1).reshape(E, F // E, E * D)
    return {k: np.ascontiguousarray(v) for k, v in out.items()}


def kernel(**inputs):
    import concourse.bacc as bacc
    from concourse.bass_utils import run_bass_kernel_spmd

    arrays = layout({k: np.asarray(v) for k, v in inputs.items()})
    nc = bacc.Bacc("TRN2", target_bir_lowering=False, num_devices=1)
    args = {k: nc.dram_tensor(f"in_{k}", v.shape, mybir.dt.from_np(v.dtype), kind="ExternalInput").ap()
            for k, v in arrays.items()}
    args["out"] = nc.dram_tensor("out_x", (P, D), F32, kind="ExternalOutput").ap()
    build(nc, args)
    r = run_bass_kernel_spmd(nc, [{f"in_{k}": v for k, v in arrays.items()}], core_ids=[0])
    return r.results[0]["out_x"].reshape(1, P, D)
```
